# Optimizing a Trainium2 kernel written in Bass

```python
import numpy as np
import jax
import jax.numpy as jnp

def _softmax(x, axis=-1):
    return jax.nn.softmax(x, axis=axis)

def _gelu(x):
    return jax.nn.gelu(x, approximate=True)

def _silu(x):
    return jax.nn.silu(x)

def _sigmoid(x):
    return jax.nn.sigmoid(x)

def _layernorm(x, axis=-1, eps=1e-05):
    m = jnp.mean(x, axis=axis, keepdims=True)
    v = jnp.var(x, axis=axis, keepdims=True)
    return (x - m) / jnp.sqrt(v + eps)

def _scatter_add(tgt, idx, src, axis=0):
    return tgt.at[idx].add(src)

def _segment_sum(src, seg, n):
    return jax.ops.segment_sum(src, seg, n)
kernel_name = 'mk_decoder_preln_d2_seqx_r8_2d64e8'

def setup_inputs(seed: int=0):
    np.random.seed(seed)
    _w = jnp.asarray

    def _rec_inputs():
        import jax
        import jax.numpy as jnp
        _rk = jax.random.key(seed)
        x = -0.0002928 + 1 * jax.random.normal(jax.random.fold_in(_rk, 1), (32, 64, 128), jnp.float32)
        _lenS = 64 - jax.random.randint(jax.random.fold_in(_rk, 7), (32,), 0, max(1, 64 // 4) + 1, jnp.int32)
        _lenS2 = 64 - jax.random.randint(jax.random.fold_in(_rk, 8), (32,), 0, max(1, 64 // 4) + 1, jnp.int32)
        _ctx_512P = jax.random.normal(jax.random.fold_in(_rk, 11), (32, 16, 64), jnp.float32)
        _ctx_512c = jax.random.dirichlet(jax.random.fold_in(_rk, 511), 0.3 * jnp.ones((16,), jnp.float32), (32, 64))
        _ctx_512t = jnp.einsum('bsk,bkd->bsd', _ctx_512c, _ctx_512P)
        _ctx_512t = _ctx_512t * jax.lax.rsqrt(jnp.mean(jnp.square(_ctx_512t)) + 1e-12) * 0.953939
        ctx_512 = -1.52775e-05 + 0.999936 * (_ctx_512t + 0.3 * jax.random.normal(jax.random.fold_in(_rk, 611), (32, 64, 64), jnp.float32))
        itok_BxS2xS_0_7 = jax.random.randint(jax.random.fold_in(_rk, 12), (32, 64, 64), 0, 8, jnp.int32)
        return (x, ctx_512, itok_BxS2xS_0_7)
    x, ctx_512, itok_BxS2xS_0_7 = _rec_inputs()

    def _L0_attn_setup():
        import jax, jax.numpy as jnp
        import numpy as np
        HEADS = 16

        def _fm(t):
            return jax.nn.elu(t) + 1.0
        key = jax.random.key(seed)
        ks = jax.random.split(key, 9)
        B, N, D = (4, 1024, 128)
        s = 1.0 / np.sqrt(D)
        return {'x': jax.random.normal(ks[0], (B, N, D), dtype=jnp.float32), 'wq': jax.random.normal(ks[1], (D, D), dtype=jnp.float32) * s, 'bq': jnp.zeros((D,), dtype=jnp.float32), 'wk': jax.random.normal(ks[2], (D, D), dtype=jnp.float32) * s, 'bk': jnp.zeros((D,), dtype=jnp.float32), 'wv': jax.random.normal(ks[3], (D, D), dtype=jnp.float32) * s, 'bv': jnp.zeros((D,), dtype=jnp.float32), 'wo': jax.random.normal(ks[4], (D, D), dtype=jnp.float32) * s, 'bo': jnp.zeros((D,), dtype=jnp.float32)}
    _L0_attn_all = _L0_attn_setup()
    _L0_attn_in = {k: v for k, v in _L0_attn_all.items() if k in ('wq', 'bq', 'wk', 'bk', 'wv', 'bv', 'wo', 'bo')}
    del _L0_attn_all

    def _L0_xattn_setup():
        import jax, jax.numpy as jnp
        import numpy as np
        NUM_HEADS = 16
        HEAD_DIM = 64
        Q_DIM = 128
        KV_DIM = 64
        INNER = NUM_HEADS * HEAD_DIM
        key = jax.random.key(seed)
        ks = jax.random.split(key, 7)
        B, N, M = (32, 128, 256)
        q = jax.random.normal(ks[0], (B, N, Q_DIM), dtype=jnp.float32)
        kv = jax.random.normal(ks[1], (B, M, KV_DIM), dtype=jnp.float32)
        Wq = jax.random.normal(ks[2], (Q_DIM, INNER), dtype=jnp.float32) / np.sqrt(Q_DIM)
        Wk = jax.random.normal(ks[3], (KV_DIM, INNER), dtype=jnp.float32) / np.sqrt(KV_DIM)
        Wv = jax.random.normal(ks[4], (KV_DIM, INNER), dtype=jnp.float32) / np.sqrt(KV_DIM)
        Wo = jax.random.normal(ks[5], (INNER, Q_DIM), dtype=jnp.float32) / np.sqrt(INNER)
        bo = jax.random.normal(ks[6], (Q_DIM,), dtype=jnp.float32) * 0.01
        return {'q': q, 'kv': kv, 'Wq': Wq, 'Wk': Wk, 'Wv': Wv, 'Wo': Wo, 'bo': bo}
    _L0_xattn_all = _L0_xattn_setup()
    _L0_xattn_in = {k: v for k, v in _L0_xattn_all.items() if k in ('Wq', 'Wk', 'Wv', 'Wo', 'bo')}
    del _L0_xattn_all

    def _L0_ffn_setup():
        import jax, jax.numpy as jnp
        import numpy as np
        D_MODEL = 128
        D_FF = 512
        N_ZONES = 8
        TOP_K = 3
        ROUTER_H = 32
        BATCH = 16
        SEQ = 256
        key = jax.random.key(seed)
        ks = jax.random.split(key, 8)
        s = lambda *dims: 1.0 / np.sqrt(dims[-2] if len(dims) > 1 else dims[-1])
        x = jax.random.normal(ks[0], (BATCH, SEQ, D_MODEL), dtype=jnp.float32)
        W1 = jax.random.normal(ks[1], (D_MODEL, ROUTER_H), dtype=jnp.float32) / np.sqrt(D_MODEL)
        b1 = jnp.zeros((ROUTER_H,), dtype=jnp.float32)
        W2 = jax.random.normal(ks[2], (ROUTER_H, N_ZONES), dtype=jnp.float32) / np.sqrt(ROUTER_H)
        b2 = jnp.zeros((N_ZONES,), dtype=jnp.float32)
        Wa = jax.random.normal(ks[3], (N_ZONES, D_MODEL, D_FF), dtype=jnp.float32) / np.sqrt(D_MODEL)
        Wb = jax.random.normal(ks[4], (N_ZONES, D_FF, D_MODEL), dtype=jnp.float32) / np.sqrt(D_FF)
        return {'x': x, 'W1': W1, 'b1': b1, 'W2': W2, 'b2': b2, 'Wa': Wa, 'Wb': Wb}
    _L0_ffn_all = _L0_ffn_setup()
    _L0_ffn_in = {k: v for k, v in _L0_ffn_all.items() if k in ('W1', 'b1', 'W2', 'b2', 'Wa', 'Wb')}
    del _L0_ffn_all

    def _L1_attn_setup():
        import jax, jax.numpy as jnp
        import numpy as np
        CHUNK = 64
        NORM_EPS = 1e-05
        DENOM_EPS = 1.0
        B, S, HID, H = (4, 512, 128, 8)
        D = HID // H

        def rmsnorm(x, w, eps=NORM_EPS):
            var = jnp.mean(x * x, axis=-1, keepdims=True)
            return x * jax.lax.rsqrt(var + eps) * w

        def chunked_linear_attn(q, k, v):
            b, s, h, d = q.shape
            n = s // CHUNK

            def to_chunks(x):
                return x.reshape(b, n, CHUNK, h, d).transpose(1, 0, 3, 2, 4)
            qc, kc, vc = (to_chunks(q), to_chunks(k), to_chunks(v))
            mask = jnp.tril(jnp.ones((CHUNK, CHUNK), dtype=q.dtype))

            def step(state, inp):
                qq, kk, vv = inp
                inter = jnp.einsum('bhcd,bhde->bhce', qq, state)
                scores = jnp.einsum('bhcd,bhed->bhce', qq, kk) * mask
                intra = jnp.einsum('bhce,bhed->bhcd', scores, vv)
                state = state + jnp.einsum('bhcd,bhce->bhde', kk, vv)
                return (state, inter + intra)
            init = jnp.zeros((b, h, d, d), dtype=q.dtype)
            _, o = jax.lax.scan(step, init, (qc, kc, vc))
            return o.transpose(1, 0, 3, 2, 4).reshape(b, s, h, d)
        key = jax.random.key(seed)
        k0, k1, k2, k3, k4 = jax.random.split(key, 5)
        hidden_states = jax.random.normal(k0, (B, S, HID), dtype=jnp.float32)
        Wq = jax.random.normal(k1, (HID, HID), dtype=jnp.float32) * 0.02
        Wk = jax.random.normal(k2, (HID, HID), dtype=jnp.float32) * 0.02
        Wv = jax.random.normal(k3, (HID, HID), dtype=jnp.float32) * 0.02
        Wo = jax.random.normal(k4, (HID, HID), dtype=jnp.float32) * 0.02
        norm_w = jnp.ones((D,), dtype=jnp.float32)
        return {'hidden_states': hidden_states, 'Wq': Wq, 'Wk': Wk, 'Wv': Wv, 'Wo': Wo, 'norm_w': norm_w}
    _L1_attn_all = _L1_attn_setup()
    _L1_attn_in = {k: v for k, v in _L1_attn_all.items() if k in ('Wq', 'Wk', 'Wv', 'Wo', 'norm_w')}
    del _L1_attn_all

    def _L1_xattn_setup():
        import jax, jax.numpy as jnp
        import numpy as np
        key = jax.random.key(seed)
        k1, k2, k3, k4, k5 = jax.random.split(key, 5)
        B, K, S, E, I, D = (4, 2, 64, 8, 128, 256)
        x = jax.random.normal(k1, (B, S, I), dtype=jnp.float32)
        weights = jax.random.uniform(k2, (B, K, S), dtype=jnp.float32)
        ensembles = jax.random.randint(k3, (B, K, S), 0, E, dtype=jnp.int64)
        lim1 = float(np.sqrt(6.0 / (D + I)))
        proj_in = jax.random.uniform(k4, (E, D, I), dtype=jnp.float32, minval=-lim1, maxval=lim1)
        proj_out = jax.random.uniform(k5, (E, I, D), dtype=jnp.float32, minval=-lim1, maxval=lim1)
        return {'x': x, 'weights': weights, 'ensembles': ensembles, 'proj_in': proj_in, 'proj_out': proj_out}
    _L1_xattn_all = _L1_xattn_setup()
    _L1_xattn_in = {k: v for k, v in _L1_xattn_all.items() if k in ('proj_in', 'proj_out')}
    del _L1_xattn_all

    def _L1_ffn_setup():
        import jax, jax.numpy as jnp
        import numpy as np
        B, N, D, F, E, K = (4, 256, 128, 512, 16, 2)
        EPS = 1e-05
        key = jax.random.key(seed)
        ks = jax.random.split(key, 6)
        scaled = lambda k, shape, fan: jax.random.normal(k, shape, jnp.float32) / np.float32(np.sqrt(fan))
        return {'x': jax.random.normal(ks[0], (B, N, D), jnp.float32), 'Wr': scaled(ks[1], (D, E), D), 'br': jnp.zeros((E,), jnp.float32), 'W1': scaled(ks[2], (E, D, F), D), 'W3': scaled(ks[3], (E, D, F), D), 'W2': scaled(ks[4], (E, F, D), F), 'gamma': jnp.ones((E, D), jnp.float32), 'beta': jnp.zeros((E, D), jnp.float32)}
    _L1_ffn_all = _L1_ffn_setup()
    _L1_ffn_in = {k: v for k, v in _L1_ffn_all.items() if k in ('Wr', 'br', 'W1', 'W3', 'W2', 'gamma', 'beta')}
    del _L1_ffn_all
    return {'x': x, 'ctx_512': ctx_512, 'itok_BxS2xS_0_7': itok_BxS2xS_0_7, 'L0_attn_wq': _L0_attn_in['wq'], 'L0_attn_bq': _L0_attn_in['bq'], 'L0_attn_wk': _L0_attn_in['wk'], 'L0_attn_bk': _L0_attn_in['bk'], 'L0_attn_wv': _L0_attn_in['wv'], 'L0_attn_bv': _L0_attn_in['bv'], 'L0_attn_wo': _L0_attn_in['wo'], 'L0_attn_bo': _L0_attn_in['bo'], 'L0_xattn_Wq': _L0_xattn_in['Wq'], 'L0_xattn_Wk': _L0_xattn_in['Wk'], 'L0_xattn_Wv': _L0_xattn_in['Wv'], 'L0_xattn_Wo': _L0_xattn_in['Wo'], 'L0_xattn_bo': _L0_xattn_in['bo'], 'L0_ffn_W1': _L0_ffn_in['W1'], 'L0_ffn_b1': _L0_ffn_in['b1'], 'L0_ffn_W2': _L0_ffn_in['W2'], 'L0_ffn_b2': _L0_ffn_in['b2'], 'L0_ffn_Wa': _L0_ffn_in['Wa'], 'L0_ffn_Wb': _L0_ffn_in['Wb'], 'L1_attn_Wq': _L1_attn_in['Wq'], 'L1_attn_Wk': _L1_attn_in['Wk'], 'L1_attn_Wv': _L1_attn_in['Wv'], 'L1_attn_Wo': _L1_attn_in['Wo'], 'L1_attn_norm_w': _L1_attn_in['norm_w'], 'L1_xattn_proj_in': _L1_xattn_in['proj_in'], 'L1_xattn_proj_out': _L1_xattn_in['proj_out'], 'L1_ffn_Wr': _L1_ffn_in['Wr'], 'L1_ffn_br': _L1_ffn_in['br'], 'L1_ffn_W1': _L1_ffn_in['W1'], 'L1_ffn_W3': _L1_ffn_in['W3'], 'L1_ffn_W2': _L1_ffn_in['W2'], 'L1_ffn_gamma': _L1_ffn_in['gamma'], 'L1_ffn_beta': _L1_ffn_in['beta']}

def reference(x, ctx_512, itok_BxS2xS_0_7, L0_attn_wq, L0_attn_bq, L0_attn_wk, L0_attn_bk, L0_attn_wv, L0_attn_bv, L0_attn_wo, L0_attn_bo, L0_xattn_Wq, L0_xattn_Wk, L0_xattn_Wv, L0_xattn_Wo, L0_xattn_bo, L0_ffn_W1, L0_ffn_b1, L0_ffn_W2, L0_ffn_b2, L0_ffn_Wa, L0_ffn_Wb, L1_attn_Wq, L1_attn_Wk, L1_attn_Wv, L1_attn_Wo, L1_attn_norm_w, L1_xattn_proj_in, L1_xattn_proj_out, L1_ffn_Wr, L1_ffn_br, L1_ffn_W1, L1_ffn_W3, L1_ffn_W2, L1_ffn_gamma, L1_ffn_beta):
    import jax
    import jax.numpy as jnp

    def _L0_attn_ref(x, wq, bq, wk, bk, wv, bv, wo, bo):
        import jax, jax.numpy as jnp
        import numpy as np
        HEADS = 16

        def _fm(t):
            return jax.nn.elu(t) + 1.0
        B, N, D = x.shape
        H = HEADS
        Dh = D // H
        q = _fm((x @ wq + bq).reshape(B, N, H, Dh))
        k = _fm((x @ wk + bk).reshape(B, N, H, Dh))
        v = (x @ wv + bv).reshape(B, N, H, Dh)
        kv = jnp.einsum('bnhd,bnhe->bhde', k, v)
        z = 1.0 / (jnp.einsum('bnhd,bhd->bnh', q, k.sum(axis=1)) + 1e-06)
        scores = jnp.einsum('bnhd,bhde,bnh->bnhe', q, kv, z)
        out = scores.reshape(B, N, D) @ wo + bo
        return out

    def _L0_xattn_ref(q, kv, Wq, Wk, Wv, Wo, bo):
        import jax, jax.numpy as jnp
        import numpy as np
        NUM_HEADS = 16
        HEAD_DIM = 64
        Q_DIM = 128
        KV_DIM = 64
        INNER = NUM_HEADS * HEAD_DIM
        B, N, _ = q.shape
        M = kv.shape[1]
        scale = HEAD_DIM ** (-0.5)
        qh = (q @ Wq).reshape(B, N, NUM_HEADS, HEAD_DIM).transpose(0, 2, 1, 3)
        kh = (kv @ Wk).reshape(B, M, NUM_HEADS, HEAD_DIM).transpose(0, 2, 1, 3)
        vh = (kv @ Wv).reshape(B, M, NUM_HEADS, HEAD_DIM).transpose(0, 2, 1, 3)
        scores = jnp.einsum('bhnd,bhmd->bhnm', qh, kh) * scale
        attn = jax.nn.softmax(scores, axis=-1)
        out = jnp.einsum('bhnm,bhmd->bhnd', attn, vh)
        out = out.transpose(0, 2, 1, 3).reshape(B, N, INNER)
        return out @ Wo + bo

    def _L0_ffn_ref(x, W1, b1, W2, b2, Wa, Wb):
        import jax, jax.numpy as jnp
        import numpy as np
        D_MODEL = 128
        D_FF = 512
        N_ZONES = 8
        TOP_K = 3
        ROUTER_H = 32
        BATCH = 16
        SEQ = 256
        pooled = x.mean(axis=1)
        h = jnp.tanh(pooled @ W1 + b1)
        logits = h @ W2 + b2
        probs = jax.nn.softmax(logits, axis=-1)
        top_p, top_i = jax.lax.top_k(probs, TOP_K)
        top_w = top_p / top_p.sum(axis=-1, keepdims=True)
        onehot = jax.nn.one_hot(top_i, N_ZONES, dtype=x.dtype)
        w = jnp.einsum('bk,bke->be', top_w, onehot)
        zone_outputs = jnp.zeros_like(x)
        for e in range(N_ZONES):
            z = jax.nn.gelu(x @ Wa[e]) @ Wb[e]
            zone_outputs = zone_outputs + z * w[:, e, None, None]
        return x + zone_outputs

    def _L1_attn_ref(hidden_states, Wq, Wk, Wv, Wo, norm_w):
        import jax, jax.numpy as jnp
        import numpy as np
        CHUNK = 64
        NORM_EPS = 1e-05
        DENOM_EPS = 1.0
        B, S, HID, H = (4, 512, 128, 8)
        D = HID // H

        def rmsnorm(x, w, eps=NORM_EPS):
            var = jnp.mean(x * x, axis=-1, keepdims=True)
            return x * jax.lax.rsqrt(var + eps) * w

        def chunked_linear_attn(q, k, v):
            b, s, h, d = q.shape
            n = s // CHUNK

            def to_chunks(x):
                return x.reshape(b, n, CHUNK, h, d).transpose(1, 0, 3, 2, 4)
            qc, kc, vc = (to_chunks(q), to_chunks(k), to_chunks(v))
            mask = jnp.tril(jnp.ones((CHUNK, CHUNK), dtype=q.dtype))

            def step(state, inp):
                qq, kk, vv = inp
                inter = jnp.einsum('bhcd,bhde->bhce', qq, state)
                scores = jnp.einsum('bhcd,bhed->bhce', qq, kk) * mask
                intra = jnp.einsum('bhce,bhed->bhcd', scores, vv)
                state = state + jnp.einsum('bhcd,bhce->bhde', kk, vv)
                return (state, inter + intra)
            init = jnp.zeros((b, h, d, d), dtype=q.dtype)
            _, o = jax.lax.scan(step, init, (qc, kc, vc))
            return o.transpose(1, 0, 3, 2, 4).reshape(b, s, h, d)
        b, s, _ = hidden_states.shape
        q = jnp.einsum('bsd,ed->bse', hidden_states, Wq).reshape(b, s, H, D)
        k = jnp.einsum('bsd,ed->bse', hidden_states, Wk).reshape(b, s, H, D)
        v = jnp.einsum('bsd,ed->bse', hidden_states, Wv).reshape(b, s, H, D)
        o = chunked_linear_attn(q, k, v)
        z = jnp.cumsum(k, axis=1)
        denom = jnp.maximum(jnp.abs(jnp.sum(q * z, axis=-1)), DENOM_EPS)[..., None]
        o = o / denom
        o = rmsnorm(o, norm_w)
        o = o.reshape(b, s, H * D)
        return jnp.einsum('bse,de->bsd', o, Wo)

    def _L1_xattn_ref(x, weights, ensembles, proj_in, proj_out):
        import jax, jax.numpy as jnp
        import numpy as np
        E = proj_in.shape[0]
        h = jax.nn.relu(jnp.einsum('edi,bsi->bsed', proj_in, x))
        o = jnp.einsum('eid,bsed->bsei', proj_out, h)
        onehot = jax.nn.one_hot(ensembles, E, dtype=x.dtype)
        gate = jnp.einsum('bks,bkse->bse', weights, onehot)
        return jnp.einsum('bsei,bse->bsi', o, gate)

    def _L1_ffn_ref(x, Wr, br, W1, W3, W2, gamma, beta):
        import jax, jax.numpy as jnp
        import numpy as np
        B, N, D, F, E, K = (4, 256, 128, 512, 16, 2)
        EPS = 1e-05
        b, n, d = x.shape
        e = Wr.shape[1]
        xf = x.reshape(-1, d)
        logits = xf @ Wr + br
        probs = jax.nn.softmax(logits, axis=-1)
        vals, idx = jax.lax.top_k(probs, K)
        w = vals / vals.sum(axis=-1, keepdims=True)
        combine = jnp.zeros((xf.shape[0], e), x.dtype)
        for k in range(K):
            combine = combine + w[:, k:k + 1] * jax.nn.one_hot(idx[:, k], e, dtype=x.dtype)
        out = jnp.zeros_like(xf)
        for ei in range(e):
            h = jax.nn.silu(xf @ W1[ei]) * (xf @ W3[ei])
            y = h @ W2[ei]
            mu = y.mean(axis=-1, keepdims=True)
            var = ((y - mu) ** 2).mean(axis=-1, keepdims=True)
            y = (y - mu) * jax.lax.rsqrt(var + EPS) * gamma[ei] + beta[ei]
            out = out + combine[:, ei:ei + 1] * y
        return out.reshape(b, n, d)
    x = x + _L0_attn_ref(_layernorm(x, axis=-1), L0_attn_wq, L0_attn_bq, L0_attn_wk, L0_attn_bk, L0_attn_wv, L0_attn_bv, L0_attn_wo, L0_attn_bo)
    x = x + _L0_xattn_ref(_layernorm(x, axis=-1), ctx_512, L0_xattn_Wq, L0_xattn_Wk, L0_xattn_Wv, L0_xattn_Wo, L0_xattn_bo)
    x = x + _L0_ffn_ref(_layernorm(x, axis=-1), L0_ffn_W1, L0_ffn_b1, L0_ffn_W2, L0_ffn_b2, L0_ffn_Wa, L0_ffn_Wb)
    x = x + _L1_attn_ref(_layernorm(x, axis=-1), L1_attn_Wq, L1_attn_Wk, L1_attn_Wv, L1_attn_Wo, L1_attn_norm_w)
    x = x + _L1_xattn_ref(_layernorm(x, axis=-1), ctx_512, itok_BxS2xS_0_7, L1_xattn_proj_in, L1_xattn_proj_out)
    x = x + _L1_ffn_ref(_layernorm(x, axis=-1), L1_ffn_Wr, L1_ffn_br, L1_ffn_W1, L1_ffn_W3, L1_ffn_W2, L1_ffn_gamma, L1_ffn_beta)
    return x

_drawn_inputs = setup_inputs


def setup_inputs(seed=0):
    import zlib

    import numpy as np

    out = dict(_drawn_inputs(seed))
    spreads = {'L0_attn_bq': (0.0, 2.0),
     'L0_attn_bk': (0.0, 2.0),
     'L0_attn_bv': (0.0, 0.1),
     'L0_attn_bo': (0.0, 0.1),
     'L0_ffn_b1': (0.0, 0.1),
     'L0_ffn_b2': (0.0, 0.1),
     'L1_attn_norm_w': (1.0, 0.6),
     'L1_ffn_br': (0.0, 0.346),
     'L1_ffn_gamma': (1.0, 0.6),
     'L1_ffn_beta': (0.0, 0.8)}
    factors = {'L0_xattn_bo': 4.07, 'L0_attn_wq': 3.264}
    for name, (base, spread) in spreads.items():
        noise = np.random.default_rng([zlib.crc32(name.encode()), seed]).standard_normal(out[name].shape)
        drawn = base * np.exp(spread * noise) if base else spread * noise
        out[name] = jnp.asarray(drawn.astype(out[name].dtype))
    for name, factor in factors.items():
        out[name] = (out[name] * factor).astype(out[name].dtype)
    return out
```

```python
from contextlib import ExitStack

import numpy as np

import concourse.bass as bass
from concourse import mybir
from concourse.alu_op_type import AluOpType as ALU

ACT = mybir.ActivationFunctionType
AX = mybir.AxisListType
F32 = mybir.dt.float32
I32 = mybir.dt.int32
U32 = mybir.dt.uint32

B, S, D = 32, 64, 128
P = 128
T = B * S // P
PAIR = 2
EPS = 1e-5
H0, DH0 = 16, 8
HX, DX = 16, 64
CD = 64
JX = HX * CD // P
E0, F0, K0, R0 = 8, 512, 3, 32
H1, D1 = 8, 16
EX, FX = 8, 256
E1, F1, K1 = 16, 512, 2
SLOTS = (K1 * B * S + E1 * (P - 1)) // P // PAIR * PAIR + PAIR
CONST_WIDTHS = [P, P + H0, H1, P, P, E1, SLOTS]
G = 4
HEADROOM = 512


class Lane:

    def __init__(self, plan, engine, sem, step=1):
        self.plan, self.engine, self.sem, self.step = plan, engine, sem, step
        self.base, self.n = 0, 0
        plan.lanes.append(self)

    def value(self, n, passes_back=0):
        if self.plan.i is None:
            return self.base + n
        per = self.per()
        return self.plan.i * per + (self.base + n - passes_back * per)

    def per(self):
        return self.plan.counts.get((self.plan.loop, self.plan.lanes.index(self)), 0)

    def did(self, instruction, label=None):
        instruction.then_inc(self.sem, self.step)
        self.n += self.step
        if label:
            self.plan.noted[(self.plan.loop, label)] = (self.plan.lanes.index(self), self.n)
        return self.total()

    def after(self, *marks):
        latest = {}
        for lane, passes_back, n in filter(None, marks):
            latest[lane] = max(latest.get(lane, (-2, 0)), (-passes_back, n))
        for lane, (behind, n) in latest.items():
            self.engine.wait_ge(lane.sem, lane.value(n, -behind))

    def apart(self, *marks):
        self.after(*marks)
        self.engine.sem_inc(self.plan.spare)

    def total(self):
        return self, 0, self.n


class Plan:

    def __init__(self, nc, known):
        self.nc, self.lanes, self.i, self.loop = nc, [], None, 0
        self.counts, self.labels = known or ({}, {})
        self.seen, self.noted = {}, {}

    def run(self, passes, body):
        self.loop += 1
        for lane in self.lanes:
            lane.base, lane.n = lane.base + lane.n, 0
        with self.nc.Fori(0, passes) as i:
            self.i = i
            body(i)
        self.i = None
        for k, lane in enumerate(self.lanes):
            self.seen[(self.loop, k)] = lane.n
            lane.base, lane.n = lane.base + passes * lane.n, 0

    def prev(self, label):
        k, n = self.labels.get((self.loop, label), (None, 0))
        return None if k is None else (self.lanes[k], 1, n)


def side_by_side(*steps):
    steps = list(steps)
    while steps:
        steps = [g for g in steps if next(g, "end") != "end"]


def build(nc, a, out, known=None, stages=6):
    plan = Plan(nc, known)
    a = dict(a)
    a["routes_w"] = nc.dram_tensor("routes_w", (B, E0), F32, kind="Internal").ap()
    for n in ("routed_rows", "expert_rows"):
        a[n] = nc.dram_tensor(n, (SLOTS * P, D), F32, kind="Internal").ap()
    ctx = ExitStack()
    with ctx:
        def sem(name):
            return ctx.enter_context(nc.semaphore(name))

        def sb(name, shape, dt=F32, at=None):
            return (at or ctx).enter_context(nc.sbuf_tensor(name, shape, dt))

        plan.spare = sem("spare")
        pe = Lane(plan, nc.tensor, sem("pe_done"))
        dve = Lane(plan, nc.vector, sem("dve_done"))
        act = Lane(plan, nc.scalar, sem("act_done"))
        pool = Lane(plan, nc.gpsimd, sem("pool_done"))
        sp = Lane(plan, nc.sync, sem("sp_done"))
        for lane in (pe, dve, act, pool):
            lane.engine.sem_inc(lane.sem, HEADROOM)
            lane.base = HEADROOM

        def loads(name):
            lane = Lane(plan, nc.sync, sem(name), 16)
            lane.engine.sem_inc(lane.sem, 16)
            lane.base = 16
            return lane

        bank = [[ctx.enter_context(nc.psum_tensor(f"bank{s}{k}", [P, 512], F32)) for k in range(4)]
                for s in range(PAIR)]
        wide = None

        def all_wait():
            marks = [lane.total() for lane in (pe, dve, act, pool)]
            for lane in (pe, dve, act, pool, sp):
                lane.after(*[m for m in marks if m[0] is not lane])
                lane.after(*[m for m in marks if m[0] is lane])

        x_ld, c_ld, w_ld, out_st = loads("x_loaded"), loads("consts_loaded"), loads("weights_loaded"), loads("stored")
        X = sb("X", [P, T, D])
        consts = sb("consts", [P, a["consts"].shape[1]])
        at = iter(np.cumsum([0] + CONST_WIDTHS).tolist())
        ident, same_head0, head_of1, causal, before, ids, slot_start = (
            consts[:, c:c + w] for c, w in zip(at, CONST_WIDTHS))
        neghalf = sb("neghalf", [P, H1])
        h = [sb(f"h{s}", [P, D]) for s in range(PAIR)]
        hT = [sb(f"hT{s}", [P, P]) for s in range(PAIR)]
        o_tok = [sb(f"o_tok{s}", [P, D]) for s in range(PAIR)]
        oT = [sb(f"oT{s}", [P, P]) for s in range(PAIR)]
        stat = [sb(f"stat{s}", [P, 6]) for s in range(PAIR)]
        mv = [sb(f"mv{s}", [P, 2]) for s in range(PAIR)]
        ve = [sb(f"ve{s}", [P, 1]) for s in range(PAIR)]
        rstd = [sb(f"rstd{s}", [P, 1]) for s in range(PAIR)]

        def load(ld, dst, src, q=nc.sync):
            return ld.did(q.dma_start(dst, src))

        def row(src, parts=P):
            return src.rearrange("(o n) -> o n", o=1).to_broadcast([parts, src.shape[0]])

        x_view = a["x"].rearrange("b s d -> (b s) d").rearrange("(t p) d -> p t d", p=P)
        load(c_ld, consts[:], a["consts"])
        for k in range(4):
            load(x_ld, X[:, 4 * k:4 * k + 4, :], x_view[:, 4 * k:4 * k + 4, :])
        HT = sb("HT", [P, T, P])
        zones_ld, ens_ld = loads("zone_weights_loaded"), loads("ensemble_weights_loaded")
        narrow_mem = sb("narrow_mem", [P, 2 * E0 * F0])
        wza = narrow_mem[:, 0:E0 * F0].rearrange("p (e f) -> p e f", e=E0)
        wzb = narrow_mem[:, E0 * F0:].rearrange("p (e c d) -> p e c d", e=E0, d=D)
        assert 2 * E0 * F0 == E1 * F1
        w2e = narrow_mem[:].rearrange("p (e d) -> p e d", d=D)
        w13 = sb("w13", [P, E1, 2 * F1])
        experts_ld, narrow_ld = loads("expert_weights_loaded"), loads("expert_second_weights_loaded")
        wpi, wpo = sb("wpi", [P, EX, FX]), sb("wpo", [P, EX, FX // P, D])
        neghalf_set = pool.did(nc.gpsimd.memset(neghalf[:], -0.5))

        def fill(dst, value):
            pool.after(pool.total())
            return pool.did(nc.gpsimd.memset(dst, value))

        def normalise(t, s, dst=None):
            dst = h[s][:] if dst is None else dst
            m = dve.did(nc.vector.bn_stats(stat[s][:], X[:, t, :]))
            dve.apart(m)
            moments = dve.did(nc.vector.bn_aggr(mv[s][:], stat[s][:]))
            dve.after(moments)
            var_eps = dve.did(nc.vector.tensor_scalar(ve[s][:], mv[s][:, 1:2], EPS, None, ALU.add))
            pool.after(var_eps)
            inverse = pool.did(nc.gpsimd.tensor_tensor(rstd[s][:], ve[s][:], neghalf[:, 0:1], ALU.pow))
            yield
            dve.after(inverse, plan.prev(f"h_turned{s}"))
            normed = dve.did(nc.vector.tensor_scalar(dst, X[:, t, :], mv[s][:, 0:1], rstd[s][:, 0:1],
                                                     ALU.subtract, ALU.mult))
            pe.after(normed)

        def transpose_h(s, dst=None):
            pe.after(plan.prev(f"h_moved{s}"))
            turned = pe.did(nc.tensor.transpose(bank[s][0][:, 0:P], h[s][:], ident), f"h_turned{s}")
            act.after(turned)
            return act.did(nc.scalar.activation(hT[s][:] if dst is None else dst, bank[s][0][:, 0:P], ACT.Copy), f"h_moved{s}")

        def experts(g, count, chunks, w_up, w_down, hid, gate, gelu):
            ups, outs = [bank[0][0], bank[1][0], bank[0][1], bank[1][1]], [bank[0][2], bank[1][2]]
            last = {}

            def read(label, mark):
                last[label] = mark
                return mark

            for e in range(count + 1):
                if e < count:
                    made = []
                    for c in range(chunks):
                        r = (e * chunks + c) % len(ups)
                        up = ups[r]
                        pe.after(last.get(f"up{r}") or plan.prev(f"up{r}"))
                        wide = pe.did(nc.tensor.matmul(up[:], w_up[:, e, c * P:(c + 1) * P], HT[:, bass.ds(g * G, G), :],
                                                       start=True, stop=True))
                        dst = hid[e % 2][:, c, :]
                        if gelu or c % 2 == 0:
                            act.after(wide)
                            made.append(read(f"up{r}", act.did(nc.scalar.activation(dst, up[:], gelu or ACT.Relu), f"up{r}")))
                        else:
                            dve.after(wide)
                            made.append(read(f"up{r}", dve.did(nc.vector.tensor_scalar(dst, up[:], 0.0, None, ALU.max), f"up{r}")))
                if e > 0:
                    f = e - 1
                    o = outs[f % 2]
                    pe.after(*ready, last.get(f"out{f % 2}") or plan.prev(f"out{f % 2}"))
                    for j in range(G):
                        for c in range(chunks):
                            m = nc.tensor.matmul(o[:, j * P:(j + 1) * P], hid[f % 2][:, c, j * P:(j + 1) * P],
                                                 w_down[:, f, c, :], start=(c == 0), stop=(c == chunks - 1))
                    narrow = pe.did(m)
                    dve.after(narrow, dve.total())
                    for j in range(G):
                        added = dve.did(nc.vector.scalar_tensor_tensor(
                            out=X[:, g * G + j, :], in0=o[:, j * P:(j + 1) * P], scalar=gate[:, g * G + j, f:f + 1],
                            in1=X[:, g * G + j, :], op0=ALU.mult, op1=ALU.add), f"out{f % 2}")
                    read(f"out{f % 2}", added)
                ready = made

        w1 = ExitStack()
        wq0, wkv0, wo0 = sb("wq0", [P, D], at=w1), sb("wkv0", [P, 2 * D], at=w1), sb("wo0", [P, D], at=w1)
        bq0, bkv0, bo0 = sb("bq0", [P, 1], at=w1), sb("bkv0", [P, 2 * D], at=w1), sb("bo0", [P, D], at=w1)
        load(w_ld, wq0[:], a["L0_attn_wq"])
        load(w_ld, wkv0[:, 0:D], a["L0_attn_wk"])
        load(w_ld, wkv0[:, D:2 * D], a["L0_attn_wv"])
        load(w_ld, wo0[:], a["L0_attn_wo"])
        load(w_ld, bq0[:], a["L0_attn_bq"].rearrange("(n o) -> n o", o=1))
        load(w_ld, bkv0[:, 0:D], row(a["L0_attn_bk"]))
        load(w_ld, bkv0[:, D:2 * D], row(a["L0_attn_bv"]))
        load(w_ld, bo0[:], row(a["L0_attn_bo"]))

        load(zones_ld, wza, a["L0_ffn_Wa"].rearrange("e d f -> d e f"))
        load(zones_ld, wzb.rearrange("p e c d -> p (e c) d"), a["L0_ffn_Wb"].rearrange("e (c p) d -> p (e c) d", p=P))
        load(experts_ld, w13[:, :, 0:F1], a["L1_ffn_W1"].rearrange("e d f -> d e f"))
        load(experts_ld, w13[:, :, F1:], a["L1_ffn_W3"].rearrange("e d f -> d e f"))
        load(ens_ld, wpi[:], a["proj_inT"])
        load(ens_ld, wpo[:].rearrange("p e c i -> p (e c) i"), a["proj_outT"].rearrange("e (c p) i -> p (e c) i", p=P))

        qf = [sb(f"qf{s}", [P, P], at=w1) for s in range(PAIR)]
        eq = [sb(f"eq{s}", [P, P], at=w1) for s in range(PAIR)]
        kb = [sb(f"kb{s}", [P, D], at=w1) for s in range(PAIR)]
        ek = [sb(f"ek{s}", [P, D], at=w1) for s in range(PAIR)]
        kf = [sb(f"kf{s}", [P, D], at=w1) for s in range(PAIR)]
        vones = [sb(f"vones{s}", [P, 2, D + H0], at=w1) for s in range(PAIR)]
        kvsum = [sb(f"kvsum{s}", [P, 2, D + H0], at=w1) for s in range(PAIR)]
        den = [sb(f"den{s}", [P, H0], at=w1) for s in range(PAIR)]
        for s in range(PAIR):
            fill(vones[s][:], 0.0)
            fill(vones[s][0:S, 0, D:], 1.0)
            fill(vones[s][S:P, 1, D:], 1.0)
        for lane in (pe, dve, act, pool):
            lane.after(pool.total(), x_ld.total(), c_ld.total(), w_ld.total())

        def linear_attention(t, s):
            yield from normalise(t, s)
            dve.after()
            pool.after(dve.total())
            biased = pool.did(nc.gpsimd.tensor_tensor(X[:, t, :], X[:, t, :], bo0[:], ALU.add))
            hT_ready = transpose_h(s)
            yield
            pe.after(hT_ready)
            q_ready = pe.did(nc.tensor.matmul(bank[s][1][:, 0:P], wq0[:], hT[s][:], start=True, stop=True))
            kv_ready = pe.did(nc.tensor.matmul(bank[s][2][:, 0:2 * D], hT[s][:], wkv0[:], start=True, stop=True))
            yield
            act.after(q_ready)
            q_exp = act.did(nc.scalar.activation(eq[s][:], bank[s][1][:, 0:P], ACT.Exp, bias=bq0[:, 0:1]))
            dve.after(kv_ready)
            k_biased = dve.did(nc.vector.tensor_tensor(kb[s][:], bank[s][2][:, 0:D], bkv0[:, 0:D], ALU.add))
            act.after(k_biased)
            k_exp = act.did(nc.scalar.activation(ek[s][:], kb[s][:], ACT.Exp))
            for half, slot in ((slice(0, S), 0), (slice(S, P), 1)):
                v_set = dve.did(nc.vector.tensor_tensor(vones[s][half, slot, 0:D], bank[s][2][half, D:2 * D],
                                                        bkv0[half, D:2 * D], ALU.add))
            yield
            dve.after(q_exp)
            q_relu = dve.did(nc.vector.tensor_scalar(qf[s][:], bank[s][1][:, 0:P], bq0[:, 0:1], 0.0, ALU.add, ALU.max))
            dve.after(q_relu)
            q_mapped = dve.did(nc.vector.scalar_tensor_tensor(out=qf[s][:], in0=eq[s][:], scalar=1.0, in1=qf[s][:],
                                                              op0=ALU.min, op1=ALU.add))
            dve.after(k_exp)
            e_min = dve.did(nc.vector.tensor_scalar(ek[s][:], ek[s][:], 1.0, None, ALU.min))
            dve.after(e_min)
            k_mapped = dve.did(nc.vector.scalar_tensor_tensor(out=kf[s][:], in0=kb[s][:], scalar=0.0, in1=ek[s][:],
                                                              op0=ALU.max, op1=ALU.add))
            pe.after(k_mapped, v_set)
            sums_ready = pe.did(nc.tensor.matmul(bank[s][3][:, 0:2 * (D + H0)], kf[s][:], vones[s][:].rearrange("p a d -> p (a d)"),
                                                 start=True, stop=True))
            yield
            dve.after(sums_ready)
            masked = dve.did(nc.vector.tensor_tensor(
                kvsum[s][:], bank[s][3][:, 0:2 * (D + H0)].rearrange("p (a d) -> p a d", a=2),
                same_head0.unsqueeze(1).to_broadcast([P, 2, D + H0]), ALU.mult))
            pe.after(masked, q_mapped)
            for b in range(2):
                applied = pe.did(nc.tensor.matmul(bank[s][2][b * S:b * S + S, 0:D + H0], qf[s][:, b * S:b * S + S],
                                                  kvsum[s][:, b, :], start=True, stop=True))
            yield
            dve.after(applied)
            d1 = dve.did(nc.vector.tensor_scalar(den[s][:], bank[s][2][:, D:D + H0], 1e-6, None, ALU.add))
            dve.after(d1)
            d2 = dve.did(nc.vector.reciprocal(den[s][:], den[s][:]))
            dve.after(d2)
            divided = dve.did(nc.vector.tensor_tensor(
                o_tok[s][:].rearrange("p (h e) -> p h e", h=H0), bank[s][2][:, 0:D].rearrange("p (h e) -> p h e", h=H0),
                den[s][:].unsqueeze(2).to_broadcast([P, H0, DH0]), ALU.mult))
            pe.after(divided)
            turned = pe.did(nc.tensor.transpose(bank[s][0][:, 0:P], o_tok[s][:], ident))
            act.after(turned)
            oT_ready = act.did(nc.scalar.activation(oT[s][:], bank[s][0][:, 0:P], ACT.Copy))
            yield
            pe.after(oT_ready)
            projected = pe.did(nc.tensor.matmul(bank[s][1][:, P:2 * P], oT[s][:], wo0[:], start=True, stop=True))
            dve.after(projected, biased)
            dve.did(nc.vector.tensor_tensor(X[:, t, :], X[:, t, :], bank[s][1][:, P:2 * P], ALU.add))

        nc.scalar.preload_act_table(ACT.Exp)
        plan.run(T // PAIR, lambda i: side_by_side(*[linear_attention(i * PAIR + s, s) for s in range(PAIR)]))
        all_wait()
        w1.close()

        if stages >= 2:
            w2 = ExitStack()
            cx_ld = loads("cross_weights_loaded")
            keys_ld = [loads(f"keys_loaded{s}") for s in range(PAIR)]
            vals_ld = [loads(f"values_loaded{s}") for s in range(PAIR)]
            wqk = sb("wqk", [P, JX, P], at=w2)
            wvo = sb("wvo", [P, JX, D], at=w2)
            box = sb("box", [P, D], at=w2)
            w2a = ExitStack()
            wqT = sb("wqT", [P, JX, P], at=w2a)
            wkT = sb("wkT", [P, JX, P], at=w2a)
            wvT = sb("wvT", [P, JX, P], at=w2a)
            wox = sb("wox", [P, JX, D], at=w2a)
            z = [fill(wkT[:], 0.0), fill(wvT[:], 0.0)]
            sp.after(*z)
            load(cx_ld, wqT[:], a["L0_xattn_WqT"].rearrange("(j p) n -> p j n", p=P))
            load(cx_ld, wox[:], a["L0_xattn_Wo"].rearrange("(j p) n -> p j n", p=P))
            load(cx_ld, box[:], row(a["L0_xattn_bo"]))
            for w, name in ((wkT, "L0_xattn_WkT"), (wvT, "L0_xattn_WvT")):
                src = a[name].rearrange("(j g p) n -> g p j n", g=2, p=DX)
                for g in range(2):
                    load(cx_ld, w[g * DX:(g + 1) * DX, :, g * CD:(g + 1) * CD], src[g])
            pe.after(cx_ld.total())
            pool.after(cx_ld.total())
            for j in range(JX):
                o = bank[0][j // 4][:, (j % 4) * P:(j % 4 + 1) * P]
                nc.tensor.matmul(o, wqT[:, j, :], wkT[:, j, :], start=True, stop=True)
                o = bank[1][j // 4][:, (j % 4) * P:(j % 4 + 1) * P]
                made = pe.did(nc.tensor.matmul(o, wvT[:, j, :], wox[:, j, :], start=True, stop=True))
            dve.after(made)
            for k in range(2):
                dve.did(nc.vector.tensor_copy(wqk[:, 4 * k:4 * k + 4, :], bank[0][k][:].rearrange("p (j n) -> p j n", j=4)))
                dve.did(nc.vector.tensor_copy(wvo[:, 4 * k:4 * k + 4, :], bank[1][k][:].rearrange("p (j n) -> p j n", j=4)))
            all_wait()
            w2a.close()
            qx = [sb(f"qx{s}", [P, JX, P], at=w2) for s in range(PAIR)]
            pr = [sb(f"pr{s}", [P, HX, S], at=w2) for s in range(PAIR)]
            prT = [sb(f"prT{s}", [P, JX, P], at=w2) for s in range(PAIR)]
            ov = [sb(f"ov{s}", [P, JX, P], at=w2) for s in range(PAIR)]
            ctxT = [sb(f"ctxT{s}", [P, 2, P], at=w2) for s in range(PAIR)]
            ctxd = [sb(f"ctxd{s}", [P, 2, P], at=w2) for s in range(PAIR)]
            top = [sb(f"top{s}", [P, HX], at=w2) for s in range(PAIR)]
            tot = [sb(f"tot{s}", [P, HX], at=w2) for s in range(PAIR)]
            for s in range(PAIR):
                fill(ctxT[s][:], 0.0)
                fill(ctxd[s][:], 0.0)
            sp.after(pool.total())

            def cross_attention(t, s):
                sp.after(plan.prev(f"scores{s}"))
                for g in range(2):
                    d = slice(g * S, (g + 1) * S)
                    keys = load(keys_ld[s], ctxT[s][d, :, d], a["ctxT"][bass.ds(t * 2, 2)].rearrange("b c m -> c b m"))
                sp.after(plan.prev(f"values{s}"))
                for g in range(2):
                    d = slice(g * S, (g + 1) * S)
                    vals = load(vals_ld[s], ctxd[s][d, :, d], a["ctx_512"][bass.ds(t * 2, 2)].rearrange("b m c -> m b c"))
                yield from normalise(t, s)
                pool.after(dve.total())
                biased = pool.did(nc.gpsimd.tensor_tensor(X[:, t, :], X[:, t, :], box[:], ALU.add))
                hT_ready = transpose_h(s)
                yield
                pe.after(hT_ready)
                for j in range(JX):
                    q = pe.did(nc.tensor.matmul(bank[s][j // 4][:, (j % 4) * P:(j % 4 + 1) * P], wqk[:, j, :], hT[s][:],
                                                start=True, stop=True)) if j % 4 == 3 else \
                        nc.tensor.matmul(bank[s][j // 4][:, (j % 4) * P:(j % 4 + 1) * P], wqk[:, j, :], hT[s][:],
                                         start=True, stop=True)
                    if j == 3:
                        act.after(q)
                        q0 = act.did(nc.scalar.activation(qx[s][:, 0:4, :], bank[s][0][:].rearrange("p (j n) -> p j n", j=4), ACT.Copy))
                yield
                act.after(q)
                q1 = act.did(nc.scalar.activation(qx[s][:, 4:8, :], bank[s][1][:].rearrange("p (j n) -> p j n", j=4), ACT.Copy))
                pe.after(keys)
                for k, ready in ((0, q0), (1, q1)):
                    pe.after(ready)
                    for j in range(4 * k, 4 * k + 4):
                        for b in range(2):
                            sc = nc.tensor.matmul(bank[s][2 + k][b * S:(b + 1) * S, (j % 4) * P:(j % 4 + 1) * P],
                                                  qx[s][:, j, b * S:(b + 1) * S], ctxT[s][:, b, :], start=True, stop=True)
                    scored = pe.did(sc, f"scores{s}")
                    hs = slice(8 * k, 8 * k + 8)
                    ps = bank[s][2 + k][:].rearrange("p (h m) -> p h m", h=8)
                    dve.after(scored)
                    mx = dve.did(nc.vector.tensor_reduce(top[s][:, hs], ps, AX.X, ALU.max))
                    dve.after(mx)
                    shifted = dve.did(nc.vector.tensor_tensor(pr[s][:, hs, :], ps,
                                                              top[s][:, hs].unsqueeze(2).to_broadcast([P, 8, S]), ALU.subtract))
                    act.after(shifted)
                    ex = act.did(nc.scalar.activation(pr[s][:, hs, :], pr[s][:, hs, :], ACT.Exp, scale=DX ** -0.5))
                    if k == 0:
                        ex0 = ex
                yield
                for k, ready in ((0, ex0), (1, ex)):
                    hs = slice(8 * k, 8 * k + 8)
                    dve.after(ready)
                    summed = dve.did(nc.vector.tensor_reduce(tot[s][:, hs], pr[s][:, hs, :], AX.X, ALU.add))
                    dve.after(summed)
                    inv = dve.did(nc.vector.reciprocal(tot[s][:, hs], tot[s][:, hs]))
                    pool.after(inv)
                    p = pool.did(nc.gpsimd.tensor_tensor(pr[s][:, hs, :], pr[s][:, hs, :],
                                                         tot[s][:, hs].unsqueeze(2).to_broadcast([P, 8, S]), ALU.mult))
                    pe.after(p)
                    for j in range(4 * k, 4 * k + 4):
                        tr = nc.tensor.transpose(bank[s][k][:, (j % 4) * P:(j % 4 + 1) * P],
                                                 pr[s][:, 2 * j:2 * j + 2, :].rearrange("p h m -> p (h m)"), ident)
                    turned = pe.did(tr)
                    src = bank[s][k][:].rearrange("p (j n) -> p j n", j=4)
                    if k == 0:
                        act.after(turned)
                        t0 = act.did(nc.scalar.activation(prT[s][:, 0:4, :], src, ACT.Copy))
                    else:
                        dve.after(turned)
                        t1 = dve.did(nc.vector.tensor_copy(prT[s][:, 4:8, :], src))
                    yield
                pe.after(vals, t0, t1)
                for b in range(2):
                    mixed = pe.did(nc.tensor.matmul(bank[s][2 + b][:], ctxd[s][:, b, :], prT[s][:, :, b * S:(b + 1) * S],
                                                    start=True, stop=True), f"values{s}")
                    src = bank[s][2 + b][:].rearrange("p (j n) -> p j n", j=JX)
                    dst = ov[s][:, :, b * S:(b + 1) * S]
                    if b == 0:
                        act.after(mixed)
                        o0 = act.did(nc.scalar.activation(dst, src, ACT.Copy))
                    else:
                        dve.after(mixed)
                        o1 = dve.did(nc.vector.tensor_copy(dst, src))
                yield
                pe.after(o0, o1)
                for j in range(JX):
                    f = nc.tensor.matmul(bank[s][0][:, P:2 * P], ov[s][:, j, :], wvo[:, j, :], start=(j == 0), stop=(j == JX - 1))
                projected = pe.did(f)
                dve.after(projected, biased)
                dve.did(nc.vector.tensor_tensor(X[:, t, :], X[:, t, :], bank[s][0][:, P:2 * P], ALU.add))

            plan.run(T // PAIR, lambda i: side_by_side(*[cross_attention(i * PAIR + s, s) for s in range(PAIR)]))
            all_wait()
            w2.close()

        if stages >= 3:
            w3 = ExitStack()
            r_ld = loads("router_loaded")
            sent = loads("routes_sent")
            routes_ld = loads("routes_loaded")
            pooled = sb("pooled", [P, B], at=w3)
            rw1, rw2 = sb("rw1", [P, R0], at=w3), sb("rw2", [R0, E0], at=w3)
            rb1, rb2 = sb("rb1", [R0, 1], at=w3), sb("rb2", [B, E0], at=w3)
            rh = sb("rh", [R0, B], at=w3)
            prob = sb("prob", [B, E0], at=w3)
            one = sb("one", [B, 1], at=w3)
            best = sb("best", [B, 8], at=w3)
            best_at = sb("best_at", [B, 8], U32, at=w3)
            zone_w = sb("zone_w", [P, T, E0], at=w3)
            best_atf = sb("best_atf", [B, 8], at=w3)
            zone_b, picked0 = sb("zone_b", [B, E0], at=w3), sb("picked0", [B, E0], at=w3)
            load(r_ld, rw1[:], a["L0_ffn_W1"])
            load(r_ld, rw2[:], a["L0_ffn_W2"])
            load(r_ld, rb1[:], a["L0_ffn_b1"].rearrange("(n o) -> n o", o=1))
            load(r_ld, rb2[:], row(a["L0_ffn_b2"], B))

            def zone_input(t, s):
                yield from normalise(t, s)
                pool.after(dve.total())
                pool.did(nc.gpsimd.tensor_tensor(X[:, t, :], X[:, t, :], h[s][:], ALU.add))
                dve.after(transpose_h(s, HT[:, t, :]))
                dve.did(nc.vector.tensor_reduce(pooled[:, bass.ds(t * 2, 2)], HT[:, t, :].rearrange("p (b n) -> p b n", b=2),
                                                AX.X, ALU.add))

            plan.run(T // PAIR, lambda i: side_by_side(*[zone_input(i * PAIR + s, s) for s in range(PAIR)]))
            all_wait()
            pe.after(r_ld.total())
            hidden = pe.did(nc.tensor.matmul(bank[0][0][0:R0, 0:B], rw1[:], pooled[:], start=True, stop=True))
            act.after(hidden, r_ld.total())
            squashed = act.did(nc.scalar.activation(rh[:], bank[0][0][0:R0, 0:B], ACT.Tanh, bias=rb1[:, 0:1], scale=1.0 / S))
            pe.after(squashed)
            logits = pe.did(nc.tensor.matmul(bank[0][1][0:B, 0:E0], rh[:], rw2[:], start=True, stop=True))
            dve.after(logits, r_ld.total())
            step = dve.did(nc.vector.tensor_tensor(prob[:], bank[0][1][0:B, 0:E0], rb2[:], ALU.add))
            dve.after(step)
            step = dve.did(nc.vector.tensor_reduce(one[:], prob[:], AX.X, ALU.max))
            dve.after(step)
            step = dve.did(nc.vector.tensor_scalar(prob[:], prob[:], one[:, 0:1], None, ALU.subtract))
            act.after(step)
            raised = act.did(nc.scalar.activation(prob[:], prob[:], ACT.Exp))
            dve.after(raised)
            for src, scaled in ((prob[:], prob), (best[:, 0:K0], best)):
                step = dve.did(nc.vector.tensor_reduce(one[:], src, AX.X, ALU.add))
                dve.after(step)
                step = dve.did(nc.vector.reciprocal(one[:], one[:]))
                dve.after(step)
                if scaled is prob:
                    step = dve.did(nc.vector.tensor_scalar(prob[:], prob[:], one[:, 0:1], None, ALU.mult))
                    dve.after(step)
                    step = dve.did(nc.vector.max(best[:], prob[:]))
                    dve.after(step)
                    step = dve.did(nc.vector.max_index(best_at[:], best[:], prob[:]))
                    dve.after(step)
            step = dve.did(nc.vector.tensor_scalar(best[:], best[:], one[:, 0:1], None, ALU.mult))
            dve.after(step)
            step = dve.did(nc.vector.tensor_copy(best_atf[:], best_at[:]))
            dve.after(step)
            for k in range(K0):
                dst = zone_b if k == 0 else picked0
                step = dve.did(nc.vector.tensor_scalar(dst[:], ids[0:B, 0:E0], best_atf[:, k:k + 1], best[:, k:k + 1],
                                                       ALU.is_equal, ALU.mult))
                dve.after(step)
                if k > 0:
                    step = dve.did(nc.vector.tensor_tensor(zone_b[:], zone_b[:], picked0[:], ALU.add))
                    dve.after(step)
            sp.after(step)
            load(sent, a["routes_w"], zone_b[:])
            sp.after(sent.total())
            for g in range(2):
                load(routes_ld, zone_w[g * S:(g + 1) * S, :, :],
                     a["routes_w"].rearrange("(o t g) k -> g o t k", o=1, g=2)[g].to_broadcast([S, T, E0]))
            ghid = [sb(f"ghid{k}", [P, F0 // P, G * P], at=w3) for k in range(2)]
            for lane in (pe, dve, act, pool):
                lane.after(dve.total(), act.total(), routes_ld.total(), zones_ld.total())
            nc.scalar.preload_act_table(ACT.Gelu_apprx_tanh)
            plan.run(T // G, lambda g: experts(g, E0, F0 // P, wza, wzb, ghid, zone_w, ACT.Gelu_apprx_tanh))
            all_wait()
            w3.close()
            load(narrow_ld, w2e, a["L1_ffn_W2"].rearrange("e (c p) d -> p (e c) d", p=P))

        if stages >= 4:
            w4 = ExitStack()
            a_ld = loads("causal_weights_loaded")
            wqk1, wv1, wo1 = sb("wqk1", [P, 2, D], at=w4), sb("wv1", [P, D], at=w4), sb("wo1", [P, D], at=w4)
            nw1 = sb("nw1", [P, 1], at=w4)
            load(a_ld, wqk1[:, 0, :], a["L1_attn_WqT"])
            load(a_ld, wqk1[:, 1, :], a["L1_attn_WkT"])
            load(a_ld, wv1[:], a["L1_attn_WvT"])
            load(a_ld, wo1[:], a["L1_attn_WoT"])
            for k in range(H1):
                load(a_ld, nw1[k * D1:(k + 1) * D1, :], a["L1_attn_norm_w"].rearrange("(n o) -> n o", o=1))
            kT = [sb(f"kT{s}", [P, P], at=w4) for s in range(PAIR)]
            qh = [sb(f"qh{s}", [P, H1, P], at=w4) for s in range(PAIR)]
            sm = [sb(f"sm{s}", [P, H1, P], at=w4) for s in range(PAIR)]
            v1 = [sb(f"v1_{s}", [P, H1, D1 + 1], at=w4) for s in range(PAIR)]
            o17 = [sb(f"o17_{s}", [P, H1, D1 + 1], at=w4) for s in range(PAIR)]
            dn = [sb(f"dn{s}", [P, H1], at=w4) for s in range(PAIR)]
            sq = [sb(f"sq{s}", [P, H1, D1], at=w4) for s in range(PAIR)]
            on = [sb(f"on{s}", [P, H1, D1], at=w4) for s in range(PAIR)]
            for s in range(PAIR):
                fill(v1[s][:], 1.0)
            pool.after(a_ld.total())
            for lane in (pe, dve, act):
                lane.after(a_ld.total(), pool.total())
            step = dve.did(nc.vector.tensor_scalar(wo1[:], wo1[:], nw1[:, 0:1], None, ALU.mult))
            pe.after(step)
            HB = 3
            W17 = H1 * (D1 + 1)

            def causal_attention(t, s):
                yield from normalise(t, s)
                hT_ready = transpose_h(s)
                yield
                pe.after(hT_ready)
                nc.tensor.matmul(bank[s][1][:, 0:P], wqk1[:, 0, :], hT[s][:], start=True, stop=True)
                nc.tensor.matmul(bank[s][1][:, P:2 * P], wqk1[:, 1, :], hT[s][:], start=True, stop=True)
                projected = pe.did(nc.tensor.matmul(bank[s][1][:, 2 * P:3 * P], hT[s][:], wv1[:], start=True, stop=True))
                yield
                act.after(projected)
                k_ready = act.did(nc.scalar.activation(kT[s][:], bank[s][1][:, P:2 * P], ACT.Copy))
                v_ready = act.did(nc.scalar.activation(v1[s][:, :, 0:D1], bank[s][1][:, 2 * P:3 * P].rearrange("p (h d) -> p h d", h=H1), ACT.Copy))
                dve.after(v_ready)
                q_ready = dve.did(nc.vector.tensor_tensor(
                    qh[s][:], bank[s][1][:, 0:P].unsqueeze(1).to_broadcast([P, H1, P]),
                    head_of1.unsqueeze(2).to_broadcast([P, H1, P]), ALU.mult))
                yield
                pe.after(k_ready, q_ready)
                for k in range(2):
                    scored = pe.did(nc.tensor.matmul(bank[s][2 + k][:], kT[s][:], qh[s][:, 4 * k:4 * k + 4, :].rearrange("p h n -> p (h n)"),
                                                     start=True, stop=True))
                    dve.after(scored)
                    masked = dve.did(nc.vector.tensor_tensor(
                        sm[s][:, 4 * k:4 * k + 4, :], bank[s][2 + k][:].rearrange("p (h n) -> p h n", h=4),
                        causal.unsqueeze(1).to_broadcast([P, 4, P]), ALU.mult))
                yield
                pe.after(masked, v_ready)
                places = [(bank[s][(0, 1, 2)[hd // HB]], hd % HB) for hd in range(H1)]
                for hd, (bk, r) in enumerate(places):
                    m = nc.tensor.matmul(bk[:, r * W17:(r + 1) * W17], sm[s][:, hd, :],
                                         v1[s][:].rearrange("p h d -> p (h d)"), start=True, stop=True)
                mixed = pe.did(m)
                dve.after(mixed)
                for hd, (bk, r) in enumerate(places):
                    at = r * W17 + hd * (D1 + 1)
                    taken = dve.did(nc.vector.tensor_copy(o17[s][:, hd, :], bk[:, at:at + D1 + 1]))
                yield
                dve.after(taken)
                row_sum = o17[s][:, :, D1]
                step = dve.did(nc.vector.scalar_tensor_tensor(out=dn[s][:], in0=row_sum, scalar=-1.0, in1=row_sum,
                                                              op0=ALU.mult, op1=ALU.max))
                dve.after(step)
                step = dve.did(nc.vector.tensor_scalar(dn[s][:], dn[s][:], 1.0, None, ALU.max))
                dve.after(step)
                step = dve.did(nc.vector.reciprocal(dn[s][:], dn[s][:]))
                dve.after(step)
                wide_dn = dn[s][:].unsqueeze(2).to_broadcast([P, H1, D1])
                step = dve.did(nc.vector.tensor_tensor(on[s][:], o17[s][:, :, 0:D1], wide_dn, ALU.mult))
                dve.after(step)
                step = dve.did(nc.vector.tensor_tensor(sq[s][:], on[s][:], on[s][:], ALU.mult))
                dve.after(step)
                step = dve.did(nc.vector.tensor_reduce(dn[s][:], sq[s][:], AX.X, ALU.add))
                dve.after(step)
                step = dve.did(nc.vector.tensor_scalar(dn[s][:], dn[s][:], 1.0 / D1, EPS, ALU.mult, ALU.add))
                pool.after(step)
                rooted = pool.did(nc.gpsimd.tensor_tensor(dn[s][:], dn[s][:], neghalf[:, 0:H1], ALU.pow))
                yield
                dve.after(rooted)
                normed = dve.did(nc.vector.tensor_tensor(on[s][:], on[s][:], wide_dn, ALU.mult))
                pe.after(normed)
                turned = pe.did(nc.tensor.transpose(bank[s][0][:, 0:P], on[s][:].rearrange("p h d -> p (h d)"), ident))
                act.after(turned)
                oT_ready = act.did(nc.scalar.activation(oT[s][:], bank[s][0][:, 0:P], ACT.Copy))
                yield
                pe.after(oT_ready)
                projected = pe.did(nc.tensor.matmul(bank[s][3][:, 0:P], oT[s][:], wo1[:], start=True, stop=True))
                dve.after(projected)
                dve.did(nc.vector.tensor_tensor(X[:, t, :], X[:, t, :], bank[s][3][:, 0:P], ALU.add))

            plan.run(T // PAIR, lambda i: side_by_side(*[causal_attention(i * PAIR + s, s) for s in range(PAIR)]))
            all_wait()
            w4.close()

        if stages >= 5:
            w5 = ExitStack()
            g_ld = loads("gates_loaded")
            chosen = sb("chosen", [P, T, S], I32, at=w5)
            weight = sb("weight", [P, T, CD], at=w5)
            picked = sb("picked", [P, T, S], at=w5)
            gate = sb("gate", [P, T, EX], at=w5)
            hid = [sb(f"hid{k}", [P, 2, G * P], at=w5) for k in range(2)]
            load(g_ld, chosen[:], a["itok_tokens"].rearrange("(t p) k -> p t k", p=P))
            load(g_ld, weight[:], a["ctx_tokens"].rearrange("(t p) k -> p t k", p=P))
            dve.after(g_ld.total())
            for e in range(EX):
                step = dve.did(nc.vector.scalar_tensor_tensor(out=picked[:], in0=chosen[:], scalar=float(e), in1=weight[:],
                                                              op0=ALU.is_equal, op1=ALU.mult))
                dve.after(step)
                step = dve.did(nc.vector.tensor_reduce(gate[:, :, e:e + 1], picked[:], AX.X, ALU.add))
                dve.after(step)

            def keep_transposed(t, s):
                yield from normalise(t, s)
                transpose_h(s, HT[:, t, :])

            plan.run(T // PAIR, lambda i: side_by_side(*[keep_transposed(i * PAIR + s, s) for s in range(PAIR)]))
            all_wait()
            pe.after(ens_ld.total())

            nc.scalar.preload_act_table(ACT.Relu)
            plan.run(T // G, lambda g: experts(g, EX, FX // P, wpi, wpo, hid, gate, None))
            all_wait()
            w5.close()

        if stages >= 6:
            w6 = ExitStack()
            t_ld = loads("router1_loaded")
            rows_sem = [Lane(plan, nc.gpsimd, sem(f"rows_moved{s}"), 16) for s in range(PAIR)]
            zero = sb("zero", [P, D], at=w6)
            wr, br = sb("wr", [P, E1], at=w6), sb("br", [P, E1], at=w6)
            load(t_ld, wr[:], a["L1_ffn_Wr"])
            load(t_ld, br[:], row(a["L1_ffn_br"]))
            pool.after(fill(zero[:], 0.0))
            rows_p = a["routed_rows"].rearrange("(j p) d -> p j d", p=P)
            for s in range(PAIR):
                half = slice(s * SLOTS // PAIR, (s + 1) * SLOTS // PAIR)
                rows_sem[s].did(nc.gpsimd.dma_start(rows_p[:, half, :], zero[:].unsqueeze(1).to_broadcast([P, SLOTS // PAIR, D])))
            lg, eqs = sb("lg", [P, T, E1], at=w6), sb("eqs", [P, T, E1], at=w6)
            first, second = sb("first", [P, T, E1], at=w6), sb("second", [P, T, E1], at=w6)
            m1, m2, rk = sb("m1", [P, T], at=w6), sb("m2", [P, T], at=w6), sb("rk", [P, T], at=w6)
            rid = sb("rid", [P, E1], at=w6)
            Hn = HT
            pe.after(t_ld.total())

            def score(t, s):
                yield from normalise(t, s)
                pool.after(dve.total())
                pool.did(nc.gpsimd.tensor_copy(Hn[:, t, :], h[s][:]))
                ready = transpose_h(s)
                yield
                pe.after(ready)
                made = pe.did(nc.tensor.matmul(bank[s][1][:, 0:E1], hT[s][:], wr[:], start=True, stop=True))
                act.after(made)
                act.did(nc.scalar.activation(lg[:, t, :], bank[s][1][:, 0:E1], ACT.Copy))

            plan.run(T // PAIR, lambda i: side_by_side(*[score(i * PAIR + s, s) for s in range(PAIR)]))
            all_wait()
            dve.after(t_ld.total())

            def chain(*instructions):
                for make in instructions:
                    last = dve.did(make())
                    dve.after(last)
                return last

            v = nc.vector
            over_t = lambda m: m[:].unsqueeze(2).to_broadcast([P, T, E1])
            over_e = lambda m: m[:].unsqueeze(1).to_broadcast([P, T, E1])
            step = chain(
                lambda: v.tensor_scalar(rid[:], ids, -1.0, float(E1), ALU.mult, ALU.add),
                lambda: v.tensor_tensor(lg[:], lg[:], over_e(br), ALU.add),
                lambda: v.tensor_reduce(m1[:], lg[:], AX.X, ALU.max),
                lambda: v.tensor_tensor(lg[:], lg[:], over_t(m1), ALU.subtract))
            act.after(step)
            dve.after(act.did(nc.scalar.activation(lg[:], lg[:], ACT.Exp)))
            chain(
                lambda: v.tensor_reduce(m1[:], lg[:], AX.X, ALU.add),
                lambda: v.reciprocal(m1[:], m1[:]),
                lambda: v.tensor_tensor(lg[:], lg[:], over_t(m1), ALU.mult))
            for most, hot in ((m1, first), (m2, second)):
                chain(
                    lambda: v.tensor_reduce(most[:], lg[:], AX.X, ALU.max),
                    lambda: v.tensor_tensor(eqs[:], lg[:], over_t(most), ALU.is_equal),
                    lambda: v.tensor_tensor(eqs[:], eqs[:], over_e(rid), ALU.mult),
                    lambda: v.tensor_reduce(rk[:], eqs[:], AX.X, ALU.max),
                    lambda: v.tensor_tensor(hot[:], over_e(rid), over_t(rk), ALU.is_equal),
                    lambda: v.scalar_tensor_tensor(out=lg[:], in0=hot[:], scalar=-2.0, in1=lg[:], op0=ALU.mult, op1=ALU.add))
            ones = sb("ones", [P, P], at=w6)
            both = eqs
            step = chain(
                lambda: v.tensor_tensor(rk[:], m1[:], m2[:], ALU.add),
                lambda: v.reciprocal(rk[:], rk[:]),
                lambda: v.tensor_tensor(m1[:], m1[:], rk[:], ALU.mult),
                lambda: v.tensor_tensor(m2[:], m2[:], rk[:], ALU.mult),
                lambda: v.memset(ones[:], 1.0),
                lambda: v.tensor_tensor(both[:], first[:], second[:], ALU.add))
            flat = both[:].rearrange("p t e -> p (t e)")
            pe.after(step)
            nc.tensor.matmul(bank[0][0][:, 0:T * E1], before, flat, start=True, stop=True)
            counted = pe.did(nc.tensor.matmul(bank[0][1][:, 0:T * E1], ones[:], flat, start=True, stop=True))
            dve.after(counted)
            sums = [sb(f"sums{k}", [P, T, E1], at=w6) for k in range(2)]
            place = sb("place", [P, T, E1], at=w6)
            size, end, begin = sb("size", [P, E1], at=w6), sb("end", [P, E1], at=w6), sb("begin", [P, E1], at=w6)
            size_i = sb("size_i", [P, E1], I32, at=w6)
            totals = bank[0][1][:, 0:T * E1].rearrange("p (t e) -> p t e", t=T)
            chain(lambda: v.tensor_copy(sums[0][:], totals))
            k, reach = 0, 1
            while reach < T:
                chain(lambda: v.tensor_copy(sums[1 - k][:, 0:reach, :], sums[k][:, 0:reach, :]),
                      lambda: v.tensor_tensor(sums[1 - k][:, reach:, :], sums[k][:, reach:, :], sums[k][:, 0:T - reach, :], ALU.add))
                k, reach = 1 - k, reach * 2
            run_sum = sums[k]
            where = sb("where", [P, T, K1], U32, at=w6)
            shift = P.bit_length() - 1
            chain(
                lambda: v.tensor_scalar(size[:], run_sum[:, T - 1, :], float(P - 1), None, ALU.add),
                lambda: v.tensor_copy(size_i[:], size[:]),
                lambda: v.tensor_scalar(size_i[:], size_i[:], shift, shift, ALU.logical_shift_right, ALU.logical_shift_left),
                lambda: v.tensor_copy(size[:], size_i[:]),
                lambda: v.tensor_tensor_scan(end[:], ones[:, 0:E1], size[:], 0.0, ALU.mult, ALU.add),
                lambda: v.tensor_tensor(begin[:], end[:], size[:], ALU.subtract),
                lambda: v.tensor_tensor(place[:], run_sum[:], totals, ALU.subtract),
                lambda: v.tensor_tensor(place[:], place[:], bank[0][0][:, 0:T * E1].rearrange("p (t e) -> p t e", t=T), ALU.add),
                lambda: v.tensor_tensor(place[:], place[:], over_e(begin), ALU.add))
            for k, hot in enumerate((first, second)):
                chain(
                    lambda: v.tensor_tensor(hot[:], hot[:], place[:], ALU.mult),
                    lambda: v.tensor_reduce(rk[:], hot[:], AX.X, ALU.add),
                    lambda: v.tensor_copy(where[:, :, k], rk[:]))
            past = sb("past", [1, SLOTS, E1], at=w6)
            slot_ef = sb("slot_ef", [1, SLOTS], at=w6)
            slot_e = sb("slot_e", [1, SLOTS], U32, at=w6)
            chain(
                lambda: v.tensor_tensor(past[:], end[0:1, :].unsqueeze(1).to_broadcast([1, SLOTS, E1]),
                                        slot_start[0:1, :].unsqueeze(2).to_broadcast([1, SLOTS, E1]), ALU.is_le),
                lambda: v.tensor_reduce(slot_ef[:], past[:], AX.X, ALU.add),
                lambda: v.tensor_scalar(slot_e[:], slot_ef[:], float(E1 - 1), None, ALU.min))
            all_wait()

            row_at = [sb(f"row_at{s}", [P, K1], U32, at=w6) for s in range(PAIR)]
            sent_row = [sb(f"sent_row{s}", [P, D], at=w6) for s in range(PAIR)]
            got = [[sb(f"got{s}{k}", [P, D], at=w6) for k in range(K1)] for s in range(PAIR)]
            pool.after(*[x.total() for x in rows_sem])

            def dispatch(t, s):
                for lane in (dve, act):
                    lane.after(plan.prev(f"sent{s}"))
                at_ready = dve.did(v.tensor_copy(row_at[s][:], where[:, t, :]))
                row_ready = act.did(nc.scalar.activation(sent_row[s][:], Hn[:, t, :], ACT.Copy))
                pool.apart(at_ready, row_ready)
                for k in range(K1):
                    rows_sem[s].did(nc.gpsimd.indirect_dma_start(
                        a["routed_rows"], bass.IndirectOffsetOnAxis(ap=row_at[s][:, k:k + 1], axis=0), sent_row[s][:], None),
                        f"sent{s}")
                yield

            plan.run(T // PAIR, lambda i: side_by_side(*[dispatch(i * PAIR + s, s) for s in range(PAIR)]))
            for lane in (sp, pool):
                lane.after(*[x.total() for x in rows_sem])
            all_wait()

            xg = [sb(f"xg{s}", [P, D], at=w6) for s in range(PAIR)]
            gb = [sb(f"gb{s}", [P, 2 * D], at=w6) for s in range(PAIR)]
            silu = [sb(f"silu{s}", [P, F1], at=w6) for s in range(PAIR)]
            prodT = [sb(f"prodT{s}", [P, F1 // P, P], at=w6) for s in range(PAIR)]
            yn = [sb(f"yn{s}", [P, D], at=w6) for s in range(PAIR)]
            xg_sem = [loads(f"slot_rows{s}") for s in range(PAIR)]
            gb_sem = [loads(f"slot_affine{s}") for s in range(PAIR)]
            yn_sem = [loads(f"slot_stored{s}") for s in range(PAIR)]
            pe.after(experts_ld.total(), narrow_ld.total())

            def slot(j, s):
                sp.after(plan.prev(f"xg_read{s}"))
                rows = load(xg_sem[s], xg[s][:], a["routed_rows"][bass.ds(j * P, P), :])
                e_sp = nc.sync.value_load(slot_e[0:1, bass.ds(j, 1)], min_val=0, max_val=E1 - 1)
                sp.after(plan.prev(f"gb_read{s}"))
                affine = load(gb_sem[s], gb[s][:], a["gamma_beta"][bass.ds(e_sp, 1), :].to_broadcast([P, 2 * D]))
                e_pe = nc.tensor.value_load(slot_e[0:1, bass.ds(j, 1)], min_val=0, max_val=E1 - 1)
                pe.after(rows)
                turned = pe.did(nc.tensor.transpose(bank[s][0][:, 0:P], xg[s][:], ident), f"xg_read{s}")
                act.after(turned)
                hT_ready = act.did(nc.scalar.activation(hT[s][:], bank[s][0][:, 0:P], ACT.Copy))
                yield
                pe.after(hT_ready)
                up1 = pe.did(nc.tensor.matmul(bank[s][1][:], hT[s][:], w13[:, e_pe, 0:F1], start=True, stop=True))
                up3 = pe.did(nc.tensor.matmul(bank[s][2][:], hT[s][:], w13[:, e_pe, F1:2 * F1], start=True, stop=True))
                act.after(up1)
                gated = act.did(nc.scalar.activation(silu[s][:], bank[s][1][:], ACT.Silu))
                dve.after(gated, up3)
                product = dve.did(v.tensor_tensor(silu[s][:], silu[s][:], bank[s][2][:], ALU.mult))
                yield
                pe.after(product)
                for c in range(F1 // P):
                    m = nc.tensor.transpose(bank[s][3][:, c * P:(c + 1) * P], silu[s][:, c * P:(c + 1) * P], ident)
                turned = pe.did(m)
                act.after(turned)
                moved = act.did(nc.scalar.activation(prodT[s][:], bank[s][3][:].rearrange("p (c n) -> p c n", c=F1 // P), ACT.Copy))
                yield
                pe.after(moved)
                for c in range(F1 // P):
                    m = nc.tensor.matmul(bank[s][0][:, 0:D], prodT[s][:, c, :], w2e[:, e_pe * (F1 // P) + c, :],
                                         start=(c == 0), stop=(c == F1 // P - 1))
                narrowed = pe.did(m)
                y = bank[s][0][:, 0:D]
                dve.after(narrowed)
                dve.apart(dve.did(v.bn_stats(stat[s][:], y)))
                dve.after(dve.did(v.bn_aggr(mv[s][:], stat[s][:])))
                var_eps = dve.did(v.tensor_scalar(ve[s][:], mv[s][:, 1:2], EPS, None, ALU.add))
                pool.after(var_eps)
                inverse = pool.did(nc.gpsimd.tensor_tensor(rstd[s][:], ve[s][:], neghalf[:, 0:1], ALU.pow))
                yield
                dve.after(inverse, plan.prev(f"y_stored{s}"))
                normed = dve.did(v.tensor_scalar(yn[s][:], y, mv[s][:, 0:1], rstd[s][:, 0:1], ALU.subtract, ALU.mult))
                pool.after(normed, affine)
                scaled = pool.did(nc.gpsimd.tensor_tensor(yn[s][:], yn[s][:], gb[s][:, 0:D], ALU.mult))
                pool.after(scaled)
                shifted = pool.did(nc.gpsimd.tensor_tensor(yn[s][:], yn[s][:], gb[s][:, D:2 * D], ALU.add), f"gb_read{s}")
                sp.after(shifted)
                load_y = yn_sem[s].did(nc.sync.dma_start(a["expert_rows"][bass.ds(j * P, P), :], yn[s][:]), f"y_stored{s}")

            nc.scalar.preload_act_table(ACT.Silu)
            plan.run(SLOTS // PAIR, lambda i: side_by_side(*[slot(i * PAIR + s, s) for s in range(PAIR)]))
            for lane in (sp, pool):
                lane.after(*[x.total() for x in yn_sem])
            all_wait()

            o_view = out.rearrange("b s d -> (b s) d")

            def combine(t, s):
                dve.after(plan.prev(f"got{s}"))
                at_ready = dve.did(v.tensor_copy(row_at[s][:], where[:, t, :]))
                pool.apart(at_ready)
                for k in range(K1):
                    rows = rows_sem[s].did(nc.gpsimd.indirect_dma_start(
                        got[s][k][:], None, a["expert_rows"], bass.IndirectOffsetOnAxis(ap=row_at[s][:, k:k + 1], axis=0)),
                        f"got{s}")
                yield
                dve.after(rows)
                for k, w in enumerate((m1, m2)):
                    added = dve.did(v.scalar_tensor_tensor(out=X[:, t, :], in0=got[s][k][:], scalar=w[:, bass.ds(t, 1)],
                                                           in1=X[:, t, :], op0=ALU.mult, op1=ALU.add))
                    dve.after(added)
                sp.after(added)
                out_st.did(nc.sync.dma_start(o_view[bass.ds(t * P, P), :], X[:, t, :]))

            plan.run(T // PAIR, lambda i: side_by_side(*[combine(i * PAIR + s, s) for s in range(PAIR)]))
            w6.close()

        if stages < 6:
            sp.after(dve.total())
            o_view = out.rearrange("b s d -> (b s) d").rearrange("(t p) d -> p t d", p=P)
            for k in range(4):
                load(out_st, o_view[:, 4 * k:4 * k + 4, :], X[:, 4 * k:4 * k + 4, :])
        sp.after(out_st.total())
    return plan.seen, plan.noted


def constants():
    r, c = np.arange(P)[:, None], np.arange(P)[None, :]
    masks = [r == c, np.concatenate([r // DH0 == c // DH0, r // DH0 == c[:, :H0]], axis=1), r // D1 == c[:, :H1],
             (r // S == c // S) & (c >= r), r < c,
             c[:, :E1] + 0 * r, P * c[:, :SLOTS] + 0 * r]
    return np.concatenate([m.astype(np.float32) for m in masks], axis=1)


def lay_out(inputs):
    a = {n: np.ascontiguousarray(v) for n, v in inputs.items()}
    a["consts"] = constants()
    a["ctxT"] = np.ascontiguousarray(a["ctx_512"].transpose(0, 2, 1))
    for n in ("Wq", "Wk", "Wv"):
        a[f"L0_xattn_{n}T"] = np.ascontiguousarray(a.pop(f"L0_xattn_{n}").T)
    for n in ("Wq", "Wk", "Wv", "Wo"):
        a[f"L1_attn_{n}T"] = np.ascontiguousarray(a.pop(f"L1_attn_{n}").T)
    a["gamma_beta"] = np.concatenate([a.pop("L1_ffn_gamma"), a.pop("L1_ffn_beta")], axis=1)
    a["proj_inT"] = np.ascontiguousarray(a.pop("L1_xattn_proj_in").transpose(2, 0, 1))
    a["proj_outT"] = np.ascontiguousarray(a.pop("L1_xattn_proj_out").transpose(0, 2, 1))
    a["ctx_tokens"] = a["ctxT"].reshape(B * S, CD)
    a["itok_tokens"] = np.ascontiguousarray(a.pop("itok_BxS2xS_0_7").transpose(0, 2, 1)).reshape(B * S, S)
    return a


def kernel(**inputs):
    import concourse.bacc as bacc
    from concourse.bass_utils import run_bass_kernel_spmd

    arrays = lay_out(inputs)

    def program(known):
        nc = bacc.Bacc("TRN2", target_bir_lowering=False, num_devices=1)
        args = {n: nc.dram_tensor(f"in_{n}", v.shape, mybir.dt.from_np(v.dtype), kind="ExternalInput").ap()
                for n, v in arrays.items()}
        out = nc.dram_tensor("out_x", (B, S, D), F32, kind="ExternalOutput").ap()
        return nc, build(nc, args, out, known)

    _, counted = program(None)
    nc, again = program(counted)
    assert again == counted
    r = run_bass_kernel_spmd(nc, [{f"in_{n}": v for n, v in arrays.items()}], core_ids=[0])
    return r.results[0]["out_x"]
```

```python
from contextlib import ExitStack

import numpy as np

import concourse.bass as bass
from concourse import mybir
from concourse.alu_op_type import AluOpType as ALU

ACT = mybir.ActivationFunctionType
AX = mybir.AxisListType
F32 = mybir.dt.float32
I32 = mybir.dt.int32
U32 = mybir.dt.uint32

B, S, D = 32, 64, 128
P = 128
T = B * S // P
EPS = 1e-5
H0, DH0 = 16, 8
HX, DX = 16, 64
CD = 64
JX = HX * CD // P
E0, F0, K0, R0 = 8, 512, 3, 32
H1, D1 = 8, 16
EX, FX = 8, 256
E1, F1, K1 = 16, 512, 2
SLOTS = (K1 * B * S + E1 * (P - 1)) // P + 1
CONST_WIDTHS = [P, P + H0, H1, P, P, E1, SLOTS]
G = 4


class Signal:

    def __init__(self, sem, base, per=1, unit=1, credit=0):
        self.sem, self.base, self.per, self.unit, self.credit = sem, base, per, unit, credit
        self.item, self.k = None, 0

    def did(self, instruction, n):
        self.item, self.k = n, self.k + 1 if n == self.item else 1
        assert self.k <= self.per
        instruction.then_inc(self.sem, self.unit)
        return self.at(n, self.k)

    def at(self, n, k=None):
        if n < -self.credit:
            return None
        return self, n, (self.per if k is None else k)


class Line(Signal):

    def __init__(self, sem, unit=1):
        super().__init__(sem, 0, 1, unit)
        self.count = 0

    def did(self, instruction):
        self.count += 1
        return super().did(instruction, Item(self.count - 1))

    def all(self):
        return self.at(Item(self.count - 1))


class Alternating:

    def __init__(self, even, odd):
        self.pair = even, odd

    def did(self, instruction, n):
        return self.pair[n.c % 2].did(instruction, n.half())

    def at(self, n):
        return self.pair[n.c % 2].at(n.half())


class Signals:

    def __init__(self, nc, ctx):
        self.nc, self.ctx, self.made, self.used = nc, ctx, {}, {}

    def new(self, count, per=1, unit=1, credit=0, queue="own"):
        kept = self.made.setdefault((unit, queue), [])
        k = self.used.setdefault((unit, queue), 0)
        if k == len(kept):
            kept.append([self.ctx.enter_context(self.nc.semaphore(f"{queue}_{unit}_{k}")), 0])
        self.used[(unit, queue)] = k + 1
        if credit:
            self.nc.vector.sem_inc(kept[k][0], credit * per * unit)
        base = kept[k][1] + credit * per * unit
        kept[k][1] = base + count * per * unit
        return Signal(kept[k][0], base, per, unit, credit)

    def alternating(self, count, per=1, queue="own"):
        return Alternating(self.new(-(-count // 2), per, 16, queue=queue), self.new(count // 2, per, 16, queue=queue))

    def recycle(self):
        self.used = {}


class Item:

    def __init__(self, c, i=None, scale=0):
        self.c, self.i, self.scale = c, i, scale

    def __sub__(self, d):
        return Item(self.c - d, self.i, self.scale)

    def __add__(self, d):
        return self - -d

    def upto(self, last):
        return self if self.i is not None else Item(min(self.c, last))

    def half(self):
        return Item(self.c // 2, self.i, self.scale // 2)

    def __lt__(self, other):
        return self.c < other

    def __eq__(self, other):
        return other is not None and self.c == other.c and self.i is other.i

    def times(self, a, b=0):
        return self.c * a + b if self.i is None else self.i * (self.scale * a) + (self.c * a + b)


def after(engine, *marks):
    latest = {}
    for signal, n, k in filter(None, marks):
        reached = n.c * signal.per + k
        if signal not in latest or reached > latest[signal][0]:
            latest[signal] = reached, n
    for signal, (reached, n) in latest.items():
        u = signal.unit
        engine.wait_ge(signal.sem, n.times(signal.per * u, (reached - n.c * signal.per) * u + signal.base))


def pipeline(nc, count, steps, lead=0):
    depth = max(lag for lag, _ in steps)

    def at(m, parity, low=0, high=None):
        for lag, step in steps:
            if high is None or low <= m.c - lag < high:
                step(m - lag, (parity - lag) % 2)

    start = depth + 2
    passes = max(0, count - start) // 2
    for m in range(start):
        at(Item(m), m % 2, 0, count)
    if passes:
        with nc.Fori(0, passes) as i:
            for u in range(2):
                at(Item(start + u, i, 2), (start + u) % 2)
    for m in range(start + 2 * passes, count + depth):
        at(Item(m), m % 2, 0, count)



def build(nc, a, out, stages=6):
    a = dict(a)
    a["routes_w"] = nc.dram_tensor("routes_w", (B, E0), F32, kind="Internal").ap()
    for n in ("routed_rows", "expert_rows"):
        a[n] = nc.dram_tensor(n, (SLOTS * P, D), F32, kind="Internal").ap()
    ctx = ExitStack()
    with ctx:
        def sem(name):
            return ctx.enter_context(nc.semaphore(name))

        def sb(name, shape, dt=F32, at=None):
            return (at or ctx).enter_context(nc.sbuf_tensor(name, shape, dt))

        def twice(name, shape, dt=F32, at=None):
            return [sb(f"{name}{u}", shape, dt, at) for u in range(2)]

        PE, DVE, ACTE, POOL, SP = nc.tensor, nc.vector, nc.scalar, nc.gpsimd, nc.sync
        v = nc.vector
        signals = Signals(nc, ctx)
        new = signals.new
        bank = [ctx.enter_context(nc.psum_tensor(f"bank{k}", [P, 512], F32)) for k in range(8)]
        pe_line, dve_line, act_line, pool_line, sp_line = (Line(sem(f"{n}_line")) for n in ("pe", "dve", "act", "pool", "sp"))
        spare = sem("spare")

        def apart(engine, *marks):
            after(engine, *marks)
            engine.sem_inc(spare)

        def stage_end(keep=False):
            ends = [line.did(engine.drain()) for engine, line in
                    ((PE, pe_line), (DVE, dve_line), (ACTE, act_line), (POOL, pool_line))]
            for engine in (PE, DVE, ACTE, POOL, SP):
                after(engine, *ends)
            if not keep:
                signals.recycle()

        def chain(*instructions):
            for make in instructions:
                done = dve_line.did(make())
                after(DVE, done)
            return done

        def fill(dst, value):
            after(POOL, pool_line.all() if pool_line.count else None)
            return pool_line.did(nc.gpsimd.memset(dst, value))

        def loads(name):
            return Line(sem(name), 16)

        def load(line, dst, src, queue=SP):
            return line.did(queue.dma_start(dst, src))

        def row(src, parts=P):
            return src.rearrange("(o n) -> o n", o=1).to_broadcast([parts, src.shape[0]])

        X = sb("X", [P, T, D])
        HT = sb("HT", [P, T, P])
        consts = sb("consts", [P, a["consts"].shape[1]])
        at = iter(np.cumsum([0] + CONST_WIDTHS).tolist())
        ident, same_head0, head_of1, causal, before, ids, slot_start = (
            consts[:, c:c + w] for c, w in zip(at, CONST_WIDTHS))
        neghalf = sb("neghalf", [P, H1])
        hT = twice("hT", [P, P])
        o_tok, oT = twice("o_tok", [P, D]), twice("oT", [P, P])
        norm_sets = [tuple(twice(f"{name}_{k}_", [P, w]) for name, w in (("h", D), ("stat", 6), ("mv", 2), ("ve", 1), ("rstd", 1)))
                     for k in range(2)]
        pooled = sb("pooled", [P, B])
        lg = sb("lg", [P, T, E1])
        narrow_mem = sb("narrow_mem", [P, 2 * E0 * F0])
        wza = narrow_mem[:, 0:E0 * F0].rearrange("p (e f) -> p e f", e=E0)
        wzb = narrow_mem[:, E0 * F0:].rearrange("p (e c d) -> p e c d", e=E0, d=D)
        assert 2 * E0 * F0 == E1 * F1
        w2e = narrow_mem[:].rearrange("p (e d) -> p e d", d=D)
        w13 = sb("w13", [P, E1, 2 * F1])
        wpi, wpo = sb("wpi", [P, EX, FX]), sb("wpo", [P, EX, FX // P, D])
        rw1, rw2, rb1, rb2 = sb("rw1", [P, R0]), sb("rw2", [R0, E0]), sb("rb1", [R0, 1]), sb("rb2", [B, E0])
        wqk1, wv1, wo1, nw1 = sb("wqk1", [P, 2, D]), sb("wv1", [P, D]), sb("wo1", [P, D]), sb("nw1", [P, 1])
        wr, br = sb("wr", [P, E1]), sb("br", [P, E1])
        r_ld, a_ld, t_ld = loads("router_loaded"), loads("causal_weights_loaded"), loads("router1_loaded")
        first_ld, zones_ld, ens_ld = loads("first_loaded"), loads("zone_weights_loaded"), loads("ensemble_weights_loaded")
        experts_ld, narrow_ld = loads("expert_weights_loaded"), loads("expert_second_weights_loaded")
        out_st = loads("stored")
        x_view = a["x"].rearrange("b s d -> (b s) d").rearrange("(t p) d -> p t d", p=P)
        load(first_ld, X[:], x_view)
        load(first_ld, consts[:], a["consts"])
        neghalf_set = fill(neghalf[:], -0.5)

        class Norm:

            def __init__(self, turn_bank, keep=None, pool_step=None, count=T, buffers=0, sharing=None, credit=0):
                self.turn, self.keep, self.pool_step, self.sharing = turn_bank, keep, pool_step, sharing or (lambda n: None)
                self.h, self.stat, self.mv, self.ve, self.rstd = norm_sets[buffers]
                self.stats, self.root, self.normed = new(count, 3, credit=credit), new(count, credit=credit), new(count, credit=credit)
                self.turned, self.moved = new(count, credit=credit), new(count, credit=credit)
                self.added = new(count, credit=credit) if pool_step else None

            def moments(self, n, u, *ready):
                apart(DVE, *ready, self.normed.at(n - 2), self.stats.at(n - 2))
                self.stats.did(v.bn_stats(self.stat[u][:], X[:, n.times(1), :]), n)

            def gather(self, n, u):
                apart(DVE, self.stats.at(n, 1), self.normed.at(n - 2))
                self.stats.did(v.bn_aggr(self.mv[u][:], self.stat[u][:]), n)

            def invert(self, n, u):
                after(DVE, self.stats.at(n, 2), self.root.at(n - 2))
                done = self.stats.did(v.tensor_scalar(self.ve[u][:], self.mv[u][:, 1:2], EPS, None, ALU.add), n)
                after(POOL, done, self.normed.at(n - 2))
                self.root.did(nc.gpsimd.tensor_tensor(self.rstd[u][:], self.ve[u][:], neghalf[:, 0:1], ALU.pow), n)

            def begin(self, n, u, *ready):
                self.moments(n, u, *ready)
                self.gather(n, u)
                self.invert(n, u)

            def finish(self, n, u, *read):
                after(DVE, self.root.at(n), self.stats.at(n), self.turned.at(n - 2), self.added.at(n - 2) if self.added else None)
                x, h = X[:, n.times(1), :], self.h[u]
                normed = self.normed.did(v.tensor_scalar(h[:], x, self.mv[u][:, 0:1], self.rstd[u][:, 0:1],
                                                         ALU.subtract, ALU.mult), n)
                if self.added:
                    after(POOL, normed)
                    self.added.did(self.pool_step(n, u, x, h[:]), n)
                after(PE, normed, self.moved.at(n - 1), self.sharing(n))
                turned = self.turned.did(nc.tensor.transpose(self.turn, h[:], ident), n)
                after(ACTE, turned, *read)
                dst = hT[u][:] if self.keep is None else self.keep[:, n.times(1), :]
                self.moved.did(nc.scalar.activation(dst, self.turn, ACT.Copy), n)

        w1 = ExitStack()
        wq0, wkv0, wo0 = sb("wq0", [P, D], at=w1), sb("wkv0", [P, 2 * D], at=w1), sb("wo0", [P, D], at=w1)
        bq0, bkv0, bo0 = sb("bq0", [P, 1], at=w1), sb("bkv0", [P, 2 * D], at=w1), sb("bo0", [P, D], at=w1)
        load(first_ld, wq0[:], a["L0_attn_wq"])
        load(first_ld, wkv0[:, 0:D], a["L0_attn_wk"])
        load(first_ld, wkv0[:, D:2 * D], a["L0_attn_wv"])
        load(first_ld, wo0[:], a["L0_attn_wo"], ACTE)
        load(first_ld, bq0[:], a["L0_attn_bq"].rearrange("(n o) -> n o", o=1), ACTE)
        load(first_ld, bkv0[:, 0:D], row(a["L0_attn_bk"]), ACTE)
        load(first_ld, bkv0[:, D:2 * D], row(a["L0_attn_bv"]), ACTE)
        load(first_ld, bo0[:], row(a["L0_attn_bo"]), ACTE)
        wqk = sb("wqk", [P, JX, P], at=w1)
        wvo = sb("wvo", [P, JX, D], at=w1)
        box = sb("box", [P, D], at=w1)
        q_exps, q_pos, qf, k_exps, k_pos, kf = (twice(n, [P, P], at=w1) for n in ("q_exps", "q_pos", "qf", "k_exps", "k_pos", "kf"))
        kvb = twice("kvb", [P, 2 * D + H0], at=w1)
        kvsum = twice("kvsum", [P, 2, D + H0], at=w1)
        den = twice("den", [P, H0], at=w1)

        w1a = ExitStack()
        wqT = sb("wqT", [P, JX, P], at=w1a)
        wkT = sb("wkT", [P, JX, P], at=w1a)
        wvT = sb("wvT", [P, JX, P], at=w1a)
        wox = sb("wox", [P, JX, D], at=w1a)
        cx_ld = loads("cross_weights_loaded")
        fill(wkT[:], 0.0)
        zeroed = fill(wvT[:], 0.0)
        load(cx_ld, wqT[:], a["L0_xattn_WqT"].rearrange("(j p) n -> p j n", p=P))
        load(cx_ld, wox[:], a["L0_xattn_Wo"].rearrange("(j p) n -> p j n", p=P))
        load(cx_ld, box[:], row(a["L0_xattn_bo"]))
        after(SP, zeroed)
        for w, name in ((wkT, "L0_xattn_WkT"), (wvT, "L0_xattn_WvT")):
            src = a[name].rearrange("(j g p) n -> g p j n", g=2, p=DX)
            for g in range(2):
                load(cx_ld, w[g * DX:(g + 1) * DX, :, g * CD:(g + 1) * CD], src[g])
        load(r_ld, rw1[:], a["L0_ffn_W1"])
        load(r_ld, rw2[:], a["L0_ffn_W2"])
        load(r_ld, rb1[:], a["L0_ffn_b1"].rearrange("(n o) -> n o", o=1))
        load(r_ld, rb2[:], row(a["L0_ffn_b2"], B))
        load(a_ld, wqk1[:, 0, :], a["L1_attn_WqT"])
        load(a_ld, wqk1[:, 1, :], a["L1_attn_WkT"])
        load(a_ld, wv1[:], a["L1_attn_WvT"])
        load(a_ld, wo1[:], a["L1_attn_WoT"])
        for k in range(H1):
            load(a_ld, nw1[k * D1:(k + 1) * D1, :], a["L1_attn_norm_w"].rearrange("(n o) -> n o", o=1))
        load(t_ld, wr[:], a["L1_ffn_Wr"])
        load(t_ld, br[:], row(a["L1_ffn_br"]))
        load(zones_ld, wza, a["L0_ffn_Wa"].rearrange("e d f -> d e f"))
        load(zones_ld, wzb.rearrange("p e c d -> p (e c) d"), a["L0_ffn_Wb"].rearrange("e (c p) d -> p (e c) d", p=P))
        load(ens_ld, wpi[:], a["proj_inT"])
        load(ens_ld, wpo[:].rearrange("p e c i -> p (e c) i"), a["proj_outT"].rearrange("e (c p) i -> p (e c) i", p=P))
        load(experts_ld, w13[:, :, 0:F1], a["L1_ffn_W1"].rearrange("e d f -> d e f"))
        load(experts_ld, w13[:, :, F1:], a["L1_ffn_W3"].rearrange("e d f -> d e f"))

        for u in range(2):
            fill(kvb[u][:, 2 * D:], 1.0)
        for engine in (PE, DVE, ACTE, POOL):
            after(engine, pool_line.all(), first_ld.all())

        norm = Norm(bank[0][:, 0:P], pool_step=lambda n, u, x, h: nc.gpsimd.tensor_tensor(x, x, bo0[:], ALU.add))
        made, q_read, biased, k_read, q_mapped, k_mapped = new(T, 2), new(T, 2), new(T), new(T, 2), new(T), new(T)
        sums_made, sums_masked, applied, divided = new(T, 2), new(T, 2), new(T), new(T, 3)
        o_turned, o_moved, projected, streamed = new(T), new(T), new(T), new(T)
        sum_banks = bank[3], bank[7]

        def attn_project(n, u):
            after(PE, norm.moved.at(n), q_read.at(n - 1), biased.at(n - 1))
            made.did(nc.tensor.matmul(bank[1][:, 0:P], wq0[:], hT[u][:], start=True, stop=True), n)
            made.did(nc.tensor.matmul(bank[2][:, 0:2 * D], hT[u][:], wkv0[:], start=True, stop=True), n)

        def attn_exps(n, u):
            after(ACTE, made.at(n, 1), q_mapped.at(n - 2))
            q_read.did(nc.scalar.activation(q_exps[u][:], bank[1][:, 0:P], ACT.Exp, bias=bq0[:, 0:1]), n)
            q_read.did(nc.scalar.activation(q_pos[u][:], bank[1][:, 0:P], ACT.Relu, bias=bq0[:, 0:1]), n)
            after(DVE, made.at(n), k_read.at(n - 2), sums_made.at(n - 2))
            m = biased.did(v.tensor_tensor(kvb[u][:, 0:2 * D], bank[2][:, 0:2 * D], bkv0[:], ALU.add), n)
            after(ACTE, m, k_mapped.at(n - 2))
            k_read.did(nc.scalar.activation(k_exps[u][:], kvb[u][:, 0:D], ACT.Exp), n)
            k_read.did(nc.scalar.activation(k_pos[u][:], kvb[u][:, 0:D], ACT.Relu), n)

        def attn_map(n, u):
            for mapped, read, exps, pos, dst, before_ in ((q_mapped, q_read.at(n), q_exps, q_pos, qf, applied.at(n - 2)),
                                                          (k_mapped, k_read.at(n), k_exps, k_pos, kf, sums_made.at(n - 2))):
                after(DVE, read, before_)
                mapped.did(v.scalar_tensor_tensor(out=dst[u][:], in0=exps[u][:], scalar=1.0, in1=pos[u][:],
                                                  op0=ALU.min, op1=ALU.add), n)

        def attn_sums(n, u):
            after(PE, k_mapped.at(n), biased.at(n), sums_masked.at(n - 1))
            for b in range(2):
                rows = slice(b * S, b * S + S)
                sums_made.did(nc.tensor.matmul(sum_banks[b][:, 0:D + H0], kf[u][rows, :], kvb[u][rows, D:], start=True, stop=True), n)

        def attn_mask(n, u):
            after(DVE, sums_made.at(n), applied.at(n - 2))
            for b in range(2):
                sums_masked.did(v.tensor_tensor(kvsum[u][:, b, :], sum_banks[b][:, 0:D + H0], same_head0, ALU.mult), n)

        def attn_apply(n, u):
            after(PE, sums_masked.at(n), q_mapped.at(n), divided.at(n - 1))
            for b in range(2):
                m = nc.tensor.matmul(bank[4][b * S:b * S + S, 0:D + H0], qf[u][:, b * S:b * S + S], kvsum[u][:, b, :],
                                     start=True, stop=True)
            applied.did(m, n)

        def attn_guard(n, u):
            after(DVE, applied.at(n), divided.at(n - 2), o_turned.at(n - 2))
            divided.did(v.tensor_scalar(den[u][:], bank[4][:, D:D + H0], 1e-6, None, ALU.add), n)

        def attn_invert(n, u):
            after(DVE, divided.at(n, 1))
            divided.did(v.reciprocal(den[u][:], den[u][:]), n)

        def attn_divide(n, u):
            after(DVE, divided.at(n, 2))
            divided.did(v.tensor_tensor(
                o_tok[u][:].rearrange("p (h e) -> p h e", h=H0), bank[4][:, 0:D].rearrange("p (h e) -> p h e", h=H0),
                den[u][:].unsqueeze(2).to_broadcast([P, H0, DH0]), ALU.mult), n)

        def attn_turn(n, u):
            after(PE, divided.at(n), o_moved.at(n - 1))
            m = o_turned.did(nc.tensor.transpose(bank[5][:, 0:P], o_tok[u][:], ident), n)
            after(ACTE, m, projected.at(n - 2))
            o_moved.did(nc.scalar.activation(oT[u][:], bank[5][:, 0:P], ACT.Copy), n)

        def attn_out(n, u):
            after(PE, o_moved.at(n), streamed.at(n - 1))
            projected.did(nc.tensor.matmul(bank[6][:, 0:P], oT[u][:], wo0[:], start=True, stop=True), n)

        def attn_stream(n, u):
            after(DVE, projected.at(n), norm.added.at(n))
            x = X[:, n.times(1), :]
            streamed.did(v.tensor_tensor(x, x, bank[6][:, 0:P], ALU.add), n)

        nc.scalar.preload_act_table(ACT.Exp)
        pipeline(nc, T, [(4, attn_sums), (5, attn_apply), (1, lambda n, u: norm.finish(n, u, made.at(n - 2))), (2, attn_project), (7, attn_out), (6, attn_turn), (0, norm.moments), (4, attn_mask), (0, norm.gather),(5, attn_guard),  (0, norm.invert),(5, attn_invert),  (3, attn_map), (5, attn_divide),  (2, attn_exps), (7, attn_stream)])
        stage_end()

        after(PE, cx_ld.all())
        for j in range(JX):
            quarter = slice((j % 4) * P, (j % 4 + 1) * P)
            nc.tensor.matmul(bank[j // 4][:, quarter], wqT[:, j, :], wkT[:, j, :], start=True, stop=True)
            m = nc.tensor.matmul(bank[2 + j // 4][:, quarter], wvT[:, j, :], wox[:, j, :], start=True, stop=True)
        m = pe_line.did(m)
        after(DVE, m)
        after(ACTE, m)
        for k in range(2):
            fours = slice(4 * k, 4 * k + 4)
            dve_line.did(v.tensor_copy(wqk[:, fours, :], bank[k][:].rearrange("p (j n) -> p j n", j=4)))
            act_line.did(nc.scalar.activation(wvo[:, fours, :], bank[2 + k][:].rearrange("p (j n) -> p j n", j=4), ACT.Copy))
        stage_end()
        w1a.close()

        if stages >= 2:
            w2 = ExitStack()
            qx = twice("qx", [P, JX, P], at=w2)
            pr = twice("pr", [P, HX, S], at=w2)
            prT = twice("prT", [P, JX, P], at=w2)
            ov = twice("ov", [P, JX, P], at=w2)
            ctxT = twice("ctxT", [P, 2, P], at=w2)
            ctxd = twice("ctxd", [P, 2, P], at=w2)
            top, tot = twice("top", [P, HX], at=w2), twice("tot", [P, HX], at=w2)
            for u in range(2):
                fill(ctxT[u][:], 0.0)
                fill(ctxd[u][:], 0.0)
            after(SP, pool_line.all())
            keys_in, vals_in = signals.alternating(T, 2, "keys"), signals.alternating(T, 2, "keys")
            norm = Norm(bank[6][:, 0:P], pool_step=lambda n, u, x, h: nc.gpsimd.tensor_tensor(x, x, box[:], ALU.add),
                        sharing=lambda n: zone_norm.moved.at(n - ZONE_LAG))
            zone_norm = Norm(bank[6][:, P:2 * P], keep=HT, buffers=1, sharing=lambda n: norm.moved.at((n + (ZONE_LAG - 1)).upto(T - 1)),
                             pool_step=lambda n, u, x, h: nc.gpsimd.tensor_tensor(x, x, h, ALU.add))
            ZONE_LAG = 5
            summed_tokens = new(T)
            queried, q_moved = new(T, 2), new(T, 2)
            scored, shifted, raised = new(T, 2), new(T, 4), new(T, 2)
            summed, shared = new(T, 4), new(T, 2)
            p_turned, p_moved, mixed, mix_moved = new(T, 2), new(T, 2), new(T, 2), new(T, 2)
            projected, streamed = new(T), new(T)

            def keys_load(n, u):
                after(SP, scored.at(n - 2))
                for g in range(2):
                    d = slice(g * S, (g + 1) * S)
                    keys_in.did(SP.dma_start(ctxT[u][d, :, d], a["ctxT"][bass.ds(n.times(2), 2)].rearrange("b c m -> c b m")), n)

            def values_load(n, u):
                after(SP, mixed.at(n - 2))
                for g in range(2):
                    d = slice(g * S, (g + 1) * S)
                    vals_in.did(SP.dma_start(ctxd[u][d, :, d], a["ctx_512"][bass.ds(n.times(2), 2)].rearrange("b m c -> m b c")), n)

            def cross_query(n, u):
                after(PE, norm.moved.at(n), q_moved.at(n - 1))
                for k in range(2):
                    for j in range(4):
                        m = nc.tensor.matmul(bank[k][:, j * P:(j + 1) * P], wqk[:, 4 * k + j, :], hT[u][:], start=True, stop=True)
                    m = queried.did(m, n)
                    after(ACTE, m, scored.at(n - 2))
                    q_moved.did(nc.scalar.activation(qx[u][:, 4 * k:4 * k + 4, :], bank[k][:].rearrange("p (j n) -> p j n", j=4), ACT.Copy), n)

            def cross_score(n, u):
                after(PE, q_moved.at(n), keys_in.at(n), shifted.at(n - 1))
                for k in range(2):
                    for j in range(4):
                        for b in range(2):
                            m = nc.tensor.matmul(bank[2 + k][b * S:(b + 1) * S, j * P:(j + 1) * P],
                                                 qx[u][:, 4 * k + j, b * S:(b + 1) * S], ctxT[u][:, b, :], start=True, stop=True)
                    heads = slice(8 * k, 8 * k + 8)
                    s = bank[2 + k][:].rearrange("p (h m) -> p h m", h=8)
                    after(DVE, scored.did(m, n), p_turned.at(n - 2))
                    after(DVE, shifted.did(v.tensor_reduce(top[u][:, heads], s, AX.X, ALU.max), n))
                    m = shifted.did(v.tensor_tensor(pr[u][:, heads, :], s, top[u][:, heads].unsqueeze(2).to_broadcast([P, 8, S]),
                                                    ALU.subtract), n)
                    after(ACTE, m)
                    raised.did(nc.scalar.activation(pr[u][:, heads, :], pr[u][:, heads, :], ACT.Exp, scale=DX ** -0.5), n)

            def cross_share(n, u):
                for k in range(2):
                    heads = slice(8 * k, 8 * k + 8)
                    after(DVE, raised.at(n, k + 1), shared.at(n - 2))
                    after(DVE, summed.did(v.tensor_reduce(tot[u][:, heads], pr[u][:, heads, :], AX.X, ALU.add), n))
                    m = summed.did(v.reciprocal(tot[u][:, heads], tot[u][:, heads]), n)
                    after(POOL, m)
                    shared.did(nc.gpsimd.tensor_tensor(pr[u][:, heads, :], pr[u][:, heads, :],
                                                       tot[u][:, heads].unsqueeze(2).to_broadcast([P, 8, S]), ALU.mult), n)

            def cross_turn(n, u):
                for k in range(2):
                    after(PE, shared.at(n, k + 1), mix_moved.at(n - 1))
                    for j in range(4 * k, 4 * k + 4):
                        m = nc.tensor.transpose(bank[4 + k][:, (j % 4) * P:(j % 4 + 1) * P],
                                                pr[u][:, 2 * j:2 * j + 2, :].rearrange("p h m -> p (h m)"), ident)
                    after(ACTE, p_turned.did(m, n), mixed.at(n - 2))
                    p_moved.did(nc.scalar.activation(prT[u][:, 4 * k:4 * k + 4, :],
                                                     bank[4 + k][:].rearrange("p (j n) -> p j n", j=4), ACT.Copy), n)

            def cross_mix(n, u):
                after(PE, p_moved.at(n), vals_in.at(n))
                for b in range(2):
                    m = mixed.did(nc.tensor.matmul(bank[4 + b][:], ctxd[u][:, b, :], prT[u][:, :, b * S:(b + 1) * S],
                                                   start=True, stop=True), n)
                    after(ACTE, m, projected.at(n - 2))
                    mix_moved.did(nc.scalar.activation(ov[u][:, :, b * S:(b + 1) * S],
                                                       bank[4 + b][:].rearrange("p (j n) -> p j n", j=JX), ACT.Copy), n)

            def cross_out(n, u):
                after(PE, mix_moved.at(n), streamed.at(n - 1))
                for j in range(JX):
                    m = nc.tensor.matmul(bank[7][:, 0:D], ov[u][:, j, :], wvo[:, j, :], start=(j == 0), stop=(j == JX - 1))
                after(DVE, projected.did(m, n), norm.added.at(n))
                x = X[:, n.times(1), :]
                streamed.did(v.tensor_tensor(x, x, bank[7][:, 0:D], ALU.add), n)

            def zone_sum(n, u):
                after(DVE, zone_norm.moved.at(n))
                summed_tokens.did(v.tensor_reduce(pooled[:, bass.ds(n.times(2), 2)],
                                                  HT[:, n.times(1), :].rearrange("p (b n) -> p b n", b=2), AX.X, ALU.add), n)

            pipeline(nc, T, [(0, keys_load), (2, values_load), (3, cross_turn),
                             (1, lambda n, u: norm.finish(n, u, queried.at(n - 2))), (ZONE_LAG, zone_norm.finish),
                             (0, norm.moments), (4, lambda n, u: zone_norm.moments(n, u, streamed.at(n))),
                             (0, norm.gather), (4, zone_norm.gather), (0, norm.invert), (4, zone_norm.invert),
                             (2, cross_score), (2, cross_share), (3, cross_mix), (1, cross_query), (ZONE_LAG, zone_sum),
                             (3, cross_out)])
            stage_end()
            w2.close()
        w1.close()

        def experts(count, chunks, w_up, w_down, hid, gate, gelu, beside=None):
            ups, outs = bank[0:4], bank[4:6]
            back = len(ups) // chunks
            total = T // G * count
            widened = new(total, chunks)
            by_act = new(total, chunks if gelu else chunks // 2, credit=back)
            by_dve = None if gelu else new(total, chunks // 2, credit=back)
            narrowed, streamed = new(total), new(total, G, credit=2)

            def widen(g, e, n):
                tokens = HT[:, bass.ds(g * G, G), :]
                for c in range(chunks):
                    up = ups[(e * chunks + c) % len(ups)]
                    act_reads = bool(gelu) or c % 2 == 0
                    after(PE, (by_act if act_reads else by_dve).at(n - back, c + 1 if gelu else None))
                    m = widened.did(nc.tensor.matmul(up[:], w_up[:, e, c * P:(c + 1) * P], tokens, start=True, stop=True), n)
                    dst = hid[e % 2][:, c, :]
                    if act_reads:
                        after(ACTE, m)
                        by_act.did(nc.scalar.activation(dst, up[:], gelu or ACT.Relu), n)
                    else:
                        after(DVE, m)
                        by_dve.did(v.tensor_scalar(dst, up[:], 0.0, None, ALU.max), n)

            def narrow(g, e, n):
                after(PE, by_act.at(n), None if gelu else by_dve.at(n), streamed.at(n - 2))
                o = outs[e % 2]
                for j in range(G):
                    for c in range(chunks):
                        m = nc.tensor.matmul(o[:, j * P:(j + 1) * P], hid[e % 2][:, c, j * P:(j + 1) * P], w_down[:, e, c, :],
                                             start=(c == 0), stop=(c == chunks - 1))
                after(DVE, narrowed.did(m, n), streamed.at(n - 1))
                for j in range(G):
                    x = X[:, g * G + j, :]
                    streamed.did(v.scalar_tensor_tensor(out=x, in0=o[:, j * P:(j + 1) * P], scalar=gate[:, g * G + j, e:e + 1],
                                                        in1=x, op0=ALU.mult, op1=ALU.add), n)

            with nc.Fori(0, T // G) as g:
                for e in range(count + 1):
                    if e < count:
                        widen(g, e, Item(e, g, count))
                    if e > 0:
                        narrow(g, e - 1, Item(e - 1, g, count))
                    if beside and e < count:
                        beside(g, e, Item(e, g, count))

        w5 = ExitStack()
        g_ld = loads("gates_loaded")
        chosen = sb("chosen", [P, T, S], I32, at=w5)
        weight = sb("weight", [P, T, CD], at=w5)
        picked = sb("picked", [P, G, S], at=w5)
        gate = sb("gate", [P, T, EX], at=w5)
        load(g_ld, chosen[:], a["itok_tokens"].rearrange("(t p) k -> p t k", p=P))
        load(g_ld, weight[:], a["ctx_tokens"].rearrange("(t p) k -> p t k", p=P))

        if stages >= 3:
            w3 = ExitStack()
            sent, routes_ld = loads("routes_sent"), loads("routes_loaded")
            rh, prob, one = sb("rh", [R0, B], at=w3), sb("prob", [B, E0], at=w3), sb("one", [B, 1], at=w3)
            best, best_atf = sb("best", [B, 8], at=w3), sb("best_atf", [B, 8], at=w3)
            best_at = sb("best_at", [B, 8], U32, at=w3)
            zone_b, picked0 = sb("zone_b", [B, E0], at=w3), sb("picked0", [B, E0], at=w3)
            zone_w = sb("zone_w", [P, T, E0], at=w3)
            ghid = twice("ghid", [P, F0 // P, G * P], at=w3)
            after(PE, r_ld.all())
            m = pe_line.did(nc.tensor.matmul(bank[6][0:R0, 0:B], rw1[:], pooled[:], start=True, stop=True))
            after(ACTE, m, r_ld.all())
            m = act_line.did(nc.scalar.activation(rh[:], bank[6][0:R0, 0:B], ACT.Tanh, bias=rb1[:, 0:1], scale=1.0 / S))
            after(PE, m)
            m = pe_line.did(nc.tensor.matmul(bank[7][0:B, 0:E0], rh[:], rw2[:], start=True, stop=True))
            after(DVE, m, r_ld.all())
            m = chain(lambda: v.tensor_tensor(prob[:], bank[7][0:B, 0:E0], rb2[:], ALU.add),
                      lambda: v.tensor_reduce(one[:], prob[:], AX.X, ALU.max),
                      lambda: v.tensor_scalar(prob[:], prob[:], one[:, 0:1], None, ALU.subtract))
            after(ACTE, m)
            after(DVE, act_line.did(nc.scalar.activation(prob[:], prob[:], ACT.Exp)))
            nc.scalar.preload_act_table(ACT.Gelu_apprx_tanh)
            chain(lambda: v.tensor_reduce(one[:], prob[:], AX.X, ALU.add),
                  lambda: v.reciprocal(one[:], one[:]),
                  lambda: v.tensor_scalar(prob[:], prob[:], one[:, 0:1], None, ALU.mult),
                  lambda: v.max(best[:], prob[:]),
                  lambda: v.max_index(best_at[:], best[:], prob[:]),
                  lambda: v.tensor_copy(best_atf[:], best_at[:]),
                  lambda: v.tensor_reduce(one[:], best[:, 0:K0], AX.X, ALU.add),
                  lambda: v.reciprocal(one[:], one[:]),
                  lambda: v.tensor_scalar(best[:], best[:], one[:, 0:1], None, ALU.mult))
            for k in range(K0):
                dst = zone_b if k == 0 else picked0
                m = chain(lambda: v.tensor_scalar(dst[:], ids[0:B, 0:E0], best_atf[:, k:k + 1], best[:, k:k + 1],
                                                  ALU.is_equal, ALU.mult))
                if k > 0:
                    m = chain(lambda: v.tensor_tensor(zone_b[:], zone_b[:], picked0[:], ALU.add))
            after(SP, m)
            load(sent, a["routes_w"], zone_b[:])
            after(SP, sent.all())
            for g in range(2):
                load(routes_ld, zone_w[g * S:(g + 1) * S, :, :],
                     a["routes_w"].rearrange("(o t g) k -> g o t k", o=1, g=2)[g].to_broadcast([S, T, E0]))

        if stages >= 3:
            after(DVE, g_ld.all())
            after(PE, zones_ld.all())
            after(DVE, routes_ld.all())
            assert E0 == EX
            gates = new(T // G * E0, 2, credit=1)

            def make_gate(g, e, n):
                tiles = bass.ds(g * G, G)
                after(DVE, gates.at(n - 1))
                after(DVE, gates.did(v.scalar_tensor_tensor(out=picked[:], in0=chosen[:, tiles, :], scalar=float(e),
                                                            in1=weight[:, tiles, :], op0=ALU.is_equal, op1=ALU.mult), n))
                gates.did(v.tensor_reduce(gate[:, tiles, e:e + 1], picked[:], AX.X, ALU.add), n)

            experts(E0, F0 // P, wza, wzb, ghid, zone_w, ACT.Gelu_apprx_tanh, make_gate)
            stage_end()
            load(narrow_ld, w2e, a["L1_ffn_W2"].rearrange("e (c p) d -> p (e c) d", p=P))

        if stages >= 4:
            w4 = ExitStack()
            kT, qT = twice("kT", [P, P], at=w4), twice("qT", [P, P], at=w4)
            qh = twice("qh", [P, H1, P], at=w4)
            sm = twice("sm", [P, H1, P], at=w4)
            v1, o17 = twice("v1_", [P, H1, D1 + 1], at=w4), twice("o17_", [P, H1, D1 + 1], at=w4)
            dn, sq, on = twice("dn", [P, H1], at=w4), twice("sq", [P, H1, D1], at=w4), twice("on", [P, H1, D1], at=w4)
            for u in range(2):
                fill(v1[u][:], 1.0)
            after(DVE, a_ld.all())
            m = chain(lambda: v.tensor_scalar(wo1[:], wo1[:], nw1[:, 0:1], None, ALU.mult))
            for engine in (PE, ACTE, DVE):
                after(engine, a_ld.all(), pool_line.all(), m)
            W17 = H1 * (D1 + 1)
            PER_BANK = 3
            norm = Norm(bank[0][:, 0:P], sharing=lambda n: ens_norm.moved.at(n - ENS_LAG))
            ens_norm = Norm(bank[0][:, P:2 * P], keep=HT, buffers=1, sharing=lambda n: norm.moved.at((n + (ENS_LAG - 1)).upto(T - 1)))
            ENS_LAG = 8
            qkv_made, qkv_moved, spread = new(T), new(T, 3), new(T)
            scored, masked = new(T, 2), new(T, 2)
            mixed, taken = new(T), new(T, H1)
            divided, rooted, normed = new(T, 7), new(T), new(T)
            o_turned, o_moved, projected, streamed = new(T), new(T), new(T), new(T)

            def causal_project(n, u):
                after(PE, norm.moved.at(n), qkv_moved.at(n - 1))
                nc.tensor.matmul(bank[1][:, 0:P], wqk1[:, 0, :], hT[u][:], start=True, stop=True)
                nc.tensor.matmul(bank[1][:, P:2 * P], wqk1[:, 1, :], hT[u][:], start=True, stop=True)
                m = qkv_made.did(nc.tensor.matmul(bank[1][:, 2 * P:3 * P], hT[u][:], wv1[:], start=True, stop=True), n)
                after(ACTE, m, spread.at(n - 2), scored.at(n - 2), mixed.at(n - 2))
                q = qkv_moved.did(nc.scalar.activation(qT[u][:], bank[1][:, 0:P], ACT.Copy), n)
                qkv_moved.did(nc.scalar.activation(kT[u][:], bank[1][:, P:2 * P], ACT.Copy), n)
                qkv_moved.did(nc.scalar.activation(v1[u][:, :, 0:D1], bank[1][:, 2 * P:3 * P].rearrange("p (h d) -> p h d", h=H1),
                                                   ACT.Copy), n)
                after(POOL, q, scored.at(n - 2))
                spread.did(nc.gpsimd.tensor_tensor(qh[u][:], qT[u][:].unsqueeze(1).to_broadcast([P, H1, P]),
                                                   head_of1.unsqueeze(2).to_broadcast([P, H1, P]), ALU.mult), n)

            def causal_score(n, u):
                after(PE, spread.at(n), qkv_moved.at(n), masked.at(n - 1))
                for k in range(2):
                    scored.did(nc.tensor.matmul(bank[2 + k][:], kT[u][:], qh[u][:, 4 * k:4 * k + 4, :].rearrange("p h n -> p (h n)"),
                                                start=True, stop=True), n)

            def causal_mask(k):
                def step(n, u):
                    after(DVE, scored.at(n, k + 1), mixed.at(n - 2))
                    masked.did(v.tensor_tensor(sm[u][:, 4 * k:4 * k + 4, :], bank[2 + k][:].rearrange("p (h n) -> p h n", h=4),
                                               causal.unsqueeze(1).to_broadcast([P, 4, P]), ALU.mult), n)
                return step

            places = [(bank[4 + hd // PER_BANK], hd % PER_BANK) for hd in range(H1)]

            def causal_mix(n, u):
                after(PE, masked.at(n), taken.at(n - 1))
                for hd, (bk, r) in enumerate(places):
                    m = nc.tensor.matmul(bk[:, r * W17:(r + 1) * W17], sm[u][:, hd, :], v1[u][:].rearrange("p h d -> p (h d)"),
                                         start=True, stop=True)
                mixed.did(m, n)

            def causal_take(n, u):
                after(DVE, mixed.at(n), divided.at(n - 2))
                for hd, (bk, r) in enumerate(places):
                    c = r * W17 + hd * (D1 + 1)
                    taken.did(v.tensor_copy(o17[u][:, hd, :], bk[:, c:c + D1 + 1]), n)

            def causal_divide(k):
                def step(n, u):
                    row_sum = o17[u][:, :, D1]
                    if k == 0:
                        after(DVE, taken.at(n), normed.at(n - 2), o_turned.at(n - 2))
                    else:
                        after(DVE, divided.at(n, k))
                    make = (
                        lambda: v.scalar_tensor_tensor(out=dn[u][:], in0=row_sum, scalar=-1.0, in1=row_sum, op0=ALU.mult, op1=ALU.max),
                        lambda: v.tensor_scalar(dn[u][:], dn[u][:], 1.0, None, ALU.max),
                        lambda: v.reciprocal(dn[u][:], dn[u][:]),
                        lambda: v.tensor_tensor(on[u][:], o17[u][:, :, 0:D1], dn[u][:].unsqueeze(2).to_broadcast([P, H1, D1]), ALU.mult),
                        lambda: v.tensor_tensor(sq[u][:], on[u][:], on[u][:], ALU.mult),
                        lambda: v.tensor_reduce(dn[u][:], sq[u][:], AX.X, ALU.add),
                        lambda: v.tensor_scalar(dn[u][:], dn[u][:], 1.0 / D1, EPS, ALU.mult, ALU.add))[k]
                    divided.did(make(), n)
                return step

            def causal_root(n, u):
                after(POOL, divided.at(n))
                rooted.did(nc.gpsimd.tensor_tensor(dn[u][:], dn[u][:], neghalf[:, 0:H1], ALU.pow), n)

            def causal_turn(n, u):
                after(DVE, rooted.at(n))
                m = normed.did(v.tensor_tensor(on[u][:], on[u][:], dn[u][:].unsqueeze(2).to_broadcast([P, H1, D1]), ALU.mult), n)
                after(PE, m, streamed.at(n - 1))
                m = o_turned.did(nc.tensor.transpose(bank[7][:, 0:P], on[u][:].rearrange("p h d -> p (h d)"), ident), n)
                after(ACTE, m, projected.at(n - 2))
                o_moved.did(nc.scalar.activation(oT[u][:], bank[7][:, 0:P], ACT.Copy), n)

            def causal_out(n, u):
                after(PE, o_moved.at(n))
                projected.did(nc.tensor.matmul(bank[7][:, P:2 * P], oT[u][:], wo1[:], start=True, stop=True), n)

            def causal_stream(n, u):
                after(DVE, projected.at(n))
                x = X[:, n.times(1), :]
                streamed.did(v.tensor_tensor(x, x, bank[7][:, P:2 * P], ALU.add), n)

            pipeline(nc, T, [(4, causal_mix), (6, causal_turn), (1, lambda n, u: norm.finish(n, u, qkv_made.at(n - 2))),
                             (ENS_LAG, ens_norm.finish), (3, causal_score),
                             (0, norm.moments), (7, lambda n, u: ens_norm.moments(n, u, streamed.at(n))),
                             (5, causal_divide(0)), (0, norm.gather), (7, ens_norm.gather), (5, causal_divide(1)),
                             (0, norm.invert), (5, causal_divide(2)), (7, ens_norm.invert), (5, causal_divide(3)), (4, causal_take),
                             (5, causal_divide(4)), (3, causal_mask(0)), (5, causal_divide(5)), (3, causal_mask(1)),
                             (5, causal_divide(6)), (6, causal_out), (5, causal_root), (2, causal_project), (6, causal_stream)])
            stage_end()
            w4.close()

        if stages >= 5:
            after(PE, ens_ld.all())
            nc.scalar.preload_act_table(ACT.Relu)
            experts(EX, FX // P, wpi, wpo, [t[:, 0:FX // P, :] for t in ghid], gate, None)
            stage_end()
            w3.close()
            w5.close()

        if stages >= 6:
            w6 = ExitStack()
            zero = sb("zero", [P, D], at=w6)
            sent_rows = signals.alternating(T + 2, K1, "rows")
            eqs = sb("eqs", [P, T, E1], at=w6)
            first, second = sb("first", [P, T, E1], at=w6), sb("second", [P, T, E1], at=w6)
            m1, m2, rk = sb("m1", [P, T], at=w6), sb("m2", [P, T], at=w6), sb("rk", [P, T], at=w6)
            rid = sb("rid", [P, E1], at=w6)
            Hn = HT
            after(POOL, fill(zero[:], 0.0))
            rows_p = a["routed_rows"].rearrange("(j p) d -> p j d", p=P)
            for u in range(2):
                for k in range(K1):
                    part = slice((2 * u + k) * SLOTS // 4, (2 * u + k + 1) * SLOTS // 4)
                    zeroed = sent_rows.did(nc.gpsimd.dma_start(rows_p[:, part, :], zero[:].unsqueeze(1).to_broadcast([P, SLOTS // 4, D])),
                                           Item(u))
            norm = Norm(bank[7][:, 0:P], pool_step=lambda n, u, x, h: nc.gpsimd.tensor_copy(Hn[:, n.times(1), :], h))
            scored, kept = new(T), new(T)
            after(PE, t_ld.all())

            def score(n, u):
                after(PE, norm.moved.at(n), kept.at(n - 1))
                m = scored.did(nc.tensor.matmul(bank[6][:, 0:E1], hT[u][:], wr[:], start=True, stop=True), n)
                after(ACTE, m)
                kept.did(nc.scalar.activation(lg[:, n.times(1), :], bank[6][:, 0:E1], ACT.Copy), n)

            pipeline(nc, T, [(0, norm.begin), (1, lambda n, u: norm.finish(n, u, scored.at(n - 2))), (1, score)])
            for engine in (POOL, SP):
                after(engine, sent_rows.at(Item(0)), sent_rows.at(Item(1)))
            stage_end(keep=True)
            after(DVE, t_ld.all())

            over_t = lambda m: m[:].unsqueeze(2).to_broadcast([P, T, E1])
            over_e = lambda m: m[:].unsqueeze(1).to_broadcast([P, T, E1])
            step = chain(
                lambda: v.tensor_scalar(rid[:], ids, -1.0, float(E1), ALU.mult, ALU.add),
                lambda: v.tensor_tensor(lg[:], lg[:], over_e(br), ALU.add),
                lambda: v.tensor_reduce(m1[:], lg[:], AX.X, ALU.max),
                lambda: v.tensor_tensor(lg[:], lg[:], over_t(m1), ALU.subtract))
            after(ACTE, step)
            after(DVE, act_line.did(nc.scalar.activation(lg[:], lg[:], ACT.Exp)))
            chain(
                lambda: v.tensor_reduce(m1[:], lg[:], AX.X, ALU.add),
                lambda: v.reciprocal(m1[:], m1[:]),
                lambda: v.tensor_tensor(lg[:], lg[:], over_t(m1), ALU.mult))
            for most, hot in ((m1, first), (m2, second)):
                chain(
                    lambda: v.tensor_reduce(most[:], lg[:], AX.X, ALU.max),
                    lambda: v.tensor_tensor(eqs[:], lg[:], over_t(most), ALU.is_equal),
                    lambda: v.tensor_tensor(eqs[:], eqs[:], over_e(rid), ALU.mult),
                    lambda: v.tensor_reduce(rk[:], eqs[:], AX.X, ALU.max),
                    lambda: v.tensor_tensor(hot[:], over_e(rid), over_t(rk), ALU.is_equal),
                    lambda: v.scalar_tensor_tensor(out=lg[:], in0=hot[:], scalar=-2.0, in1=lg[:], op0=ALU.mult, op1=ALU.add))
            ones = sb("ones", [P, P], at=w6)
            both = eqs
            step = chain(
                lambda: v.tensor_tensor(rk[:], m1[:], m2[:], ALU.add),
                lambda: v.reciprocal(rk[:], rk[:]),
                lambda: v.tensor_tensor(m1[:], m1[:], rk[:], ALU.mult),
                lambda: v.tensor_tensor(m2[:], m2[:], rk[:], ALU.mult),
                lambda: v.memset(ones[:], 1.0),
                lambda: v.tensor_tensor(both[:], first[:], second[:], ALU.add))
            flat = both[:].rearrange("p t e -> p (t e)")
            after(PE, step)
            nc.tensor.matmul(bank[0][:, 0:T * E1], before, flat, start=True, stop=True)
            counted = pe_line.did(nc.tensor.matmul(bank[1][:, 0:T * E1], ones[:], flat, start=True, stop=True))
            after(DVE, counted)
            sums = [sb(f"sums{k}", [P, T, E1], at=w6) for k in range(2)]
            place = sb("place", [P, T, E1], at=w6)
            size, end, begin = sb("size", [P, E1], at=w6), sb("end", [P, E1], at=w6), sb("begin", [P, E1], at=w6)
            size_i = sb("size_i", [P, E1], I32, at=w6)
            totals = bank[1][:, 0:T * E1].rearrange("p (t e) -> p t e", t=T)
            chain(lambda: v.tensor_copy(sums[0][:], totals))
            k, reach = 0, 1
            while reach < T:
                chain(lambda: v.tensor_copy(sums[1 - k][:, 0:reach, :], sums[k][:, 0:reach, :]),
                      lambda: v.tensor_tensor(sums[1 - k][:, reach:, :], sums[k][:, reach:, :], sums[k][:, 0:T - reach, :], ALU.add))
                k, reach = 1 - k, reach * 2
            run_sum = sums[k]
            where = sb("where", [P, T, K1], U32, at=w6)
            shift = P.bit_length() - 1
            chain(
                lambda: v.tensor_scalar(size[:], run_sum[:, T - 1, :], float(P - 1), None, ALU.add),
                lambda: v.tensor_copy(size_i[:], size[:]),
                lambda: v.tensor_scalar(size_i[:], size_i[:], shift, shift, ALU.logical_shift_right, ALU.logical_shift_left),
                lambda: v.tensor_copy(size[:], size_i[:]),
                lambda: v.tensor_tensor_scan(end[:], ones[:, 0:E1], size[:], 0.0, ALU.mult, ALU.add),
                lambda: v.tensor_tensor(begin[:], end[:], size[:], ALU.subtract),
                lambda: v.tensor_tensor(place[:], run_sum[:], totals, ALU.subtract),
                lambda: v.tensor_tensor(place[:], place[:], bank[0][:, 0:T * E1].rearrange("p (t e) -> p t e", t=T), ALU.add),
                lambda: v.tensor_tensor(place[:], place[:], over_e(begin), ALU.add))
            for k, hot in enumerate((first, second)):
                chain(
                    lambda: v.tensor_tensor(hot[:], hot[:], place[:], ALU.mult),
                    lambda: v.tensor_reduce(rk[:], hot[:], AX.X, ALU.add),
                    lambda: v.tensor_copy(where[:, :, k], rk[:]))
            past = sb("past", [1, SLOTS, E1], at=w6)
            slot_ef = sb("slot_ef", [1, SLOTS], at=w6)
            slot_e = sb("slot_e", [1, SLOTS], U32, at=w6)
            chain(
                lambda: v.tensor_tensor(past[:], end[0:1, :].unsqueeze(1).to_broadcast([1, SLOTS, E1]),
                                        slot_start[0:1, :].unsqueeze(2).to_broadcast([1, SLOTS, E1]), ALU.is_le),
                lambda: v.tensor_reduce(slot_ef[:], past[:], AX.X, ALU.add),
                lambda: v.tensor_scalar(slot_e[:], slot_ef[:], float(E1 - 1), None, ALU.min))
            stage_end(keep=True)

            row_at = twice("row_at", [P, K1], U32, at=w6)
            sent_row = twice("sent_row", [P, D], at=w6)
            placed, copied = new(T), new(T)

            def dispatch(n, u):
                for engine in (DVE, ACTE):
                    after(engine, sent_rows.at(n))
                m1_ = placed.did(v.tensor_copy(row_at[u][:], where[:, n.times(1), :]), n)
                m2_ = copied.did(nc.scalar.activation(sent_row[u][:], Hn[:, n.times(1), :], ACT.Copy), n)
                apart(POOL, m1_, m2_)
                for k in range(K1):
                    sent_rows.did(nc.gpsimd.indirect_dma_start(
                        a["routed_rows"], bass.IndirectOffsetOnAxis(ap=row_at[u][:, k:k + 1], axis=0), sent_row[u][:], None), n + 2)

            pipeline(nc, T, [(0, dispatch)])
            for engine in (POOL, SP):
                after(engine, sent_rows.at(Item(T)), sent_rows.at(Item(T + 1)))
            stage_end()

            _, stat, mv, ve, rstd = norm_sets[0]
            xg, yn = twice("xg", [P, D], at=w6), twice("yn", [P, D], at=w6)
            gb = twice("gb", [P, 2 * D], at=w6)
            silu = twice("silu", [P, F1], at=w6)
            prodT = twice("prodT", [P, F1 // P, P], at=w6)
            rows_in, affine_in, y_out = (signals.alternating(SLOTS, queue="slots") for _ in range(3))
            x_turned, x_moved = new(SLOTS), new(SLOTS)
            widened, gated, product = new(SLOTS, 2), new(SLOTS), new(SLOTS)
            p_turned, p_moved, narrowed = new(SLOTS), new(SLOTS), new(SLOTS)
            measured, rooted, normed, scaled = new(SLOTS, 3), new(SLOTS), new(SLOTS), new(SLOTS, 2)
            after(PE, experts_ld.all(), narrow_ld.all())

            def expert_of(engine, n):
                return engine.value_load(slot_e[0:1, bass.ds(n.times(1), 1)], min_val=0, max_val=E1 - 1)

            def slot_load(n, u):
                after(SP, x_turned.at(n - 2))
                rows_in.did(SP.dma_start(xg[u][:], a["routed_rows"][bass.ds(n.times(P), P), :]), n)

            def slot_affine(n, u):
                e = expert_of(SP, n)
                after(SP, scaled.at(n - 2))
                affine_in.did(SP.dma_start(gb[u][:], a["gamma_beta"][bass.ds(e, 1), :].to_broadcast([P, 2 * D])), n)

            def slot_turn(n, u):
                after(PE, rows_in.at(n), x_moved.at(n - 1))
                m = x_turned.did(nc.tensor.transpose(bank[7][:, 0:P], xg[u][:], ident), n)
                after(ACTE, m, widened.at(n - 2))
                x_moved.did(nc.scalar.activation(hT[u][:], bank[7][:, 0:P], ACT.Copy), n)

            def slot_widen(n, u):
                e = expert_of(PE, n)
                after(PE, x_moved.at(n), gated.at(n - 2), product.at(n - 2))
                up1, up3 = bank[2 * u], bank[2 * u + 1]
                m1_ = widened.did(nc.tensor.matmul(up1[:], hT[u][:], w13[:, e, 0:F1], start=True, stop=True), n)
                m3_ = widened.did(nc.tensor.matmul(up3[:], hT[u][:], w13[:, e, F1:2 * F1], start=True, stop=True), n)
                after(ACTE, m1_, p_turned.at(n - 2))
                m = gated.did(nc.scalar.activation(silu[u][:], up1[:], ACT.Silu), n)
                after(DVE, m, m3_)
                product.did(v.tensor_tensor(silu[u][:], silu[u][:], up3[:], ALU.mult), n)

            def slot_turn_hidden(n, u):
                after(PE, product.at(n), p_moved.at(n - 1))
                for c in range(F1 // P):
                    m = nc.tensor.transpose(bank[4][:, c * P:(c + 1) * P], silu[u][:, c * P:(c + 1) * P], ident)
                after(ACTE, p_turned.did(m, n), narrowed.at(n - 2))
                p_moved.did(nc.scalar.activation(prodT[u][:], bank[4][:].rearrange("p (c n) -> p c n", c=F1 // P), ACT.Copy), n)

            def slot_narrow(n, u):
                e = expert_of(PE, n)
                after(PE, p_moved.at(n), normed.at(n - 2))
                y = bank[5 + u][:, 0:D]
                for c in range(F1 // P):
                    m = nc.tensor.matmul(y, prodT[u][:, c, :], w2e[:, e * (F1 // P) + c, :], start=(c == 0), stop=(c == F1 // P - 1))
                after(DVE, narrowed.did(m, n))
                apart(DVE, measured.did(v.bn_stats(stat[u][:], y), n))
                after(DVE, measured.did(v.bn_aggr(mv[u][:], stat[u][:]), n))
                m = measured.did(v.tensor_scalar(ve[u][:], mv[u][:, 1:2], EPS, None, ALU.add), n)
                after(POOL, m)
                rooted.did(nc.gpsimd.tensor_tensor(rstd[u][:], ve[u][:], neghalf[:, 0:1], ALU.pow), n)

            def slot_finish(n, u):
                after(DVE, rooted.at(n), y_out.at(n - 2))
                m = normed.did(v.tensor_scalar(yn[u][:], bank[5 + u][:, 0:D], mv[u][:, 0:1], rstd[u][:, 0:1],
                                               ALU.subtract, ALU.mult), n)
                after(POOL, m, affine_in.at(n))
                after(POOL, scaled.did(nc.gpsimd.tensor_tensor(yn[u][:], yn[u][:], gb[u][:, 0:D], ALU.mult), n))
                scaled.did(nc.gpsimd.tensor_tensor(yn[u][:], yn[u][:], gb[u][:, D:2 * D], ALU.add), n)

            def slot_store(n, u):
                after(SP, scaled.at(n))
                y_out.did(SP.dma_start(a["expert_rows"][bass.ds(n.times(P), P), :], yn[u][:]), n)

            nc.scalar.preload_act_table(ACT.Silu)
            pipeline(nc, SLOTS, [(0, slot_load), (5, slot_store), (3, slot_affine), (3, slot_turn_hidden), (1, slot_turn),
                                 (4, slot_finish), (2, slot_widen), (3, slot_narrow)])
            for engine in (POOL, SP):
                after(engine, y_out.at(Item(SLOTS - 2)), y_out.at(Item(SLOTS - 1)))
            stage_end()

            got = [twice(f"got{k}_", [P, D], at=w6) for k in range(K1)]
            got_rows = signals.alternating(T, K1, "rows")
            stored = signals.alternating(T, queue="slots")
            placed, taken = new(T), new(T, K1)
            o_view = out.rearrange("b s d -> (b s) d")

            def fetch(n, u):
                after(DVE, got_rows.at(n - 2))
                m = placed.did(v.tensor_copy(row_at[u][:], where[:, n.times(1), :]), n)
                apart(POOL, m, taken.at(n - 2))
                for k in range(K1):
                    got_rows.did(nc.gpsimd.indirect_dma_start(
                        got[k][u][:], None, a["expert_rows"], bass.IndirectOffsetOnAxis(ap=row_at[u][:, k:k + 1], axis=0)), n)

            def combine(n, u):
                after(DVE, got_rows.at(n))
                x = X[:, n.times(1), :]
                for k, w in enumerate((m1, m2)):
                    m = taken.did(v.scalar_tensor_tensor(out=x, in0=got[k][u][:], scalar=w[:, bass.ds(n.times(1), 1)],
                                                         in1=x, op0=ALU.mult, op1=ALU.add), n)
                    after(DVE, m)
                after(SP, m)
                stored.did(SP.dma_start(o_view[bass.ds(n.times(P), P), :], x), n)

            pipeline(nc, T, [(0, fetch), (1, combine)])
            after(SP, stored.at(Item(T - 2)), stored.at(Item(T - 1)))
            w6.close()

        if stages < 6:
            if stages < 3: w5.close()
            if 3 <= stages < 5:
                w3.close()
                w5.close()
            after(SP, *[line.all() for line in (pe_line, dve_line, cx_ld, zones_ld, ens_ld, experts_ld, g_ld)])
            if stages >= 3: after(SP, narrow_ld.all())
            load(out_st, out.rearrange("b s d -> (b s) d").rearrange("(t p) d -> p t d", p=P), X[:])
            after(SP, out_st.all())


def constants():
    r, c = np.arange(P)[:, None], np.arange(P)[None, :]
    masks = [r == c, np.concatenate([r // DH0 == c // DH0, r // DH0 == c[:, :H0]], axis=1), r // D1 == c[:, :H1],
             (r // S == c // S) & (c >= r), r < c,
             c[:, :E1] + 0 * r, P * c[:, :SLOTS] + 0 * r]
    return np.concatenate([m.astype(np.float32) for m in masks], axis=1)


def lay_out(inputs):
    a = {n: np.ascontiguousarray(v) for n, v in inputs.items()}
    a["consts"] = constants()
    a["ctxT"] = np.ascontiguousarray(a["ctx_512"].transpose(0, 2, 1))
    for n in ("Wq", "Wk", "Wv"):
        a[f"L0_xattn_{n}T"] = np.ascontiguousarray(a.pop(f"L0_xattn_{n}").T)
    for n in ("Wq", "Wk", "Wv", "Wo"):
        a[f"L1_attn_{n}T"] = np.ascontiguousarray(a.pop(f"L1_attn_{n}").T)
    a["gamma_beta"] = np.concatenate([a.pop("L1_ffn_gamma"), a.pop("L1_ffn_beta")], axis=1)
    a["proj_inT"] = np.ascontiguousarray(a.pop("L1_xattn_proj_in").transpose(2, 0, 1))
    a["proj_outT"] = np.ascontiguousarray(a.pop("L1_xattn_proj_out").transpose(0, 2, 1))
    a["ctx_tokens"] = a["ctxT"].reshape(B * S, CD)
    a["itok_tokens"] = np.ascontiguousarray(a.pop("itok_BxS2xS_0_7").transpose(0, 2, 1)).reshape(B * S, S)
    return a


def kernel(**inputs):
    import concourse.bacc as bacc
    from concourse.bass_utils import run_bass_kernel_spmd

    arrays = lay_out(inputs)

    nc = bacc.Bacc("TRN2", target_bir_lowering=False, num_devices=1)
    args = {n: nc.dram_tensor(f"in_{n}", v.shape, mybir.dt.from_np(v.dtype), kind="ExternalInput").ap()
            for n, v in arrays.items()}
    build(nc, args, nc.dram_tensor("out_x", (B, S, D), F32, kind="ExternalOutput").ap())
    r = run_bass_kernel_spmd(nc, [{f"in_{n}": v for n, v in arrays.items()}], core_ids=[0])
    return r.results[0]["out_x"]
```

```python
from contextlib import ExitStack

import numpy as np

import concourse.bass as bass
from concourse import mybir
from concourse.alu_op_type import AluOpType as ALU

ACT = mybir.ActivationFunctionType
AX = mybir.AxisListType
F32 = mybir.dt.float32
I32 = mybir.dt.int32
U32 = mybir.dt.uint32
F32R = mybir.dt.float32r

B, S, D = 32, 64, 128
P = 128
T = B * S // P
EPS = 1e-5
H0, DH0 = 16, 8
HX, DX = 16, 64
CD = 64
JX = HX * CD // P
E0, F0, K0, R0 = 8, 512, 3, 32
H1, D1 = 8, 16
EX, FX = 8, 256
E1, F1, K1 = 16, 512, 2
SLOTS = (K1 * B * S + E1 * (P - 1)) // P
CAP = T * P
SPARE_ROW = E1 * CAP
IDLE = K1 * B * S
CONST_WIDTHS = [P, P + H0, H1, P, P, E1, SLOTS, E1, K1 * T, 1]
G = 4


class Signal:

    def __init__(self, sem, base, per=1, unit=1, credit=0):
        self.sem, self.base, self.per, self.unit, self.credit = sem, base, per, unit, credit
        self.item, self.k = None, 0

    def did(self, instruction, n):
        self.item, self.k = n, self.k + 1 if n == self.item else 1
        assert self.k <= self.per
        instruction.then_inc(self.sem, self.unit)
        return self.at(n, self.k)

    def did_after(self, engine, n, *marks):
        after(engine, *marks)
        engine.sem_inc(self.sem, self.unit)

    def at(self, n, k=None):
        if n < -self.credit:
            return None
        return self, n, (self.per if k is None else k)


class Line(Signal):

    def __init__(self, sem, unit=1):
        super().__init__(sem, 0, 1, unit)
        self.count = 0

    def did(self, instruction):
        self.count += 1
        return super().did(instruction, Item(self.count - 1))

    def all(self):
        return self.at(Item(self.count - 1))


class Alternating:

    def __init__(self, even, odd):
        self.pair = even, odd

    def did(self, instruction, n):
        return self.pair[n.c % 2].did(instruction, n.half())

    def at(self, n):
        return self.pair[n.c % 2].at(n.half())


class Signals:

    def __init__(self, nc, ctx):
        self.nc, self.ctx, self.made, self.used = nc, ctx, {}, {}

    def new(self, count, per=1, unit=1, credit=0, queue="own"):
        kept = self.made.setdefault((unit, queue), [])
        k = self.used.setdefault((unit, queue), 0)
        if k == len(kept):
            kept.append([self.ctx.enter_context(self.nc.semaphore(f"{queue}_{unit}_{k}")), 0])
        self.used[(unit, queue)] = k + 1
        if credit:
            self.nc.vector.sem_inc(kept[k][0], credit * per * unit)
        base = kept[k][1] + credit * per * unit
        kept[k][1] = base + count * per * unit
        return Signal(kept[k][0], base, per, unit, credit)

    def alternating(self, count, per=1, queue="own"):
        return Alternating(self.new(-(-count // 2), per, 16, queue=queue), self.new(count // 2, per, 16, queue=queue))

    def recycle(self):
        self.used = {}


class Item:

    def __init__(self, c, i=None, scale=0):
        self.c, self.i, self.scale = c, i, scale

    def __sub__(self, d):
        return Item(self.c - d, self.i, self.scale)

    def __add__(self, d):
        return self - -d

    def upto(self, last):
        return self if self.i is not None else Item(min(self.c, last))

    def half(self):
        return Item(self.c // 2, self.i, self.scale // 2)

    def __lt__(self, other):
        return self.c < other

    def __eq__(self, other):
        return other is not None and self.c == other.c and self.i is other.i

    def times(self, a, b=0):
        return self.c * a + b if self.i is None else self.i * (self.scale * a) + (self.c * a + b)


def after(engine, *marks):
    latest = {}
    for signal, n, k in filter(None, marks):
        reached = n.c * signal.per + k
        if signal not in latest or reached > latest[signal][0]:
            latest[signal] = reached, n
    for signal, (reached, n) in latest.items():
        u = signal.unit
        engine.wait_ge(signal.sem, n.times(signal.per * u, (reached - n.c * signal.per) * u + signal.base))


def exact_product(nc, out, lhsT, rhs):
    (lhsT, lhsT_low), (rhs, rhs_low) = ([x.bitcast(F32R) for x in pair] for pair in (lhsT, rhs))
    nc.tensor.matmul(out, lhsT, rhs, start=True, stop=False)
    nc.tensor.matmul(out, lhsT_low, rhs, start=False, stop=False)
    return nc.tensor.matmul(out, lhsT, rhs_low, start=False, stop=True)


def pipeline(nc, count, steps):
    depth = max(lag for lag, _ in steps)

    def at(m, parity, low=0, high=None):
        for lag, step in steps:
            if high is None or low <= m.c - lag < high:
                step(m - lag, (parity - lag) % 2)

    start = depth + 2
    passes = max(0, count - start) // 2
    for m in range(start):
        at(Item(m), m % 2, 0, count)
    if passes:
        with nc.Fori(0, passes) as i:
            for u in range(2):
                at(Item(start + u, i, 2), (start + u) % 2)
    for m in range(start + 2 * passes, count + depth):
        at(Item(m), m % 2, 0, count)



def build(nc, a, out, stages=6):
    a = dict(a)
    a["routes_w"] = nc.dram_tensor("routes_w", (B, E0), F32, kind="Internal").ap()
    a["routed_rows"] = nc.dram_tensor("routed_rows", (SPARE_ROW + P, D + 1), F32, kind="Internal").ap()
    a["answers"] = nc.dram_tensor("answers", (IDLE + SLOTS * P, D), F32, kind="Internal").ap()
    ctx = ExitStack()
    with ctx:
        def sem(name):
            return ctx.enter_context(nc.semaphore(name))

        def sb(name, shape, dt=F32, at=None):
            return (at or ctx).enter_context(nc.sbuf_tensor(name, shape, dt))

        def twice(name, shape, dt=F32, at=None):
            return [sb(f"{name}{u}", shape, dt, at) for u in range(2)]

        PE, DVE, ACTE, POOL, SP = nc.tensor, nc.vector, nc.scalar, nc.gpsimd, nc.sync
        v = nc.vector
        signals = Signals(nc, ctx)
        new = signals.new
        bank = [ctx.enter_context(nc.psum_tensor(f"bank{k}", [P, 512], F32)) for k in range(8)]
        pe_line, dve_line, act_line, pool_line, sp_line = (Line(sem(f"{n}_line")) for n in ("pe", "dve", "act", "pool", "sp"))
        spare = sem("spare")

        def apart(engine, *marks):
            after(engine, *marks)
            engine.sem_inc(spare)

        def stage_end(keep=False):
            ends = [line.did(engine.drain()) for engine, line in
                    ((PE, pe_line), (DVE, dve_line), (ACTE, act_line), (POOL, pool_line))]
            for engine in (PE, DVE, ACTE, POOL, SP):
                after(engine, *ends)
            if not keep:
                signals.recycle()

        def chain(*instructions):
            for make in instructions:
                done = dve_line.did(make())
                after(DVE, done)
            return done

        def fill(dst, value):
            after(POOL, pool_line.all() if pool_line.count else None)
            return pool_line.did(nc.gpsimd.memset(dst, value))

        def loads(name):
            return Line(sem(name), 16)

        def load(line, dst, src, queue=SP):
            return line.did(queue.dma_start(dst, src))

        def row(src, parts=P):
            return src.rearrange("(o n) -> o n", o=1).to_broadcast([parts, src.shape[0]])

        X = sb("X", [P, T, D])
        HT = sb("HT", [P, T, P])
        consts = sb("consts", [P, a["consts"].shape[1]])
        at = iter(np.cumsum([0] + CONST_WIDTHS).tolist())
        ident, same_head0, head_of1, causal, before, ids, slot_start, first_rows, places_of, idle_place = (
            consts[:, c:c + w] for c, w in zip(at, CONST_WIDTHS))
        neghalf = sb("neghalf", [P, H1])
        hT = twice("hT", [P, P])
        o_tok, oT = twice("o_tok", [P, D]), twice("oT", [P, P])
        norm_sets = [tuple(twice(f"{name}_{k}_", [P, w]) for name, w in (("h", D), ("stat", 6), ("mv", 2), ("ve", 1), ("rstd", 1)))
                     for k in range(2)]
        pad_row = sb("pad_row", [P, D + 1])
        pooled = sb("pooled", [P, B])
        narrow_mem = sb("narrow_mem", [P, 2 * E0 * F0])
        wza = narrow_mem[:, 0:E0 * F0].rearrange("p (e f) -> p e f", e=E0)
        wzb = narrow_mem[:, E0 * F0:].rearrange("p (e c d) -> p e c d", e=E0, d=D)
        assert 2 * E0 * F0 == E1 * F1
        w2e = narrow_mem[:].rearrange("p (e d) -> p e d", d=D)
        ZONE_PART = E0 * F0 // T
        wpi, wpo = sb("wpi", [P, EX, FX]), sb("wpo", [P, EX, FX // P, D])
        rw1, rw2, rb1, rb2 = sb("rw1", [P, R0]), sb("rw2", [R0, E0]), sb("rb1", [R0, 1]), sb("rb2", [B, E0])
        wqk1, wv1, wo1, nw1 = sb("wqk1", [P, 2, D]), sb("wv1", [P, D]), sb("wo1", [P, D]), sb("nw1", [P, 1])
        wr, br = sb("wr", [P, E1]), sb("br", [P, E1])
        r_ld, a_ld, t_ld = loads("router_loaded"), loads("causal_weights_loaded"), loads("router1_loaded")
        first_ld, zones_ld, ens_ld = loads("first_loaded"), loads("zone_weights_loaded"), loads("ensemble_weights_loaded")
        experts_ld, narrow_ld = loads("expert_weights_loaded"), loads("expert_second_weights_loaded")
        chosen = sb("chosen", [P, T, S], I32)
        weight = sb("weight", [P, T, CD])
        picked, gate = sb("picked", [P, G, S]), sb("gate", [P, T, EX])
        ghid = twice("ghid", [P, F0 // P, G * P])
        g_ld = loads("gates_loaded")
        wz = ExitStack()
        wza_high, wza_low, HT_low0 = sb("wza_high", [P, E0 * F0], at=wz), sb("wza_low", [P, E0 * F0], at=wz), sb("HT_low0", [P, T, P], at=wz)
        out_st, padded = loads("stored"), loads("rows_padded")
        x_view = a["x"].rearrange("b s d -> (b s) d").rearrange("(t p) d -> p t d", p=P)
        load(first_ld, X[:], x_view)
        load(first_ld, consts[:], a["consts"])
        neghalf_set = fill(neghalf[:], -0.5)

        def splitter(src, high, low):
            rounded, lowered = new(T), new(T)

            def step(n, u):
                m = rounded.did(v.tensor_copy(high(n).bitcast(F32R), src(n)), n)
                after(POOL, m)
                lowered.did(nc.gpsimd.tensor_tensor(low(n).bitcast(F32R), src(n), high(n), ALU.subtract), n)
            return step

        class Norm:

            def __init__(self, turn_bank, keep=None, pool_step=None, count=T, buffers=0, sharing=None, credit=0,
                         h_of=None, hT_of=None, low=None, sums=None):
                self.turn, self.pool_step, self.sharing = turn_bank, pool_step, sharing or (lambda n: None)
                self.low, self.sums = low, sums
                if low is not None:
                    self.lowered = new(count, 2 if sums is not None else 1)
                self.hT_of = hT_of or (lambda n, u: hT[u][:] if keep is None else keep[:, n.times(1), :])
                self.h_of = h_of or (lambda n, u: norm_sets[buffers][0][u][:])
                _, self.stat, self.mv, self.ve, self.rstd = norm_sets[buffers]
                self.stats, self.root, self.normed = new(count, 3, credit=credit), new(count, credit=credit), new(count, credit=credit)
                self.turned, self.moved = new(count, credit=credit), new(count, credit=credit)
                self.added = new(count, credit=credit) if pool_step else None

            def moments(self, n, u, *ready):
                apart(DVE, *ready, self.normed.at(n - 2), self.stats.at(n - 2))
                self.stats.did(v.bn_stats(self.stat[u][:], X[:, n.times(1), :]), n)

            def gather(self, n, u):
                apart(DVE, self.stats.at(n, 1), self.normed.at(n - 2))
                self.stats.did(v.bn_aggr(self.mv[u][:], self.stat[u][:]), n)

            def invert(self, n, u):
                after(DVE, self.stats.at(n, 2), self.root.at(n - 2))
                done = self.stats.did(v.tensor_scalar(self.ve[u][:], self.mv[u][:, 1:2], EPS, None, ALU.add), n)
                after(POOL, done, self.normed.at(n - 2))
                self.root.did(nc.gpsimd.tensor_tensor(self.rstd[u][:], self.ve[u][:], neghalf[:, 0:1], ALU.pow), n)

            def begin(self, n, u, *ready):
                self.moments(n, u, *ready)
                self.gather(n, u)
                self.invert(n, u)

            def finish(self, n, u, *read, free=None):
                after(DVE, free, self.root.at(n), self.stats.at(n), self.turned.at(n - 2), self.added.at(n - 2) if self.added else None)
                x, h = X[:, n.times(1), :], self.h_of(n, u)
                normed = self.normed.did(v.tensor_scalar(h, x, self.mv[u][:, 0:1], self.rstd[u][:, 0:1],
                                                         ALU.subtract, ALU.mult), n)
                if self.added:
                    after(POOL, normed)
                    self.added.did(self.pool_step(n, u, x, h), n)
                after(PE, normed, self.moved.at(n - 1), self.sharing(n), self.lowered.at(n - 1) if self.low is not None else None)
                turned = self.turned.did(nc.tensor.transpose(self.turn, h, ident), n)
                after(ACTE, turned, *read)
                dst = self.hT_of(n, u)
                self.moved.did(nc.scalar.activation(dst.bitcast(F32R) if self.low is not None else dst, self.turn, ACT.Copy), n)

            def lower(self, n, u):
                after(DVE, self.moved.at(n))
                self.lowered.did(v.tensor_tensor(self.low[:, n.times(1), :].bitcast(F32R), self.turn, self.hT_of(n, u), ALU.subtract), n)
                if self.sums is not None:
                    self.lowered.did(v.tensor_reduce(self.sums[:, bass.ds(n.times(2), 2)],
                                                     self.turn.rearrange("p (b n) -> p b n", b=2), AX.X, ALU.add), n)

        w1 = ExitStack()
        wq0, wkv0, wo0 = sb("wq0", [P, D], at=w1), sb("wkv0", [P, 2 * D], at=w1), sb("wo0", [P, D], at=w1)
        bq0, bkv0, bo0 = sb("bq0", [P, 1], at=w1), sb("bkv0", [P, 2 * D], at=w1), sb("bo0", [P, D], at=w1)
        load(first_ld, wq0[:], a["L0_attn_wq"])
        load(first_ld, wkv0[:, 0:D], a["L0_attn_wk"])
        load(first_ld, wkv0[:, D:2 * D], a["L0_attn_wv"])
        load(first_ld, wo0[:], a["L0_attn_wo"], ACTE)
        load(first_ld, bq0[:], a["L0_attn_bq"].rearrange("(n o) -> n o", o=1), ACTE)
        load(first_ld, bkv0[:, 0:D], row(a["L0_attn_bk"]), ACTE)
        load(first_ld, bkv0[:, D:2 * D], row(a["L0_attn_bv"]), ACTE)
        load(first_ld, bo0[:], row(a["L0_attn_bo"]), ACTE)
        wqk = sb("wqk", [P, JX, P], at=w1)
        wvo = sb("wvo", [P, JX, D], at=w1)
        box = sb("box", [P, D], at=w1)
        q_exps, q_pos, qf, k_exps, k_pos, kf = (twice(n, [P, P], at=w1) for n in ("q_exps", "q_pos", "qf", "k_exps", "k_pos", "kf"))
        kvb = twice("kvb", [P, 2 * D + H0], at=w1)
        kvsum = twice("kvsum", [P, 2, D + H0], at=w1)
        den = twice("den", [P, H0], at=w1)

        w1a = ExitStack()
        wqT = sb("wqT", [P, JX, P], at=w1a)
        wkT = sb("wkT", [P, JX, P], at=w1a)
        wvT = sb("wvT", [P, JX, P], at=w1a)
        wox = sb("wox", [P, JX, D], at=w1a)
        cx_ld = loads("cross_weights_loaded")
        fill(wkT[:], 0.0)
        zeroed = fill(wvT[:], 0.0)
        load(cx_ld, wqT[:], a["L0_xattn_WqT"].rearrange("(j p) n -> p j n", p=P))
        load(cx_ld, wox[:], a["L0_xattn_Wo"].rearrange("(j p) n -> p j n", p=P))
        load(cx_ld, box[:], row(a["L0_xattn_bo"]))
        after(SP, zeroed)
        for w, name in ((wkT, "L0_xattn_WkT"), (wvT, "L0_xattn_WvT")):
            src = a[name].rearrange("(j g p) n -> g p j n", g=2, p=DX)
            for g in range(2):
                load(cx_ld, w[g * DX:(g + 1) * DX, :, g * CD:(g + 1) * CD], src[g])
        load(r_ld, rw1[:], a["L0_ffn_W1"])
        load(r_ld, rw2[:], a["L0_ffn_W2"])
        load(r_ld, rb1[:], a["L0_ffn_b1"].rearrange("(n o) -> n o", o=1))
        load(r_ld, rb2[:], row(a["L0_ffn_b2"], B))
        load(a_ld, wqk1[:, 0, :], a["L1_attn_WqT"])
        load(a_ld, wqk1[:, 1, :], a["L1_attn_WkT"])
        load(a_ld, wv1[:], a["L1_attn_WvT"])
        load(a_ld, wo1[:], a["L1_attn_WoT"])
        for k in range(H1):
            load(a_ld, nw1[k * D1:(k + 1) * D1, :], a["L1_attn_norm_w"].rearrange("(n o) -> n o", o=1))
        load(t_ld, wr[:], a["L1_ffn_Wr"])
        load(t_ld, br[:], row(a["L1_ffn_br"]))
        load(zones_ld, wza, a["L0_ffn_Wa"].rearrange("e d f -> d e f"))
        load(zones_ld, wzb.rearrange("p e c d -> p (e c) d"), a["L0_ffn_Wb"].rearrange("e (c p) d -> p (e c) d", p=P))
        load(ens_ld, wpi[:], a["proj_inT"])
        load(ens_ld, wpo[:].rearrange("p e c i -> p (e c) i"), a["proj_outT"].rearrange("e (c p) i -> p (e c) i", p=P))

        for u in range(2):
            fill(kvb[u][:, 2 * D:], 1.0)
        for engine in (PE, DVE, ACTE, POOL):
            after(engine, pool_line.all(), first_ld.all())

        norm = Norm(bank[0][:, 0:P], pool_step=lambda n, u, x, h: nc.gpsimd.tensor_tensor(x, x, bo0[:], ALU.add))
        made, q_read, biased, k_read, q_mapped, k_mapped = new(T, 2), new(T, 2), new(T), new(T, 2), new(T), new(T)
        sums_made, sums_masked, applied, divided = new(T, 2), new(T, 2), new(T), new(T, 3)
        o_turned, o_moved, projected, streamed = new(T), new(T), new(T), new(T)
        sum_banks = bank[3], bank[7]

        def attn_project(n, u):
            after(PE, norm.moved.at(n), q_read.at(n - 1), biased.at(n - 1))
            made.did(nc.tensor.matmul(bank[1][:, 0:P], wq0[:], hT[u][:], start=True, stop=True), n)
            made.did(nc.tensor.matmul(bank[2][:, 0:2 * D], hT[u][:], wkv0[:], start=True, stop=True), n)

        def attn_exps(n, u):
            after(ACTE, made.at(n, 1), q_mapped.at(n - 2))
            q_read.did(nc.scalar.activation(q_exps[u][:], bank[1][:, 0:P], ACT.Exp, bias=bq0[:, 0:1]), n)
            q_read.did(nc.scalar.activation(q_pos[u][:], bank[1][:, 0:P], ACT.Relu, bias=bq0[:, 0:1]), n)
            after(DVE, made.at(n), k_read.at(n - 2), sums_made.at(n - 2))
            m = biased.did(v.tensor_tensor(kvb[u][:, 0:2 * D], bank[2][:, 0:2 * D], bkv0[:], ALU.add), n)
            after(ACTE, m, k_mapped.at(n - 2))
            k_read.did(nc.scalar.activation(k_exps[u][:], kvb[u][:, 0:D], ACT.Exp), n)
            k_read.did(nc.scalar.activation(k_pos[u][:], kvb[u][:, 0:D], ACT.Relu), n)

        def attn_map(n, u):
            for mapped, read, exps, pos, dst, before_ in ((q_mapped, q_read.at(n), q_exps, q_pos, qf, applied.at(n - 2)),
                                                          (k_mapped, k_read.at(n), k_exps, k_pos, kf, sums_made.at(n - 2))):
                after(DVE, read, before_)
                mapped.did(v.scalar_tensor_tensor(out=dst[u][:], in0=exps[u][:], scalar=1.0, in1=pos[u][:],
                                                  op0=ALU.min, op1=ALU.add), n)

        def attn_sums(n, u):
            after(PE, k_mapped.at(n), biased.at(n), sums_masked.at(n - 1))
            for b in range(2):
                rows = slice(b * S, b * S + S)
                sums_made.did(nc.tensor.matmul(sum_banks[b][:, 0:D + H0], kf[u][rows, :], kvb[u][rows, D:], start=True, stop=True), n)

        def attn_mask(n, u):
            after(DVE, sums_made.at(n), applied.at(n - 2))
            for b in range(2):
                sums_masked.did(v.tensor_tensor(kvsum[u][:, b, :], sum_banks[b][:, 0:D + H0], same_head0, ALU.mult), n)

        def attn_apply(n, u):
            after(PE, sums_masked.at(n), q_mapped.at(n), divided.at(n - 1))
            for b in range(2):
                m = nc.tensor.matmul(bank[4][b * S:b * S + S, 0:D + H0], qf[u][:, b * S:b * S + S], kvsum[u][:, b, :],
                                     start=True, stop=True)
            applied.did(m, n)

        def attn_guard(n, u):
            after(DVE, applied.at(n), divided.at(n - 2), o_turned.at(n - 2))
            divided.did(v.tensor_scalar(den[u][:], bank[4][:, D:D + H0], 1e-6, None, ALU.add), n)

        def attn_invert(n, u):
            after(DVE, divided.at(n, 1))
            divided.did(v.reciprocal(den[u][:], den[u][:]), n)

        def attn_divide(n, u):
            after(DVE, divided.at(n, 2))
            divided.did(v.tensor_tensor(
                o_tok[u][:].rearrange("p (h e) -> p h e", h=H0), bank[4][:, 0:D].rearrange("p (h e) -> p h e", h=H0),
                den[u][:].unsqueeze(2).to_broadcast([P, H0, DH0]), ALU.mult), n)

        def attn_turn(n, u):
            after(PE, divided.at(n), o_moved.at(n - 1))
            m = o_turned.did(nc.tensor.transpose(bank[5][:, 0:P], o_tok[u][:], ident), n)
            after(ACTE, m, projected.at(n - 2))
            o_moved.did(nc.scalar.activation(oT[u][:], bank[5][:, 0:P], ACT.Copy), n)

        def attn_out(n, u):
            after(PE, o_moved.at(n), streamed.at(n - 1))
            projected.did(nc.tensor.matmul(bank[6][:, 0:P], oT[u][:], wo0[:], start=True, stop=True), n)

        def attn_stream(n, u):
            after(DVE, projected.at(n), norm.added.at(n))
            x = X[:, n.times(1), :]
            streamed.did(v.tensor_tensor(x, x, bank[6][:, 0:P], ALU.add), n)

        nc.scalar.preload_act_table(ACT.Exp)
        pipeline(nc, T, [(4, attn_sums), (5, attn_apply), (1, lambda n, u: norm.finish(n, u, made.at(n - 2))), (2, attn_project), (7, attn_out), (6, attn_turn), (0, norm.moments), (4, attn_mask), (0, norm.gather),(5, attn_guard),  (0, norm.invert),(5, attn_invert),  (3, attn_map), (5, attn_divide),  (2, attn_exps), (7, attn_stream)])
        stage_end()

        after(PE, cx_ld.all())
        for j in range(JX):
            quarter = slice((j % 4) * P, (j % 4 + 1) * P)
            nc.tensor.matmul(bank[j // 4][:, quarter], wqT[:, j, :], wkT[:, j, :], start=True, stop=True)
            m = nc.tensor.matmul(bank[2 + j // 4][:, quarter], wvT[:, j, :], wox[:, j, :], start=True, stop=True)
        m = pe_line.did(m)
        after(DVE, m)
        after(ACTE, m)
        for k in range(2):
            fours = slice(4 * k, 4 * k + 4)
            dve_line.did(v.tensor_copy(wqk[:, fours, :], bank[k][:].rearrange("p (j n) -> p j n", j=4)))
            act_line.did(nc.scalar.activation(wvo[:, fours, :], bank[2 + k][:].rearrange("p (j n) -> p j n", j=4), ACT.Copy))
        stage_end()
        w1a.close()

        if stages >= 2:
            w2 = ExitStack()
            qx = twice("qx", [P, JX, P], at=w2)
            pr = twice("pr", [P, HX, S], at=w2)
            prT = twice("prT", [P, JX, P], at=w2)
            ov = twice("ov", [P, JX, P], at=w2)
            ctxT = twice("ctxT", [P, 2, P], at=w2)
            ctxd = twice("ctxd", [P, 2, P], at=w2)
            top, tot = twice("top", [P, HX], at=w2), twice("tot", [P, HX], at=w2)
            for u in range(2):
                fill(ctxT[u][:], 0.0)
                fill(ctxd[u][:], 0.0)
            after(SP, pool_line.all())
            keys_in, vals_in = signals.alternating(T, 2, "keys"), signals.alternating(T, 2, "keys")
            norm = Norm(bank[6][:, 0:P], pool_step=lambda n, u, x, h: nc.gpsimd.tensor_tensor(x, x, box[:], ALU.add),
                        sharing=lambda n: zone_norm.lowered.at(n - ZONE_LAG))
            zone_norm = Norm(bank[6][:, P:2 * P], keep=HT, buffers=1, sharing=lambda n: norm.moved.at((n + (ZONE_LAG - 1)).upto(T - 1)),
                             pool_step=lambda n, u, x, h: nc.gpsimd.tensor_tensor(x, x, h, ALU.add), low=HT_low0, sums=pooled)
            ZONE_LAG = 5
            queried, q_moved = new(T, 2), new(T, 2)
            scored, shifted, raised = new(T, 2), new(T, 4), new(T, 2)
            summed, shared = new(T, 4), new(T, 2)
            p_turned, p_moved, mixed, mix_moved = new(T, 2), new(T, 2), new(T, 2), new(T, 2)
            projected, streamed = new(T), new(T)

            def keys_load(n, u):
                after(SP, scored.at(n - 2))
                for g in range(2):
                    d = slice(g * S, (g + 1) * S)
                    keys_in.did(SP.dma_start(ctxT[u][d, :, d], a["ctxT"][bass.ds(n.times(2), 2)].rearrange("b c m -> c b m")), n)

            def values_load(n, u):
                after(SP, mixed.at(n - 2))
                for g in range(2):
                    d = slice(g * S, (g + 1) * S)
                    vals_in.did(SP.dma_start(ctxd[u][d, :, d], a["ctx_512"][bass.ds(n.times(2), 2)].rearrange("b m c -> m b c")), n)

            def cross_query(n, u):
                after(PE, norm.moved.at(n), q_moved.at(n - 1))
                for k in range(2):
                    for j in range(4):
                        m = nc.tensor.matmul(bank[k][:, j * P:(j + 1) * P], wqk[:, 4 * k + j, :], hT[u][:], start=True, stop=True)
                    m = queried.did(m, n)
                    after(ACTE, m, scored.at(n - 2))
                    q_moved.did(nc.scalar.activation(qx[u][:, 4 * k:4 * k + 4, :], bank[k][:].rearrange("p (j n) -> p j n", j=4), ACT.Copy), n)

            def cross_score(n, u):
                after(PE, q_moved.at(n), keys_in.at(n), shifted.at(n - 1))
                for k in range(2):
                    for j in range(4):
                        for b in range(2):
                            m = nc.tensor.matmul(bank[2 + k][b * S:(b + 1) * S, j * P:(j + 1) * P],
                                                 qx[u][:, 4 * k + j, b * S:(b + 1) * S], ctxT[u][:, b, :], start=True, stop=True)
                    heads = slice(8 * k, 8 * k + 8)
                    s = bank[2 + k][:].rearrange("p (h m) -> p h m", h=8)
                    after(DVE, scored.did(m, n), p_turned.at(n - 2))
                    after(DVE, shifted.did(v.tensor_reduce(top[u][:, heads], s, AX.X, ALU.max), n))
                    m = shifted.did(v.tensor_tensor(pr[u][:, heads, :], s, top[u][:, heads].unsqueeze(2).to_broadcast([P, 8, S]),
                                                    ALU.subtract), n)
                    after(ACTE, m)
                    raised.did(nc.scalar.activation(pr[u][:, heads, :], pr[u][:, heads, :], ACT.Exp, scale=DX ** -0.5), n)

            def cross_share(n, u):
                for k in range(2):
                    heads = slice(8 * k, 8 * k + 8)
                    after(DVE, raised.at(n, k + 1), shared.at(n - 2))
                    after(DVE, summed.did(v.tensor_reduce(tot[u][:, heads], pr[u][:, heads, :], AX.X, ALU.add), n))
                    m = summed.did(v.reciprocal(tot[u][:, heads], tot[u][:, heads]), n)
                    after(POOL, m)
                    shared.did(nc.gpsimd.tensor_tensor(pr[u][:, heads, :], pr[u][:, heads, :],
                                                       tot[u][:, heads].unsqueeze(2).to_broadcast([P, 8, S]), ALU.mult), n)

            def cross_turn(n, u):
                for k in range(2):
                    after(PE, shared.at(n, k + 1), mix_moved.at(n - 1))
                    for j in range(4 * k, 4 * k + 4):
                        m = nc.tensor.transpose(bank[4 + k][:, (j % 4) * P:(j % 4 + 1) * P],
                                                pr[u][:, 2 * j:2 * j + 2, :].rearrange("p h m -> p (h m)"), ident)
                    after(ACTE, p_turned.did(m, n), mixed.at(n - 2))
                    p_moved.did(nc.scalar.activation(prT[u][:, 4 * k:4 * k + 4, :],
                                                     bank[4 + k][:].rearrange("p (j n) -> p j n", j=4), ACT.Copy), n)

            def cross_mix(n, u):
                after(PE, p_moved.at(n), vals_in.at(n))
                for b in range(2):
                    m = mixed.did(nc.tensor.matmul(bank[4 + b][:], ctxd[u][:, b, :], prT[u][:, :, b * S:(b + 1) * S],
                                                   start=True, stop=True), n)
                    after(ACTE, m, projected.at(n - 2))
                    mix_moved.did(nc.scalar.activation(ov[u][:, :, b * S:(b + 1) * S],
                                                       bank[4 + b][:].rearrange("p (j n) -> p j n", j=JX), ACT.Copy), n)

            def cross_out(n, u):
                after(PE, mix_moved.at(n), streamed.at(n - 1))
                for j in range(JX):
                    m = nc.tensor.matmul(bank[7][:, 0:D], ov[u][:, j, :], wvo[:, j, :], start=(j == 0), stop=(j == JX - 1))
                after(DVE, projected.did(m, n), norm.added.at(n))
                x = X[:, n.times(1), :]
                streamed.did(v.tensor_tensor(x, x, bank[7][:, 0:D], ALU.add), n)

            for engine in (DVE, POOL):
                after(engine, zones_ld.all())
            zone_part = lambda w: lambda n: w[:, bass.ds(n.times(ZONE_PART), ZONE_PART)]
            split_weights = splitter(*map(zone_part, (narrow_mem[:, 0:E0 * F0], wza_high, wza_low)))

            pipeline(nc, T, [(0, keys_load), (2, values_load), (3, cross_turn),
                             (1, lambda n, u: norm.finish(n, u, queried.at(n - 2))), (ZONE_LAG, zone_norm.finish),
                             (0, norm.moments), (4, lambda n, u: zone_norm.moments(n, u, streamed.at(n))),
                             (0, norm.gather), (4, zone_norm.gather), (0, norm.invert), (4, zone_norm.invert),
                             (2, cross_score), (2, cross_share), (3, cross_mix), (1, cross_query), (ZONE_LAG, zone_norm.lower),
                             (0, split_weights), (3, cross_out)])
            stage_end()
            w2.close()
        w1.close()

        def experts(count, chunks, w_up, w_up_low, tokens_low, w_down, hid, gate, gelu, beside=None, behind=None, gated=None):
            ups, outs = bank[0:4], bank[4:6]
            back = len(ups) // chunks
            total = T // G * count
            widened = new(total, chunks)
            by_act = new(total, chunks if gelu else chunks // 2, credit=back)
            by_dve = None if gelu else new(total, chunks // 2, credit=back)
            narrowed, streamed = new(total), new(total, G, credit=2)
            after(DVE, gated)

            def widen(g, e, n):
                tokens, low = (t[:, bass.ds(g * G, G), :] for t in (HT, tokens_low))
                for c in range(chunks):
                    up = ups[(e * chunks + c) % len(ups)]
                    act_reads = bool(gelu) or c % 2 == 0
                    after(PE, (by_act if act_reads else by_dve).at(n - back, c + 1 if gelu else None))
                    m = widened.did(exact_product(nc, up[:], [w[:, e, c * P:(c + 1) * P] for w in (w_up, w_up_low)], (tokens, low)), n)
                    dst = hid[e % 2][:, c, :]
                    if act_reads:
                        after(ACTE, m)
                        by_act.did(nc.scalar.activation(dst, up[:], gelu or ACT.Relu), n)
                    else:
                        after(DVE, m)
                        by_dve.did(v.tensor_scalar(dst, up[:], 0.0, None, ALU.max), n)

            def narrow(g, e, n):
                after(PE, by_act.at(n), None if gelu else by_dve.at(n), streamed.at(n - 2))
                o = outs[e % 2]
                for j in range(G):
                    for c in range(chunks):
                        m = nc.tensor.matmul(o[:, j * P:(j + 1) * P], hid[e % 2][:, c, j * P:(j + 1) * P], w_down[:, e, c, :],
                                             start=(c == 0), stop=(c == chunks - 1))
                after(DVE, narrowed.did(m, n), streamed.at(n - 1))
                for j in range(G):
                    x = X[:, g * G + j, :]
                    streamed.did(v.scalar_tensor_tensor(out=x, in0=o[:, j * P:(j + 1) * P], scalar=gate[:, g * G + j, e:e + 1],
                                                        in1=x, op0=ALU.mult, op1=ALU.add), n)

            def group(g, item):
                for e in range(count + 1):
                    if e < count:
                        widen(g, e, item(e))
                    if e > 0:
                        narrow(g, e - 1, item(e - 1))
                    if e < count:
                        yield e

            if behind is None:
                with nc.Fori(0, T // G) as g:
                    for e in group(g, lambda e: Item(e, g, count)):
                        if beside:
                            beside(g, e, Item(e, g, count))
                return
            for e in group(0, Item):
                pass
            with nc.Fori(0, T // G - 1) as i:
                for e in group(i + 1, lambda e: Item(e + count, i, count)):
                    behind(e, Item(0, i, 1), streamed.at(Item(count - 1, i, count)))
            for e in range(count):
                behind(e, Item(T // G - 1), streamed.at(Item(total - 1)))

        load(g_ld, chosen[:], a["itok_tokens"].rearrange("(t p) k -> p t k", p=P))
        load(g_ld, weight[:], a["ctx_tokens"].rearrange("(t p) k -> p t k", p=P))

        if stages >= 3:
            w3 = ExitStack()
            sent, routes_ld = loads("routes_sent"), loads("routes_loaded")
            rh, prob, one = sb("rh", [R0, B], at=w3), sb("prob", [B, E0], at=w3), sb("one", [B, 1], at=w3)
            best, best_atf = sb("best", [B, 8], at=w3), sb("best_atf", [B, 8], at=w3)
            best_at = sb("best_at", [B, 8], U32, at=w3)
            zone_b, picked0 = sb("zone_b", [B, E0], at=w3), sb("picked0", [B, E0], at=w3)
            zone_w = sb("zone_w", [P, T, E0], at=w3)
            zeroed = fill(pad_row[:], 0.0)
            after(DVE, zeroed)
            pad_made = chain(lambda: v.tensor_copy(pad_row[:, D:], idle_place))
            after(PE, r_ld.all())
            m = pe_line.did(nc.tensor.matmul(bank[6][0:R0, 0:B], rw1[:], pooled[:], start=True, stop=True))
            after(ACTE, m, r_ld.all())
            m = act_line.did(nc.scalar.activation(rh[:], bank[6][0:R0, 0:B], ACT.Tanh, bias=rb1[:, 0:1], scale=1.0 / S))
            after(PE, m)
            m = pe_line.did(nc.tensor.matmul(bank[7][0:B, 0:E0], rh[:], rw2[:], start=True, stop=True))
            after(DVE, m, r_ld.all())
            m = chain(lambda: v.tensor_tensor(prob[:], bank[7][0:B, 0:E0], rb2[:], ALU.add),
                      lambda: v.tensor_reduce(one[:], prob[:], AX.X, ALU.max),
                      lambda: v.tensor_scalar(prob[:], prob[:], one[:, 0:1], None, ALU.subtract))
            after(ACTE, m)
            after(DVE, act_line.did(nc.scalar.activation(prob[:], prob[:], ACT.Exp)))
            nc.scalar.preload_act_table(ACT.Gelu_apprx_tanh)
            chain(lambda: v.tensor_reduce(one[:], prob[:], AX.X, ALU.add),
                  lambda: v.reciprocal(one[:], one[:]),
                  lambda: v.tensor_scalar(prob[:], prob[:], one[:, 0:1], None, ALU.mult),
                  lambda: v.max(best[:], prob[:]),
                  lambda: v.max_index(best_at[:], best[:], prob[:]),
                  lambda: v.tensor_copy(best_atf[:], best_at[:]),
                  lambda: v.tensor_reduce(one[:], best[:, 0:K0], AX.X, ALU.add),
                  lambda: v.reciprocal(one[:], one[:]),
                  lambda: v.tensor_scalar(best[:], best[:], one[:, 0:1], None, ALU.mult))
            for k in range(K0):
                dst = zone_b if k == 0 else picked0
                m = chain(lambda: v.tensor_scalar(dst[:], ids[0:B, 0:E0], best_atf[:, k:k + 1], best[:, k:k + 1],
                                                  ALU.is_equal, ALU.mult))
                if k > 0:
                    m = chain(lambda: v.tensor_tensor(zone_b[:], zone_b[:], picked0[:], ALU.add))
            after(SP, m)
            load(sent, a["routes_w"], zone_b[:])
            after(SP, sent.all())
            for g in range(2):
                load(routes_ld, zone_w[g * S:(g + 1) * S, :, :],
                     a["routes_w"].rearrange("(o t g) k -> g o t k", o=1, g=2)[g].to_broadcast([S, T, E0]))
            after(SP, pad_made)
            load(padded, a["routed_rows"].rearrange("(j p) d -> p j d", p=P),
                 pad_row[:].unsqueeze(1).to_broadcast([P, SPARE_ROW // P + 1, D + 1]))

        if stages >= 3:
            after(DVE, g_ld.all())
            after(PE, zones_ld.all())
            assert E0 == EX
            gates = new(T // G * E0, 2, credit=1)

            def make_gate(g, e, n):
                tiles = bass.ds(g * G, G)
                after(DVE, gates.at(n - 1))
                after(DVE, gates.did(v.scalar_tensor_tensor(out=picked[:], in0=chosen[:, tiles, :], scalar=float(e),
                                                            in1=weight[:, tiles, :], op0=ALU.is_equal, op1=ALU.mult), n))
                gates.did(v.tensor_reduce(gate[:, tiles, e:e + 1], picked[:], AX.X, ALU.add), n)

            wza_high, wza_low = (w[:].rearrange("p (e f) -> p e f", e=E0) for w in (wza_high, wza_low))
            experts(E0, F0 // P, wza_high, wza_low, HT_low0, wzb, ghid, zone_w, ACT.Gelu_apprx_tanh, make_gate, gated=routes_ld.all())
            stage_end()
            w3.close()
            wz.close()
        w13 = sb("w13", [P, E1, 2 * F1])
        wpi_high, wpi_low = sb("wpi_high", [P, EX, FX]), sb("wpi_low", [P, EX, FX])
        HT_low1 = sb("HT_low1", [P, T, P])
        rows = sb("rows", [P, G, K1, D + 1])
        lg, eqs, both = sb("lg", [P, G, E1]), sb("eqs", [P, G, E1]), sb("both", [P, G, E1])
        hots = [sb(f"hot{k}", [P, G, E1]) for k in range(K1)]
        earlier = sb("earlier", [P, G + 1, E1])
        tops, rk = sb("tops", [P, K1, G]), sb("rk", [P, K1, G])
        row_at = sb("row_at", [P, K1, G], U32)
        place = sb("place", [P, G, E1])
        shares = sb("shares", [P, K1, T])
        next_row = sb("next_row", [P, E1])
        rid, ones = sb("rid", [P, E1]), sb("ones", [P, P])
        hT4 = sb("hT4", [P, G, P])
        size, end, gap, size_i = sb("size", [1, E1]), sb("end", [1, E1]), sb("gap", [1, E1]), sb("size_i", [1, E1], I32)
        slot_ef, slot_rf = sb("slot_ef", [1, SLOTS]), sb("slot_rf", [1, SLOTS])
        slot_e, slot_row = sb("slot_e", [1, SLOTS], U32), sb("slot_row", [1, SLOTS], U32)
        if stages >= 3:
            load(narrow_ld, w2e, a["L1_ffn_W2"].rearrange("e (c p) d -> p (e c) d", p=P))
            load(experts_ld, w13[:, :, 0:F1], a["L1_ffn_W1"].rearrange("e d f -> d e f"))
            load(experts_ld, w13[:, :, F1:], a["L1_ffn_W3"].rearrange("e d f -> d e f"))

        if stages >= 4:
            w4 = ExitStack()
            kT, qT = twice("kT", [P, P], at=w4), twice("qT", [P, P], at=w4)
            by_head = [t[:].rearrange("p c n -> p (c n)").rearrange("p (k h n) -> p k h n", k=2, h=H1) for t in ghid]
            qh = [t[:, 0] for t in by_head]
            sm = [t[:, 1] for t in by_head]
            v1, o17 = twice("v1_", [P, H1, D1 + 1], at=w4), twice("o17_", [P, H1, D1 + 1], at=w4)
            dn, sq, on = twice("dn", [P, H1], at=w4), twice("sq", [P, H1, D1], at=w4), twice("on", [P, H1, D1], at=w4)
            for u in range(2):
                fill(v1[u][:], 1.0)
            after(DVE, a_ld.all())
            m = chain(lambda: v.tensor_scalar(wo1[:], wo1[:], nw1[:, 0:1], None, ALU.mult))
            for engine in (PE, ACTE, DVE):
                after(engine, a_ld.all(), pool_line.all(), m)
            W17 = H1 * (D1 + 1)
            PER_BANK = 3
            norm = Norm(bank[0][:, 0:P], sharing=lambda n: ens_norm.lowered.at(n - ENS_LAG))
            ens_norm = Norm(bank[0][:, P:2 * P], keep=HT, buffers=1, sharing=lambda n: norm.moved.at((n + (ENS_LAG - 1)).upto(T - 1)),
                            low=HT_low1)
            ENS_LAG = 9
            qkv_made, qkv_moved, spread = new(T), new(T, 3), new(T)
            scored, masked = new(T, 2), new(T, 2)
            mixed, taken = new(T), new(T, H1)
            divided, rooted, normed = new(T, 7), new(T), new(T)
            o_turned, o_moved, projected, streamed = new(T), new(T), new(T), new(T)

            def causal_project(n, u):
                after(PE, norm.moved.at(n), qkv_moved.at(n - 1))
                nc.tensor.matmul(bank[1][:, 0:P], wqk1[:, 0, :], hT[u][:], start=True, stop=True)
                nc.tensor.matmul(bank[1][:, P:2 * P], wqk1[:, 1, :], hT[u][:], start=True, stop=True)
                m = qkv_made.did(nc.tensor.matmul(bank[1][:, 2 * P:3 * P], hT[u][:], wv1[:], start=True, stop=True), n)
                after(ACTE, m, spread.at(n - 2), scored.at(n - 2), mixed.at(n - 2))
                q = qkv_moved.did(nc.scalar.activation(qT[u][:], bank[1][:, 0:P], ACT.Copy), n)
                qkv_moved.did(nc.scalar.activation(kT[u][:], bank[1][:, P:2 * P], ACT.Copy), n)
                qkv_moved.did(nc.scalar.activation(v1[u][:, :, 0:D1], bank[1][:, 2 * P:3 * P].rearrange("p (h d) -> p h d", h=H1),
                                                   ACT.Copy), n)
                after(POOL, q, scored.at(n - 2))
                spread.did(nc.gpsimd.tensor_tensor(qh[u], qT[u][:].unsqueeze(1).to_broadcast([P, H1, P]),
                                                   head_of1.unsqueeze(2).to_broadcast([P, H1, P]), ALU.mult), n)

            def causal_score(n, u):
                after(PE, spread.at(n), qkv_moved.at(n), masked.at(n - 1))
                for k in range(2):
                    scored.did(nc.tensor.matmul(bank[2 + k][:], kT[u][:], qh[u][:, 4 * k:4 * k + 4, :].rearrange("p h n -> p (h n)"),
                                                start=True, stop=True), n)

            def causal_mask(k):
                def step(n, u):
                    after(DVE, scored.at(n, k + 1), mixed.at(n - 2))
                    masked.did(v.tensor_tensor(sm[u][:, 4 * k:4 * k + 4, :], bank[2 + k][:].rearrange("p (h n) -> p h n", h=4),
                                               causal.unsqueeze(1).to_broadcast([P, 4, P]), ALU.mult), n)
                return step

            places = [(bank[4 + hd // PER_BANK], hd % PER_BANK) for hd in range(H1)]

            def causal_mix(n, u):
                after(PE, masked.at(n), taken.at(n - 1))
                for hd, (bk, r) in enumerate(places):
                    m = nc.tensor.matmul(bk[:, r * W17:(r + 1) * W17], sm[u][:, hd, :], v1[u][:].rearrange("p h d -> p (h d)"),
                                         start=True, stop=True)
                mixed.did(m, n)

            def causal_take(n, u):
                after(DVE, mixed.at(n), divided.at(n - 2))
                for hd, (bk, r) in enumerate(places):
                    c = r * W17 + hd * (D1 + 1)
                    taken.did(v.tensor_copy(o17[u][:, hd, :], bk[:, c:c + D1 + 1]), n)

            def causal_divide(k):
                def step(n, u):
                    row_sum = o17[u][:, :, D1]
                    if k == 0:
                        after(DVE, taken.at(n), normed.at(n - 2))
                    else:
                        after(DVE, divided.at(n, k), o_turned.at(n - 2) if k == 3 else None)
                    make = (
                        lambda: v.scalar_tensor_tensor(out=dn[u][:], in0=row_sum, scalar=-1.0, in1=row_sum, op0=ALU.mult, op1=ALU.max),
                        lambda: v.tensor_scalar(dn[u][:], dn[u][:], 1.0, None, ALU.max),
                        lambda: v.reciprocal(dn[u][:], dn[u][:]),
                        lambda: v.tensor_tensor(on[u][:], o17[u][:, :, 0:D1], dn[u][:].unsqueeze(2).to_broadcast([P, H1, D1]), ALU.mult),
                        lambda: v.tensor_tensor(sq[u][:], on[u][:], on[u][:], ALU.mult),
                        lambda: v.tensor_reduce(dn[u][:], sq[u][:], AX.X, ALU.add),
                        lambda: v.tensor_scalar(dn[u][:], dn[u][:], 1.0 / D1, EPS, ALU.mult, ALU.add))[k]
                    divided.did(make(), n)
                return step

            def causal_root(n, u):
                after(POOL, divided.at(n))
                rooted.did(nc.gpsimd.tensor_tensor(dn[u][:], dn[u][:], neghalf[:, 0:H1], ALU.pow), n)

            def causal_turn(n, u):
                after(DVE, rooted.at(n))
                m = normed.did(v.tensor_tensor(on[u][:], on[u][:], dn[u][:].unsqueeze(2).to_broadcast([P, H1, D1]), ALU.mult), n)
                after(PE, m, streamed.at(n - 1))
                m = o_turned.did(nc.tensor.transpose(bank[7][:, 0:P], on[u][:].rearrange("p h d -> p (h d)"), ident), n)
                after(ACTE, m, projected.at(n - 2))
                o_moved.did(nc.scalar.activation(oT[u][:], bank[7][:, 0:P], ACT.Copy), n)

            def causal_out(n, u):
                after(PE, o_moved.at(n))
                projected.did(nc.tensor.matmul(bank[7][:, P:2 * P], oT[u][:], wo1[:], start=True, stop=True), n)

            def causal_stream(n, u):
                after(DVE, projected.at(n))
                x = X[:, n.times(1), :]
                streamed.did(v.tensor_tensor(x, x, bank[7][:, P:2 * P], ALU.add), n)

            ENS_PART = EX * FX // T
            for engine in (DVE, POOL):
                after(engine, ens_ld.all())
            ens_part = lambda w: lambda n: w[:].rearrange("p e f -> p (e f)")[:, bass.ds(n.times(ENS_PART), ENS_PART)]
            split_weights = splitter(*map(ens_part, (wpi, wpi_high, wpi_low)))
            pipeline(nc, T, [(4, causal_mix), (7, causal_turn), (1, lambda n, u: norm.finish(n, u, qkv_made.at(n - 2))), (ENS_LAG, ens_norm.finish), (3, causal_score), (0, norm.moments), (8, lambda n, u: ens_norm.moments(n, u, streamed.at(n))), (5, causal_divide(0)), (0, norm.gather), (8, ens_norm.gather), (5, causal_divide(1)), (0, norm.invert), (5, causal_divide(2)), (8, ens_norm.invert), (5, causal_divide(3)), (4, causal_take), (5, causal_divide(4)), (3, causal_mask(0)), (5, causal_divide(5)), (3, causal_mask(1)), (5, causal_divide(6)), (7, causal_out), (2, causal_project), (5, causal_root), (7, causal_stream), (0, split_weights), (ENS_LAG, ens_norm.lower)])
            stage_end()
            w4.close()

        if stages >= 5:
            after(PE, ens_ld.all())
            nc.scalar.preload_act_table(ACT.Relu)

            GROUPS = T // G
            norm = Norm(bank[7][:, 0:P], credit=2, h_of=lambda n, u: rows[:, n.c % G, 0, 0:D],
                        hT_of=lambda n, u: hT4[:, n.c % G, :])
            rows_sent = new(GROUPS, K1 * G, 16, queue="rows")
            rows_free = new(GROUPS, credit=1)
            scored, raised, ranked = new(GROUPS, credit=1), new(GROUPS, credit=1), new(GROUPS, credit=1)
            copied = new(GROUPS, G, credit=1)
            after(DVE, t_ld.all(), pool_line.all())
            chain(lambda: v.tensor_scalar(rid[:], ids, -1.0, float(E1), ALU.mult, ALU.add),
                  lambda: v.memset(ones[:], 1.0),
                  lambda: v.memset(earlier[:], 0.0),
                  lambda: v.tensor_copy(next_row[:], first_rows))
            for engine in (PE, ACTE):
                after(engine, t_ld.all(), dve_line.all())
            over_t = lambda m: m.unsqueeze(2).to_broadcast([P, G, E1])
            over_e = lambda m: m.unsqueeze(1).to_broadcast([P, G, E1])
            logits = bank[6][:, 0:G * E1].rearrange("p (t e) -> p t e", t=G)
            counts = bank[6][:, G * E1:(2 * G + 1) * E1].rearrange("p (t e) -> p t e", t=G + 1)
            ranks, totals = counts[:, 0:G, :], counts[:, G, :]
            flat = lambda m: m.rearrange("p t e -> p (t e)")

            def tiles_of(g):
                return bass.ds(g.times(G), G)

            def routing(g):
                logit = [
                    lambda: v.tensor_tensor(lg[:], logits, over_e(br[:]), ALU.add),
                    lambda: v.tensor_reduce(rk[:, 0, :], lg[:], AX.X, ALU.max),
                    lambda: v.tensor_tensor(lg[:], lg[:], over_t(rk[:, 0, :]), ALU.subtract)]
                softmax = [
                    lambda: v.tensor_reduce(rk[:, 0, :], lg[:], AX.X, ALU.add),
                    lambda: v.reciprocal(rk[:, 0, :], rk[:, 0, :]),
                    lambda: v.tensor_tensor(lg[:], lg[:], over_t(rk[:, 0, :]), ALU.mult)]
                choices = []
                for k in range(K1):
                    choices += [
                        lambda k=k: v.tensor_reduce(tops[:, k, :], lg[:], AX.X, ALU.max),
                        lambda k=k: v.tensor_tensor(eqs[:], lg[:], over_t(tops[:, k, :]), ALU.is_equal),
                        lambda: v.tensor_tensor(eqs[:], eqs[:], over_e(rid[:]), ALU.mult),
                        lambda k=k: v.tensor_reduce(rk[:, k, :], eqs[:], AX.X, ALU.max),
                        lambda k=k: v.tensor_tensor(hots[k][:], over_e(rid[:]), over_t(rk[:, k, :]), ALU.is_equal)]
                    if k == 0:
                        choices += [lambda: v.scalar_tensor_tensor(out=lg[:], in0=hots[0][:], scalar=-2.0, in1=lg[:],
                                                                   op0=ALU.mult, op1=ALU.add)]
                choices += [lambda: v.tensor_tensor(both[:], hots[0][:], hots[1][:], ALU.add)]
                choices += [lambda t=t: v.tensor_tensor(earlier[:, t + 1, :], earlier[:, t, :], both[:, t, :], ALU.add) for t in range(G)]
                share = [
                    lambda: v.tensor_tensor(rk[:, 0, :], tops[:, 0, :], tops[:, 1, :], ALU.add),
                    lambda: v.reciprocal(rk[:, 0, :], rk[:, 0, :]),
                    lambda: v.tensor_tensor(shares[:, :, tiles_of(g)], tops[:], rk[:, 0:1, :].to_broadcast([P, K1, G]), ALU.mult),
                    lambda: v.tensor_copy(rows[:, :, :, D], places_of.rearrange("p (t k) -> p t k", k=K1)[:, tiles_of(g), :])]
                placing = [
                    lambda: v.tensor_tensor(place[:], ranks, over_e(next_row[:]), ALU.add),
                    lambda: v.tensor_tensor(next_row[:], next_row[:], totals, ALU.add)]
                for k in range(K1):
                    placing += [
                        lambda k=k: v.tensor_tensor(hots[k][:], hots[k][:], place[:], ALU.mult),
                        lambda k=k: v.tensor_reduce(rk[:, k, :], hots[k][:], AX.X, ALU.add)]
                placing += [lambda: v.tensor_copy(row_at[:], rk[:])]
                return logit, softmax, choices, share, placing

            parts = routing(Item(0))
            routed = new(GROUPS, sum(map(len, parts)), credit=1)
            reached = [sum(map(len, parts[:k + 1])) for k in range(len(parts))]
            LOGIT, SOFTMAX, CHOICES, SHARE, PLACING = range(5)

            def route(g, part, *marks):
                marks += (routed.at(g, reached[part - 1]) if part else routed.at(g - 1)),
                for make in routing(g)[part]:
                    after(DVE, *marks)
                    marks = (routed.did(make(), g),)

            def tile(g, t):
                return Item(g.c * G + t, g.i, g.scale * G)

            def norm_begin(g, t, ready=None):
                norm.begin(tile(g, t), t % 2, ready)

            def norm_finish(g, t):
                n = tile(g, t)
                norm.finish(n, t % 2, scored.at(g - 1), free=rows_free.at(g - 1))

            def second_row(g, t):
                after(ACTE, norm.normed.at(tile(g, t)), rows_free.at(g - 1))
                copied.did(nc.scalar.activation(rows[:, t, 1, 0:D], rows[:, t, 0, 0:D], ACT.Copy), g)

            def score(g, t):
                after(PE, norm.moved.at(tile(g, t)), routed.at(g - 1))
                m = nc.tensor.matmul(bank[6][:, t * E1:(t + 1) * E1], hT4[:, t, :], wr[:], start=True, stop=True)
                if t == G - 1:
                    scored.did(m, g)

            def rank(g):
                after(PE, routed.at(g, reached[CHOICES]))
                nc.tensor.matmul(flat(counts), ones[:], flat(earlier[:]), start=True, stop=False)
                m = nc.tensor.matmul(flat(ranks), before, flat(both[:]), start=False, stop=True)
                ranked.did(m, g)

            def send(g, t):
                for k in range(K1):
                    rows_sent.did(nc.gpsimd.indirect_dma_start(
                        a["routed_rows"], bass.IndirectOffsetOnAxis(ap=row_at[:, k, t:t + 1], axis=0), rows[:, t, k, :], None), g)

            def behind(e, g, ready):
                if e == 0:
                    for t in (0, 1):
                        norm_begin(g, t, ready)
                elif e == 1:
                    for t in (0, 1):
                        norm_finish(g, t)
                    for t in (2, 3):
                        norm_begin(g, t, ready)
                elif e == 2:
                    for t in (2, 3):
                        norm_finish(g, t)
                    for t in range(G):
                        second_row(g, t)
                elif e == 3:
                    for t in range(G):
                        score(g, t)
                    route(g, LOGIT, scored.at(g))
                    after(ACTE, routed.at(g, reached[LOGIT]))
                    raised.did(nc.scalar.activation(lg[:], lg[:], ACT.Exp), g)
                elif e == 4:
                    route(g, SOFTMAX, raised.at(g))
                    route(g, CHOICES)
                elif e == 5:
                    rank(g)
                    route(g, SHARE, rows_free.at(g - 1))
                    route(g, PLACING, ranked.at(g))
                elif e == 6:
                    apart(POOL, routed.at(g), copied.at(g), norm.normed.at(tile(g, G - 1)))
                    for t in range(G):
                        send(g, t)
                elif e == 7:
                    rows_free.did_after(POOL, g, rows_sent.at(g))

            assert G == 4 and EX == 8
            after(POOL, padded.all())
            experts(EX, FX // P, wpi_high, wpi_low, HT_low1, wpo, [t[:, 0:FX // P, :] for t in ghid], gate, None, behind=behind)
            for engine in (POOL, SP):
                after(engine, rows_sent.at(Item(GROUPS - 1)))
            nc.scalar.preload_act_table(ACT.Silu)
            w6 = ExitStack()
            past, past_gap = (t[0:1, :, :].rearrange("p c n -> p (c n)")[:, 0:SLOTS * E1].rearrange("p (s e) -> p s e", e=E1) for t in ghid)
            shift = P.bit_length() - 1
            over_slots = lambda m: m.unsqueeze(1).to_broadcast([1, SLOTS, E1])
            after(DVE, routed.at(Item(GROUPS - 1)))
            chain(
                lambda: v.tensor_tensor(size[:], next_row[0:1, :], first_rows[0:1, :], ALU.subtract),
                lambda: v.tensor_scalar(size[:], size[:], float(P - 1), None, ALU.add),
                lambda: v.tensor_copy(size_i[:], size[:]),
                lambda: v.tensor_scalar(size_i[:], size_i[:], shift, shift, ALU.logical_shift_right, ALU.logical_shift_left),
                lambda: v.tensor_copy(size[:], size_i[:]),
                lambda: v.tensor_tensor_scan(end[:], ones[0:1, 0:E1], size[:], 0.0, ALU.mult, ALU.add),
                lambda: v.tensor_scalar(gap[:], size[:], -1.0, float(CAP), ALU.mult, ALU.add),
                lambda: v.tensor_tensor(past, over_slots(end[:]), slot_start[0:1, :].unsqueeze(2).to_broadcast([1, SLOTS, E1]),
                                        ALU.is_le),
                lambda: v.tensor_reduce(slot_ef[:], past, AX.X, ALU.add),
                lambda: v.tensor_scalar(slot_e[:], slot_ef[:], float(E1 - 1), None, ALU.min),
                lambda: v.tensor_tensor(past_gap, past, over_slots(gap[:]), ALU.mult),
                lambda: v.tensor_reduce(slot_rf[:], past_gap, AX.X, ALU.add),
                lambda: v.tensor_tensor(slot_rf[:], slot_rf[:], slot_start[0:1, :], ALU.add),
                lambda: v.tensor_scalar(slot_row[:], slot_rf[:], float(SPARE_ROW), None, ALU.min))
            stage_end()

        if stages >= 6:
            _, stat, mv, ve, rstd = norm_sets[0]
            xg, yn = twice("xg", [P, D + 1], at=w6), twice("yn", [P, D], at=w6)
            places, answer_at = sb("places", [P, SLOTS], at=w6), twice("answer_at", [P, 1], U32, at=w6)
            aside = twice("aside", [P, 1], at=w6)
            gb = twice("gb", [P, 2 * D], at=w6)
            silu = [t[:, 0, :] for t in ghid]
            prodT = [t[:, 1, :].rearrange("p (c n) -> p c n", n=P) for t in ghid]
            rows_in, affine_in = (signals.alternating(SLOTS, queue="slots") for _ in range(2))
            answered = signals.alternating(SLOTS, queue="answers")
            x_turned, x_moved, noted, addressed = new(SLOTS), new(SLOTS), new(SLOTS, 2), new(SLOTS)
            widened, gated, product = new(SLOTS, 2), new(SLOTS), new(SLOTS)
            p_turned, p_moved, narrowed = new(SLOTS), new(SLOTS), new(SLOTS)
            moments, rooted, normed, scaled = new(SLOTS, 3), new(SLOTS), new(SLOTS), new(SLOTS, 2)
            after(PE, experts_ld.all(), narrow_ld.all())
            expert = {}

            def number_of(engine, table, n, last):
                return engine.value_load(table[0:1, bass.ds(n.times(1), 1)], min_val=0, max_val=last)

            def slot_load(n, u):
                first = number_of(SP, slot_row, n, SPARE_ROW)
                apart(SP, x_turned.at(n - 2))
                apart(SP, noted.at(n - 2))
                rows_in.did(SP.dma_start(xg[u][:], a["routed_rows"][bass.ds(first, P), :]), n)

            def slot_affine(n, u):
                e = number_of(SP, slot_e, n, E1 - 1)
                after(SP, scaled.at(n - 2))
                affine_in.did(SP.dma_start(gb[u][:], a["gamma_beta"][bass.ds(e, 1), :].to_broadcast([P, 2 * D])), n)

            def slot_turn(n, u):
                after(PE, rows_in.at(n), x_moved.at(n - 1))
                m = x_turned.did(nc.tensor.transpose(bank[7][:, 0:P], xg[u][:, 0:D], ident), n)
                after(ACTE, m, widened.at(n - 2))
                x_moved.did(nc.scalar.activation(hT[u][:], bank[7][:, 0:P], ACT.Copy), n)

            def slot_note(n, u):
                now = bass.ds(n.times(1), 1)
                after(DVE, rows_in.at(n), noted.at(n - 2))
                m = noted.did(v.scalar_tensor_tensor(out=aside[u][:], in0=xg[u][:, D:], scalar=float(IDLE), in1=slot_start[:, now],
                                                     op0=ALU.is_ge, op1=ALU.mult), n)
                after(DVE, m)
                noted.did(v.tensor_tensor(places[:, now], aside[u][:], xg[u][:, D:], ALU.add), n)

            def slot_address(n, u):
                after(DVE, noted.at(n), answered.at(n - 2))
                addressed.did(v.tensor_copy(answer_at[u][:], places[:, bass.ds(n.times(1), 1)]), n)

            def slot_widen(n, u):
                e = expert["widen"]
                after(PE, x_moved.at(n), gated.at(n - 2), product.at(n - 2))
                gate_up, value_up = bank[2 * u], bank[2 * u + 1]
                g = widened.did(nc.tensor.matmul(gate_up[:], hT[u][:], w13[:, e, 0:F1], start=True, stop=True), n)
                w = widened.did(nc.tensor.matmul(value_up[:], hT[u][:], w13[:, e, F1:2 * F1], start=True, stop=True), n)
                after(ACTE, g, p_turned.at(n - 2))
                m = gated.did(nc.scalar.activation(silu[u], gate_up[:], ACT.Silu), n)
                after(DVE, m, w)
                product.did(v.tensor_tensor(silu[u], silu[u], value_up[:], ALU.mult), n)

            def slot_turn_hidden(n, u):
                after(PE, product.at(n), p_moved.at(n - 1))
                for c in range(F1 // P):
                    m = nc.tensor.transpose(bank[4][:, c * P:(c + 1) * P], silu[u][:, c * P:(c + 1) * P], ident)
                after(ACTE, p_turned.did(m, n), narrowed.at(n - 2))
                p_moved.did(nc.scalar.activation(prodT[u], bank[4][:].rearrange("p (c n) -> p c n", c=F1 // P), ACT.Copy), n)

            def slot_expert(step):
                def load_number(n, u):
                    expert[step] = number_of(PE, slot_e, n, E1 - 1)
                return load_number

            def slot_narrow(n, u):
                e = expert["narrow"]
                after(PE, p_moved.at(n), normed.at(n - 2))
                y = bank[5 + u][:, 0:D]
                for c in range(F1 // P):
                    m = nc.tensor.matmul(y, prodT[u][:, c, :], w2e[:, e * (F1 // P) + c, :], start=(c == 0), stop=(c == F1 // P - 1))
                narrowed.did(m, n)

            def slot_moments(n, u):
                y = bank[5 + u][:, 0:D]
                apart(DVE, narrowed.at(n))
                apart(DVE, moments.did(v.bn_stats(stat[u][:], y), n))
                after(DVE, moments.did(v.bn_aggr(mv[u][:], stat[u][:]), n))
                m = moments.did(v.tensor_scalar(ve[u][:], mv[u][:, 1:2], EPS, None, ALU.add), n)
                after(POOL, m)
                rooted.did(nc.gpsimd.tensor_tensor(rstd[u][:], ve[u][:], neghalf[:, 0:1], ALU.pow), n)

            def slot_finish(n, u):
                after(DVE, rooted.at(n), answered.at(n - 2))
                m = normed.did(v.tensor_scalar(yn[u][:], bank[5 + u][:, 0:D], mv[u][:, 0:1], rstd[u][:, 0:1],
                                               ALU.subtract, ALU.mult), n)
                after(POOL, m, affine_in.at(n))
                after(POOL, scaled.did(nc.gpsimd.tensor_tensor(yn[u][:], yn[u][:], gb[u][:, 0:D], ALU.mult), n))
                m = scaled.did(nc.gpsimd.tensor_tensor(yn[u][:], yn[u][:], gb[u][:, D:2 * D], ALU.add), n)
                apart(POOL, m, addressed.at(n))
                answered.did(nc.gpsimd.indirect_dma_start(
                    a["answers"], bass.IndirectOffsetOnAxis(ap=answer_at[u][:, 0:1], axis=0), yn[u][:], None), n)

            pipeline(nc, SLOTS, [(0, slot_load), (4, slot_affine), (4, slot_expert("narrow")), (1, slot_turn), (1, slot_note),
                                 (4, slot_narrow), (2, slot_expert("widen")), (3, slot_turn_hidden), (5, slot_address), (5, slot_finish), (4, slot_moments), (2, slot_widen)])
            for engine in (ACTE, SP):
                after(engine, answered.at(Item(SLOTS - 2)), answered.at(Item(SLOTS - 1)))
            stage_end()

            got = w13[:].rearrange("p e f -> p (e f)")[:, 0:T * K1 * D].rearrange("p (t k d) -> p t k d", k=K1, d=D)
            answers_p = a["answers"][0:IDLE, :].rearrange("(t p k) d -> p t (k d)", p=P, k=K1)
            o_view = out.rearrange("b s d -> (b s) d").rearrange("(t p) d -> p t d", p=P)
            arrived = [loads(f"answers_loaded{g}") for g in range(T // G)]
            for g in range(T // G):
                tiles = slice(g * G, (g + 1) * G)
                load(arrived[g], got[:, tiles, :, :].rearrange("p t k d -> p t (k d)"), answers_p[:, tiles, :])
            for g in range(T // G):
                after(ACTE, arrived[g].all())
                tiles = slice(g * G, (g + 1) * G)
                for k in range(K1):
                    for t in range(g * G, (g + 1) * G):
                        m = act_line.did(nc.scalar.activation(got[:, t, k, :], got[:, t, k, :], ACT.Copy, scale=shares[:, k, t:t + 1]))
                    after(DVE, m, dve_line.all())
                    m = dve_line.did(v.tensor_tensor(X[:, tiles, :], X[:, tiles, :], got[:, tiles, k, :], ALU.add))
                after(SP, m)
                load(out_st, o_view[:, tiles, :], X[:, tiles, :])
            after(SP, out_st.all())
            w6.close()

        if stages < 6:
            if stages < 3: wz.close()
            after(SP, *[line.all() for line in (pe_line, dve_line, cx_ld, zones_ld, ens_ld, experts_ld, g_ld)])
            if stages >= 3: after(SP, narrow_ld.all())
            load(out_st, out.rearrange("b s d -> (b s) d").rearrange("(t p) d -> p t d", p=P), X[:])
            after(SP, out_st.all())


def constants():
    r, c = np.arange(P)[:, None], np.arange(P)[None, :]
    masks = [r == c, np.concatenate([r // DH0 == c // DH0, r // DH0 == c[:, :H0]], axis=1), r // D1 == c[:, :H1],
             (r // S == c // S) & (c >= r), r < c,
             c[:, :E1] + 0 * r, P * c[:, :SLOTS] + 0 * r, CAP * c[:, :E1] + 0 * r,
             K1 * (P * (c[:, :K1 * T] // K1) + r) + c[:, :K1 * T] % K1, IDLE + r]
    return np.concatenate([m.astype(np.float32) for m in masks], axis=1)


def lay_out(inputs):
    a = {n: np.ascontiguousarray(v) for n, v in inputs.items()}
    a["consts"] = constants()
    a["ctxT"] = np.ascontiguousarray(a["ctx_512"].transpose(0, 2, 1))
    for n in ("Wq", "Wk", "Wv"):
        a[f"L0_xattn_{n}T"] = np.ascontiguousarray(a.pop(f"L0_xattn_{n}").T)
    for n in ("Wq", "Wk", "Wv", "Wo"):
        a[f"L1_attn_{n}T"] = np.ascontiguousarray(a.pop(f"L1_attn_{n}").T)
    a["gamma_beta"] = np.concatenate([a.pop("L1_ffn_gamma"), a.pop("L1_ffn_beta")], axis=1)
    a["proj_inT"] = np.ascontiguousarray(a.pop("L1_xattn_proj_in").transpose(2, 0, 1))
    a["proj_outT"] = np.ascontiguousarray(a.pop("L1_xattn_proj_out").transpose(0, 2, 1))
    a["ctx_tokens"] = a["ctxT"].reshape(B * S, CD)
    a["itok_tokens"] = np.ascontiguousarray(a.pop("itok_BxS2xS_0_7").transpose(0, 2, 1)).reshape(B * S, S)
    return a


def kernel(**inputs):
    import concourse.bacc as bacc
    from concourse.bass_utils import run_bass_kernel_spmd

    arrays = lay_out(inputs)

    nc = bacc.Bacc("TRN2", target_bir_lowering=False, num_devices=1)
    args = {n: nc.dram_tensor(f"in_{n}", v.shape, mybir.dt.from_np(v.dtype), kind="ExternalInput").ap()
            for n, v in arrays.items()}
    build(nc, args, nc.dram_tensor("out_x", (B, S, D), F32, kind="ExternalOutput").ap())
    r = run_bass_kernel_spmd(nc, [{f"in_{n}": v for n, v in arrays.items()}], core_ids=[0])
    return r.results[0]["out_x"]
```
